# Optimizing a Trainium2 kernel written in Bass

```python
import numpy as np
import jax
import jax.numpy as jnp

def _softmax(x, axis=-1):
    return jax.nn.softmax(x, axis=axis)

def _gelu(x):
    return jax.nn.gelu(x, approximate=True)

def _silu(x):
    return jax.nn.silu(x)

def _sigmoid(x):
    return jax.nn.sigmoid(x)

def _layernorm(x, axis=-1, eps=1e-05):
    m = jnp.mean(x, axis=axis, keepdims=True)
    v = jnp.var(x, axis=axis, keepdims=True)
    return (x - m) / jnp.sqrt(v + eps)

def _scatter_add(tgt, idx, src, axis=0):
    return tgt.at[idx].add(src)

def _segment_sum(src, seg, n):
    return jax.ops.segment_sum(src, seg, n)
kernel_name = 'mk_seq_preln_d1_jaxref_r4_f7c8f6'

def setup_inputs(seed: int=0):
    np.random.seed(seed)
    _w = jnp.asarray

    def _L0_attn_setup():
        import jax, jax.numpy as jnp
        import numpy as np
        HEADS = 16
        key = jax.random.key(seed)
        ks = jax.random.split(key, 5)
        B, T, D = (2, 512, 512)
        s = 0.02
        return {'x': jax.random.normal(ks[0], (B, T, D), dtype=jnp.float32), 'Wq': jax.random.normal(ks[1], (D, D), dtype=jnp.float32) * s, 'Wk': jax.random.normal(ks[2], (D, D), dtype=jnp.float32) * s, 'Wv': jax.random.normal(ks[3], (D, D), dtype=jnp.float32) * s, 'Wo': jax.random.normal(ks[4], (D, D), dtype=jnp.float32) * s}
    _L0_attn_in = _L0_attn_setup()

    def _L0_ffn_setup():
        import jax, jax.numpy as jnp
        import numpy as np
        EPS = 1e-06
        K_STEPS = 4
        USE_GATING = True

        def layer_norm(x, gamma, beta):
            mu = jnp.mean(x, axis=-1, keepdims=True)
            var = jnp.mean(jnp.square(x - mu), axis=-1, keepdims=True)
            return (x - mu) * jax.lax.rsqrt(var + EPS) * gamma + beta
        key = jax.random.key(seed)
        B, L, D, H = (4, 1024, 512, 2048)
        ks = jax.random.split(key, 16)
        s = 0.02
        return {'x': jax.random.normal(ks[0], (B, L, D), dtype=jnp.float32), 'in_gamma': jnp.ones((D,), jnp.float32), 'in_beta': jnp.zeros((D,), jnp.float32), 'agg_w': jax.random.normal(ks[1], (D, D), jnp.float32) * s, 'agg_b': jnp.zeros((D,), jnp.float32), 'pn_gamma': jnp.ones((D,), jnp.float32), 'pn_beta': jnp.zeros((D,), jnp.float32), 'd1_w': jax.random.normal(ks[2], (D, H), jnp.float32) * s, 'd1_b': jnp.zeros((H,), jnp.float32), 'd2_w': jax.random.normal(ks[3], (H, D), jnp.float32) * s, 'd2_b': jnp.zeros((D,), jnp.float32), 'bc_w': jax.random.normal(ks[4], (D, D), jnp.float32) * s, 'bc_b': jnp.zeros((D,), jnp.float32), 'gate_w': jax.random.normal(ks[5], (D, D), jnp.float32) * s, 'gate_b': jnp.zeros((D,), jnp.float32), 'out_gamma': jnp.ones((D,), jnp.float32), 'out_beta': jnp.zeros((D,), jnp.float32)}
    _L0_ffn_in = _L0_ffn_setup()
    _d = {'L0_attn_x': _L0_attn_in['x'], 'L0_attn_Wq': _L0_attn_in['Wq'], 'L0_attn_Wk': _L0_attn_in['Wk'], 'L0_attn_Wv': _L0_attn_in['Wv'], 'L0_attn_Wo': _L0_attn_in['Wo'], 'L0_ffn_in_gamma': _L0_ffn_in['in_gamma'], 'L0_ffn_in_beta': _L0_ffn_in['in_beta'], 'L0_ffn_agg_w': _L0_ffn_in['agg_w'], 'L0_ffn_agg_b': _L0_ffn_in['agg_b'], 'L0_ffn_pn_gamma': _L0_ffn_in['pn_gamma'], 'L0_ffn_pn_beta': _L0_ffn_in['pn_beta'], 'L0_ffn_d1_w': _L0_ffn_in['d1_w'], 'L0_ffn_d1_b': _L0_ffn_in['d1_b'], 'L0_ffn_d2_w': _L0_ffn_in['d2_w'], 'L0_ffn_d2_b': _L0_ffn_in['d2_b'], 'L0_ffn_bc_w': _L0_ffn_in['bc_w'], 'L0_ffn_bc_b': _L0_ffn_in['bc_b'], 'L0_ffn_gate_w': _L0_ffn_in['gate_w'], 'L0_ffn_gate_b': _L0_ffn_in['gate_b'], 'L0_ffn_out_gamma': _L0_ffn_in['out_gamma'], 'L0_ffn_out_beta': _L0_ffn_in['out_beta']}
    _x0 = _d['L0_attn_x']
    _d['L0_attn_x'] = jax.random.normal(jax.random.fold_in(jax.random.key(seed), 1), (4, 2048, 512), dtype=_x0.dtype)
    del _x0
    return _d

def reference(L0_attn_x, L0_attn_Wq, L0_attn_Wk, L0_attn_Wv, L0_attn_Wo, L0_ffn_in_gamma, L0_ffn_in_beta, L0_ffn_agg_w, L0_ffn_agg_b, L0_ffn_pn_gamma, L0_ffn_pn_beta, L0_ffn_d1_w, L0_ffn_d1_b, L0_ffn_d2_w, L0_ffn_d2_b, L0_ffn_bc_w, L0_ffn_bc_b, L0_ffn_gate_w, L0_ffn_gate_b, L0_ffn_out_gamma, L0_ffn_out_beta):

    def _L0_attn_ref(x, Wq, Wk, Wv, Wo):
        import jax, jax.numpy as jnp
        import numpy as np
        HEADS = 16
        B, T, _ = x.shape
        H = HEADS
        Dh = Wq.shape[1] // H
        q = (x @ Wq).reshape(B, T, H, Dh)
        k = (x @ Wk).reshape(B, T, H, Dh)
        v = (x @ Wv).reshape(B, T, H, Dh)
        scores = jnp.einsum('bthd,bshd->bhts', q, k)
        mask = jnp.tril(jnp.ones((T, T), dtype=scores.dtype))
        scores = scores * mask
        attn = jax.nn.softmax(scores / T ** 0.5, axis=-1)
        out = jnp.einsum('bhts,bshd->bthd', attn, v).reshape(B, T, H * Dh)
        return out @ Wo

    def _L0_ffn_ref(x, in_gamma, in_beta, agg_w, agg_b, pn_gamma, pn_beta, d1_w, d1_b, d2_w, d2_b, bc_w, bc_b, gate_w, gate_b, out_gamma, out_beta):
        import jax, jax.numpy as jnp
        import numpy as np
        EPS = 1e-06
        K_STEPS = 4
        USE_GATING = True

        def layer_norm(x, gamma, beta):
            mu = jnp.mean(x, axis=-1, keepdims=True)
            var = jnp.mean(jnp.square(x - mu), axis=-1, keepdims=True)
            return (x - mu) * jax.lax.rsqrt(var + EPS) * gamma + beta
        x_norm = layer_norm(x, in_gamma, in_beta)
        thought = x_norm[:, -1, :] @ agg_w + agg_b
        for _ in range(K_STEPS):
            t = layer_norm(thought, pn_gamma, pn_beta)
            t = jax.nn.gelu(t @ d1_w + d1_b, approximate=False)
            thought = thought + (t @ d2_w + d2_b)
        broadcast = (thought @ bc_w + bc_b)[:, None, :]
        if USE_GATING:
            gate = jax.nn.sigmoid(x @ gate_w + gate_b)
            out = x + gate * broadcast
        else:
            out = x + broadcast
        return layer_norm(out, out_gamma, out_beta)
    x = L0_attn_x
    x = x + _L0_attn_ref(_layernorm(x, axis=-1), L0_attn_Wq, L0_attn_Wk, L0_attn_Wv, L0_attn_Wo)
    x = x + _L0_ffn_ref(_layernorm(x, axis=-1), L0_ffn_in_gamma, L0_ffn_in_beta, L0_ffn_agg_w, L0_ffn_agg_b, L0_ffn_pn_gamma, L0_ffn_pn_beta, L0_ffn_d1_w, L0_ffn_d1_b, L0_ffn_d2_w, L0_ffn_d2_b, L0_ffn_bc_w, L0_ffn_bc_b, L0_ffn_gate_w, L0_ffn_gate_b, L0_ffn_out_gamma, L0_ffn_out_beta)
    return x

_drawn_inputs = setup_inputs


def setup_inputs(seed=0):
    import zlib

    import numpy as np

    out = dict(_drawn_inputs(seed))
    spreads = {'L0_ffn_in_gamma': (1.0, 0.6),
     'L0_ffn_in_beta': (0.0, 0.736),
     'L0_ffn_agg_b': (0.0, 0.35),
     'L0_ffn_pn_gamma': (1.0, 0.6),
     'L0_ffn_pn_beta': (0.0, 0.659),
     'L0_ffn_d1_b': (0.0, 0.311),
     'L0_ffn_d2_b': (0.0, 0.1),
     'L0_ffn_bc_b': (0.0, 0.334),
     'L0_ffn_gate_b': (0.0, 0.8),
     'L0_ffn_out_gamma': (1.0, 0.2),
     'L0_ffn_out_beta': (0.0, 0.1)}
    factors = {'L0_attn_Wq': 8.0, 'L0_attn_Wk': 8.0, 'L0_attn_Wv': 8.0, 'L0_attn_Wo': 8.0}
    for name, (base, spread) in spreads.items():
        noise = np.random.default_rng([zlib.crc32(name.encode()), seed]).standard_normal(out[name].shape)
        drawn = base * np.exp(spread * noise) if base else spread * noise
        out[name] = jnp.asarray(drawn.astype(out[name].dtype))
    for name, factor in factors.items():
        out[name] = (out[name] * factor).astype(out[name].dtype)
    return out
```

```python
import concourse.bass as bass
from concourse import mybir
from concourse.alu_op_type import AluOpType as ALU
from contextlib import ExitStack

ACT = mybir.ActivationFunctionType
AX = mybir.AxisListType
F32 = mybir.dt.float32
F32R = mybir.dt.float32r
BF16 = mybir.dt.bfloat16

P = 128
B, T, D = 4, 2048, 512
HEADS = 16
DH = D // HEADS
HG = P // DH
GROUPS = HEADS // HG
KC = D // P
CH = 512
RT = CH // P
CHUNKS = B * T // CH
TC = T // CH
SB = T // P
HF = 2048
HC = HF // P
STEPS = 4
LN_EPS, FFN_EPS = 1e-5, 1e-6
SCALE = float(T) ** -0.5


def positive(value):
    return not isinstance(value, int) or value > 0


def peeled(eng, body, n):
    body(0)
    with eng.Fori(1, n - 1) as i:
        body(i)
    body(n - 1)


def is_last(i, n):
    return isinstance(i, int) and i == n - 1


def project(nc, x, Wq, Wk, Wv, qk_scr, v_scr):
    ctx = ExitStack()
    sb = lambda name, shape, dt=F32: ctx.enter_context(nc.sbuf_tensor(name, shape, dt))
    pb = lambda name, shape: ctx.enter_context(nc.psum_tensor(name, shape, F32))
    sem = lambda name: ctx.enter_context(nc.semaphore(name))
    QK_TILES, V_TILES = 2 * GROUPS, RT
    BANKS = 6
    with ctx:
        w_raw = sb("w_raw", [P, 3, KC, D])
        w_hi = sb("w_hi", [P, 3, KC, D], F32R)
        w_lo = sb("w_lo", [P, 3, KC, D], F32R)
        x_in = sb("x_in", [P, 2, RT, D])
        xT_hi = sb("xT_hi", [P, 2, KC, CH], F32R)
        xT_lo = sb("xT_lo", [P, 2, KC, CH], F32R)
        qk_out = sb("qk_out", [P, QK_TILES, 2, CH], F32R)
        v_out = sb("v_out", [P, V_TILES, D])
        stats = sb("stats", [P, 2, RT, 6])
        moments = sb("moments", [P, 2, RT, 2])
        var_eps = sb("var_eps", [P, 2, RT])
        rstd = sb("rstd", [P, 2, RT])
        minus_half = sb("minus_half", [P, RT])
        eps = sb("eps", [P, RT])
        ident = sb("ident", [P, P])
        ps_t = pb("ps_t", [P, 2, CH])
        ps_mm = pb("ps_mm", [P, BANKS, CH])

        w_loaded = sem("w_loaded")
        w_hi_ready, w_lo_ready = sem("w_hi_ready"), sem("w_lo_ready")
        x_loaded = [sem(f"x_loaded{p}") for p in range(2)]
        const_ready = sem("const_ready")
        stats_ready, moments_ready = sem("stats_ready"), sem("moments_ready")
        eps_ready, rstd_ready = sem("eps_ready"), sem("rstd_ready")
        norm_ready = sem("norm_ready")
        transposed = sem("transposed")
        xT_hi_ready, xT_lo_ready = sem("xT_hi_ready"), sem("xT_lo_ready")
        product_ready = sem("product_ready")
        qk_hi_ready, qk_lo_ready, v_ready = sem("qk_hi_ready"), sem("qk_lo_ready"), sem("v_ready")
        qk_stored = [sem(f"qk_stored{k}") for k in range(QK_TILES)]
        v_stored = [sem(f"v_stored{r}") for r in range(V_TILES)]

        block = ctx.enter_context(nc.Block())
        N = CHUNKS // 2

        x_rows = x.rearrange("b (r p) d -> p (b r) d", p=P)
        qk_cols = qk_scr.rearrange("w s (g p) t -> w g p s t", p=P)

        @block.sync
        def _(sp):
            for w, W in enumerate((Wq, Wk, Wv)):
                sp.dma_start(w_raw[:, w], W.rearrange("(k p) n -> p k n", p=P)).then_inc(w_loaded, 16)

            def load(i, par):
                n = 2 * i + par
                if positive(KC * (n - 1)):
                    sp.wait_ge(transposed, KC * (n - 1))
                sp.dma_start(x_in[:, par], x_rows[:, bass.ds(n * RT, RT), :]).then_inc(x_loaded[par], 16)

            def store(i, par):
                n = 2 * i + par
                for k in range(QK_TILES):
                    sp.wait_ge(qk_lo_ready, QK_TILES * n + k + 1)
                    sp.dma_start(qk_cols[k // GROUPS, k % GROUPS, :, :, bass.ds(n * CH, CH)],
                                 qk_out[:, k].bitcast(F32)).then_inc(qk_stored[k], 16)
                for r in range(V_TILES):
                    sp.wait_ge(v_ready, V_TILES * n + r + 1)
                    sp.dma_start(v_scr[bass.ds(n * CH + r * P, P), :], v_out[:, r]).then_inc(v_stored[r], 16)

            def pair(i):
                for par in range(2):
                    store(i, par)
                    if not is_last(i, N):
                        load(i + 1, par)

            load(0, 0)
            load(0, 1)
            peeled(sp, pair, N)
            for s in qk_stored + v_stored:
                sp.wait_ge(s, 16 * CHUNKS)

        @block.gpsimd
        def _(pool):
            pool.memset(minus_half[:, :], -0.5).then_inc(const_ready, 1)
            pool.memset(eps[:, :], LN_EPS).then_inc(const_ready, 1)
            pool.memset(ident[:, :], 0.0).then_inc(const_ready, 1)
            pool.wait_ge(const_ready, 3)
            pool.affine_select(out=ident[:, :], in_=ident[:, :], compare_op=ALU.not_equal, fill=1.0,
                               base=0, pattern=[[-1, P]], channel_multiplier=1).then_inc(const_ready, 1)

            def pair(i):
                for par in range(2):
                    n = 2 * i + par
                    pool.wait_ge(moments_ready, RT * (n + 1))
                    if positive(RT * (n - 1)):
                        pool.wait_ge(norm_ready, RT * (n - 1))
                    pool.tensor_tensor(var_eps[:, par], moments[:, par, :, 1], eps[:, :], ALU.add).then_inc(eps_ready, 1)
                    pool.wait_ge(eps_ready, n + 1)
                    pool.tensor_tensor(rstd[:, par], var_eps[:, par], minus_half[:, :],
                                       ALU.pow).then_inc(rstd_ready, 1)

            peeled(pool, pair, N)

        @block.vector
        def _(dve):
            def chunk_stats(n, par, first=False):
                dve.wait_ge(x_loaded[par], (n // 2 + 1) * 16 if isinstance(n, int) else (n - par) * 8 + 16)
                if positive(n - 1):
                    dve.wait_ge(rstd_ready, n - 1)
                for r in range(RT):
                    nc.vector.bn_stats(stats[:, par, r], x_in[:, par, r]).then_inc(stats_ready, 1)

            def chunk_moments(n, par):
                for r in range(RT):
                    nc.vector.bn_aggr(moments[:, par, r], stats[:, par, r]).then_inc(moments_ready, 1)

            def chunk_norm(n, par):
                dve.wait_ge(rstd_ready, n + 1)
                dve.wait_ge(moments_ready, RT * (n + 1))
                for r in range(RT):
                    nc.vector.tensor_scalar(x_in[:, par, r], x_in[:, par, r], moments[:, par, r, 0:1],
                                            rstd[:, par, r:r + 1], ALU.subtract, ALU.mult).then_inc(norm_ready, 1)

            def xT_low(n, par, c):
                dve.wait_ge(xT_hi_ready, KC * n + c + 1)
                nc.vector.tensor_tensor(xT_lo[:, par, c], ps_t[:, c % 2], xT_hi[:, par, c].bitcast(F32),
                                        ALU.subtract).then_inc(xT_lo_ready, 1)

            def qk_low(n, k, stats_too=False):
                if stats_too:
                    dve.wait_ge(stats_ready, RT * (n + 2))
                dve.wait_ge(qk_hi_ready, QK_TILES * n + k + 1)
                nc.vector.tensor_tensor(qk_out[:, k, 1], ps_mm[:, k % BANKS], qk_out[:, k, 0].bitcast(F32),
                                        ALU.subtract).then_inc(qk_lo_ready, 1)

            chunk_stats(0, 0)
            dve.wait_ge(stats_ready, RT)
            chunk_moments(0, 0)
            chunk_norm(0, 0)
            dve.wait_ge(w_loaded, 48)
            for w in range(3):
                dve.wait_ge(w_hi_ready, w + 1)
                nc.vector.tensor_tensor(w_lo[:, w], w_raw[:, w], w_hi[:, w].bitcast(F32),
                                        ALU.subtract).then_inc(w_lo_ready, 1)
            for c in range(KC):
                xT_low(0, 0, c)

            def pair(i):
                for par in range(2):
                    n = 2 * i + par
                    more = not (is_last(i, N) and par == 1)
                    if more:
                        chunk_stats(n + 1, 1 - par)
                    for k in range(4):
                        qk_low(n, k, stats_too=more and k == 0)
                        if more and k == 0:
                            chunk_moments(n + 1, 1 - par)
                    if more:
                        chunk_norm(n + 1, 1 - par)
                    for k in range(4, QK_TILES):
                        qk_low(n, k)
                        if more and k >= 5:
                            for c in ((0, 1), (2,), (3,))[k - 5]:
                                xT_low(n + 1, 1 - par, c)

            peeled(dve, pair, N)

        @block.scalar
        def _(act):
            act.wait_ge(w_loaded, 48)
            for w in range(3):
                nc.scalar.activation(w_hi[:, w], w_raw[:, w], ACT.Copy).then_inc(w_hi_ready, 1)

            def xT_high(n, par, c):
                act.wait_ge(transposed, KC * n + c + 1)
                if positive((QK_TILES + V_TILES) * (n - 1)):
                    act.wait_ge(product_ready, (QK_TILES + V_TILES) * (n - 1))
                nc.scalar.activation(xT_hi[:, par, c], ps_t[:, c % 2], ACT.Copy).then_inc(xT_hi_ready, 1)

            for c in range(KC):
                xT_high(0, 0, c)

            def pair(i):
                for par in range(2):
                    n = 2 * i + par
                    more = not (is_last(i, N) and par == 1)
                    for k in range(QK_TILES):
                        act.wait_ge(product_ready, (QK_TILES + V_TILES) * n + k + 1)
                        if positive(16 * n):
                            act.wait_ge(qk_stored[k], 16 * n)
                        nc.scalar.activation(qk_out[:, k, 0], ps_mm[:, k % BANKS], ACT.Copy).then_inc(qk_hi_ready, 1)
                        if more and k >= 5:
                            for c in ((0, 1), (2,), (3,))[k - 5]:
                                xT_high(n + 1, 1 - par, c)
                    for r in range(V_TILES):
                        act.wait_ge(product_ready, (QK_TILES + V_TILES) * n + QK_TILES + r + 1)
                        if positive(16 * n):
                            act.wait_ge(v_stored[r], 16 * n)
                        nc.scalar.activation(v_out[:, r], ps_mm[:, (QK_TILES + r) % BANKS], ACT.Copy).then_inc(v_ready, 1)

            peeled(act, pair, N)

        @block.tensor
        def _(pe):
            def transposes(n, par, c):
                if c == 0:
                    pe.wait_ge(norm_ready, RT * (n + 1))
                if positive(KC * n + c - 1):
                    pe.wait_ge(xT_lo_ready, KC * n + c - 1)
                for r in range(RT):
                    last = nc.tensor.transpose(ps_t[:, c % 2, r * P:(r + 1) * P], x_in[:, par, r, c * P:(c + 1) * P],
                                               ident[:, :])
                last.then_inc(transposed, 1)

            def bank_free(n, k):
                if k >= BANKS:
                    pe.wait_ge(qk_lo_ready, QK_TILES * n + k - BANKS + 1)
                elif k + BANKS < QK_TILES:
                    if positive(n):
                        pe.wait_ge(qk_lo_ready, QK_TILES * (n - 1) + k + BANKS + 1)
                elif positive(n):
                    pe.wait_ge(v_ready, V_TILES * (n - 1) + k + BANKS - QK_TILES + 1)

            def product(n, par, k):
                bank_free(n, k)
                terms = ((w_hi, xT_hi), (w_hi, xT_lo), (w_lo, xT_hi))
                for c in range(KC):
                    for t, (w, xT) in enumerate(terms):
                        if k < QK_TILES:
                            g = k % GROUPS
                            lhsT, rhs = w[:, k // GROUPS, c, g * P:(g + 1) * P], xT[:, par, c]
                        else:
                            r = k - QK_TILES
                            lhsT, rhs = xT[:, par, c, r * P:(r + 1) * P], w[:, 2, c]
                        last = nc.tensor.matmul(ps_mm[:, k % BANKS], lhsT, rhs, start=(c == 0 and t == 0),
                                                stop=(c == KC - 1 and t == 2))
                last.then_inc(product_ready, 1)

            pe.wait_ge(const_ready, 4)
            for c in range(KC):
                transposes(0, 0, c)
            pe.wait_ge(w_lo_ready, 3)

            def pair(i):
                for par in range(2):
                    n = 2 * i + par
                    more = not (is_last(i, N) and par == 1)
                    pe.wait_ge(xT_lo_ready, KC * (n + 1))
                    for k in range(QK_TILES + V_TILES):
                        product(n, par, k)
                        if more and 5 <= k < 8:
                            for c in ((0, 1), (2,), (3,))[k - 5]:
                                transposes(n + 1, 1 - par, c)

            peeled(pe, pair, N)


def attend(nc, qk_scr, v_scr, att_scr):
    ctx = ExitStack()
    sb = lambda name, shape, dt=F32: ctx.enter_context(nc.sbuf_tensor(name, shape, dt))
    pb = lambda name, shape: ctx.enter_context(nc.psum_tensor(name, shape, F32))
    sem = lambda name: ctx.enter_context(nc.semaphore(name))

    QK_ROWS, STACK = 3 * DH, 3 * DH + 2
    FAR = -float(2 ** 100)
    STEPS_ = 2 * TC
    N = B * GROUPS // 2
    STEP_SLOTS = [RT * (ls % TC + 1) for ls in range(STEPS_)]
    NEXT_TILES = [HG * RT * ((ls + 1) % TC + 1) for ls in range(STEPS_)]
    FIRST = HG * RT + 1
    SLOTS_BEFORE = [sum(STEP_SLOTS[:ls]) for ls in range(STEPS_ + 1)]
    USES_BEFORE = [sum(n + 3 for n in NEXT_TILES[:ls]) for ls in range(STEPS_ + 1)]
    READS_BEFORE = [sum(n + 2 for n in NEXT_TILES[:ls]) for ls in range(STEPS_ + 1)]

    def step_no(i, ls):
        return STEPS_ * i + ls

    def slot_no(i, ls, j=0):
        return SLOTS_BEFORE[STEPS_] * i + SLOTS_BEFORE[ls] + j

    def use_no(i, ls, v=0):
        return FIRST + USES_BEFORE[STEPS_] * i + USES_BEFORE[ls] + v

    def read_no(i, ls, v=0):
        return FIRST + READS_BEFORE[STEPS_] * i + READS_BEFORE[ls] + v

    def side_bank(ls, v):
        return (FIRST + USES_BEFORE[ls] + v) % 2

    assert USES_BEFORE[STEPS_] % 2 == 0 and SLOTS_BEFORE[STEPS_] % 2 == 0

    def turn_slot(c):
        return RT * (c + 1) - (2 if c == 0 else 3)

    def share(c, j):
        n, slots = HG * RT * ((c + 1) % TC + 1), turn_slot(c) + 1
        return range(n * j // slots, n * (j + 1) // slots) if j < slots else range(0)

    def tile(c, m):
        h, rest = divmod(m, RT * (c + 1))
        tb, sc = divmod(rest, c + 1)
        return h, tb, sc, P * (tb + 1) if sc == c else CH, sc == c

    with ctx:
        k_stack = sb("k_stack", [P, 2, HG, T], F32R)
        q_stack = sb("q_stack", [P, TC, HG, CH], F32R)
        v_in = sb("v_in", [P, 2, SB, P])
        v_later = sb("v_later", [P, 2, SB - 2, P])
        probs = sb("probs", [P, 2, HG, CH])
        weight0 = sb("weight0", [P, CH])
        later_v = sb("later_v", [P, CH])
        later_n = sb("later_n", [P, CH])
        count = sb("count", [P, T])
        count_i = sb("count_i", [P, T], mybir.dt.int32)
        top = sb("top", [P, CH])
        bottom = sb("bottom", [P, CH])
        inverse = sb("inverse", [P, CH])
        att = sb("att", [P, CH])
        att_out = sb("att_out", [P, 2, 2, CH], F32R)
        maxima = [sb(f"maxima{x}", [P, HG, RT, TC + 1]) for x in range(2)]
        neg_max = sb("neg_max", [P, HG, RT])
        nm_hi = sb("nm_hi", [HG * RT, P], F32R)
        nm_lo = sb("nm_lo", [HG * RT, P], F32R)
        pick = sb("pick", [P, HG, P], F32R)
        ones = sb("ones", [P, P])
        ident = sb("ident2", [P, P])
        later = sb("later", [P, P])
        ident_b = sb("ident_b", [P, P], BF16)
        mask_qk = sb("mask_qk", [P, P], BF16)
        mask_kq = sb("mask_kq", [P, P], BF16)

        ps_scores = pb("ps_scores", [P, 2, 2, CH])
        ps_top = pb("ps_top", [P, CH])
        ps_bottom = pb("ps_bottom", [P, CH])
        ps_side = pb("ps_side", [P, 2, CH])

        const_ready, const_step = sem("const_ready"), sem("const_step")
        step_loaded = [sem(f"step_loaded{c}") for c in range(TC)]
        v_loaded = [sem(f"v_loaded{p}") for p in range(2)]
        scores_ready, probs_ready, probs_used = sem("scores_ready"), sem("probs_ready"), sem("probs_used")
        side_ready, side_read, weight0_ready = sem("side_ready"), sem("side_read"), sem("weight0_ready")
        neg_max_ready, nm_hi_ready, nm_stored = sem("neg_max_ready"), sem("nm_hi_ready"), sem("nm_stored")
        v_later_ready = sem("v_later_ready")
        later_n_ready = sem("later_n_ready")
        sums_read, inverse_ready = sem("sums_read"), sem("inverse_ready")
        att_ready, att_hi_ready, att_lo_ready = sem("att_ready"), sem("att_hi_ready"), sem("att_lo_ready")
        att_stored = [sem(f"att_stored{p}") for p in range(2)]

        block = ctx.enter_context(nc.Block())
        GROUP_SLOTS = slot_no(0, TC)

        @block.sync
        def _(sp):
            def load(i, ls):
                s, c, par = step_no(i, ls), ls % TC, ls // TC % 2
                b, g = i // 2, (i % 2) * 2 + par
                slots = slot_no(i + (ls - TC + 1) // STEPS_, (ls - TC + 1) % STEPS_)
                if positive(slots):
                    sp.wait_ge(scores_ready, 2 * slots)
                for w, stack, parts in ((0, q_stack[:, c], (0, 0, 1)),
                                        (1, k_stack[:, par, :, c * CH:(c + 1) * CH], (0, 1, 0))):
                    for r, part in enumerate(parts):
                        src = qk_scr[w, part, bass.ds(g * P, P), bass.ds(b * T + c * CH, CH)]
                        sp.dma_start(stack[r * DH:(r + 1) * DH].bitcast(F32),
                                     src.rearrange("(h d) t -> d h t", d=DH)).then_inc(step_loaded[c], 16)
                if c == 0:
                    if positive(slot_no(i, ls) - GROUP_SLOTS):
                        sp.wait_ge(probs_used, slot_no(i, ls) - GROUP_SLOTS)
                    src = v_scr[bass.ds(b * T, T), bass.ds(g * P, P)]
                    sp.dma_start(v_in[:, par], src.rearrange("(k p) n -> p k n", p=P)).then_inc(v_loaded[par], 16)

            def store(i, ls):
                s, c, par = step_no(i, ls), ls % TC, ls // TC % 2
                b, g = i // 2, (i % 2) * 2 + par
                sp.wait_ge(att_lo_ready, s + 1)
                dst = att_scr[:, bass.ds(g * P, P), bass.ds(b * T + c * CH, CH)]
                sp.dma_start(dst.rearrange("w p t -> p w t"), att_out[:, ls % 2].bitcast(F32)).then_inc(att_stored[ls % 2], 16)

            def max_rows(i, ls):
                s, c = step_no(i, ls), ls % TC
                sp.wait_ge(side_read, read_no(i, ls))
                for r, nm in enumerate((nm_hi, nm_lo)):
                    row = q_stack[QK_ROWS + r:QK_ROWS + r + 1, c].rearrange("o h (b t) -> o (h b) t", t=P)
                    sp.dma_start(row.bitcast(F32), nm[:, :].bitcast(F32)).then_inc(nm_stored, 16)

            def after(i, ls, n):
                return i + (ls + n) // STEPS_, (ls + n) % STEPS_

            def body(i):
                for ls in range(STEPS_):
                    if not (is_last(i, N) and ls + 3 >= STEPS_):
                        load(*after(i, ls, 3))
                    if not (isinstance(i, int) and i == 0 and ls == 0):
                        store(*after(i, ls, -1))
                    if not (is_last(i, N) and ls + 1 >= STEPS_):
                        max_rows(*after(i, ls, 1))

            for ls in range(3):
                load(0, ls)
            max_rows(0, 0)
            peeled(sp, body, N)
            store(N - 1, STEPS_ - 1)
            for s in att_stored:
                sp.wait_ge(s, 16 * STEPS_ * N // 2)

        @block.gpsimd
        def _(pool):
            steps = [0]

            def step(instruction):
                instruction.then_inc(const_step, 1)
                steps[0] += 1
                pool.wait_ge(const_step, steps[0])

            step(pool.memset(ones[:, :], 1.0))
            step(pool.memset(ident[:, :], 0.0))
            step(pool.affine_select(out=ident[:, :], in_=ident[:, :], compare_op=ALU.not_equal, fill=1.0,
                                    base=0, pattern=[[-1, P]], channel_multiplier=1))
            step(pool.tensor_copy(ident_b[:, :], ident[:, :]))
            step(pool.affine_select(out=later[:, :], in_=ones[:, :], compare_op=ALU.is_gt, fill=0.0,
                                    base=0, pattern=[[-1, P]], channel_multiplier=1))
            step(pool.memset(mask_qk[:, :], 0.0))
            step(pool.memset(mask_kq[:, :], 0.0))
            step(pool.affine_select(out=mask_qk[:, :], in_=mask_qk[:, :], compare_op=ALU.is_ge, fill=FAR,
                                    base=0, pattern=[[-1, P]], channel_multiplier=1))
            step(pool.affine_select(out=mask_kq[:, :], in_=mask_kq[:, :], compare_op=ALU.is_ge, fill=FAR,
                                    base=0, pattern=[[1, P]], channel_multiplier=-1))
            step(pool.iota(count_i[:, :], pattern=[[-1, T]], base=T - 1, channel_multiplier=0))
            step(pool.tensor_copy(count[:, :], count_i[:, :]))
            step(pool.memset(maxima[0][:, :, :, :], 0.0))
            step(pool.memset(maxima[1][:, :, :, :], 0.0))
            last_query = maxima[1][:, :, RT - 1, 0]
            step(pool.affine_select(out=last_query, in_=last_query, compare_op=ALU.is_gt, fill=FAR,
                                    base=P - 1, pattern=[[0, HG]], channel_multiplier=-1))
            step(pool.memset(k_stack[QK_ROWS:STACK, :, :, :].bitcast(F32), 1.0))
            step(pool.memset(pick[:, :, :].bitcast(F32), 0.0))
            for h in range(HG):
                step(pool.memset(pick[QK_ROWS:STACK, h, h * DH:(h + 1) * DH].bitcast(F32), 1.0))
            pool.memset(later_n[:, 0:2], 0.0).then_inc(const_ready, 1)

            def sum_later(i, par):
                n = SB - 2
                g = 2 * i + par
                pool.wait_ge(v_loaded[par], 16 * (i + 1))
                if positive(slot_no(i, TC * par) - GROUP_SLOTS):
                    pool.wait_ge(probs_used, slot_no(i, TC * par) - GROUP_SLOTS)
                for k in reversed(range(n)):
                    behind = v_in[:, par, SB - 1] if k == n - 1 else v_later[:, par, k + 1]
                    if k < n - 1:
                        pool.wait_ge(v_later_ready, n * g + n - 1 - k)
                    pool.tensor_tensor(v_later[:, par, k], v_in[:, par, k + 1], behind, ALU.add)\
                        .then_inc(v_later_ready, 1)

            def finish(i, ls):
                s, w = step_no(i, ls), ls % 2
                pool.wait_ge(inverse_ready, s + 1)
                if positive(s):
                    pool.wait_ge(att_lo_ready, s)
                pool.tensor_tensor(att[:, :], top[:, :], inverse[:, :], ALU.mult).then_inc(att_ready, 1)
                pool.wait_ge(att_ready, s + 1)
                if positive(16 * (s // 2 if isinstance(s, int) else 4 * i + ls // 2)):
                    pool.wait_ge(att_stored[w], 16 * (4 * i + ls // 2))
                pool.tensor_tensor(att_out[:, w, 0], top[:, :], inverse[:, :], ALU.mult).then_inc(att_hi_ready, 1)
                pool.wait_ge(att_hi_ready, s + 1)
                pool.tensor_tensor(att_out[:, w, 1], att[:, :], att_out[:, w, 0].bitcast(F32), ALU.subtract)\
                    .then_inc(att_lo_ready, 1)

            def body(i):
                for ls in range(STEPS_):
                    s, c = step_no(i, ls), ls % TC
                    pool.wait_ge(weight0_ready, s + 1)
                    if positive(s):
                        pool.wait_ge(sums_read, s)
                    pool.tensor_tensor(later_n[:, :], weight0[:, :], count[:, c * CH:(c + 1) * CH], ALU.mult)\
                        .then_inc(later_n_ready, 1)
                    if not (isinstance(i, int) and i == 0 and ls == 0):
                        finish(i + (ls - 1) // STEPS_, (ls - 1) % STEPS_)
                    if c == TC - 2 and not (is_last(i, N) and ls >= TC):
                        sum_later(i + (ls + TC) // STEPS_, (ls // TC + 1) % 2)

            sum_later(0, 0)
            peeled(pool, body, N)
            finish(N - 1, STEPS_ - 1)

        @block.vector
        def _(dve):
            def take_max(c, m, bank, ready, first_write_after):
                h, tb, sc, width, _ = tile(c, m)
                dve.wait_ge(side_ready, ready)
                out = maxima[c == TC - 1][:, h, tb, sc + 1:sc + 2]
                nc.vector.tensor_reduce(out, ps_side[:, bank, 0:width], AX.X, ALU.max).then_inc(side_read, 1)

            def negate(c, s, reads):
                dve.wait_ge(side_read, reads)
                if positive(s):
                    dve.wait_ge(nm_hi_ready, s)
                nc.vector.tensor_reduce(neg_max[:, :, :], maxima[c == TC - 1][:, :, :, 0:c + 2], AX.X, ALU.max,
                                        negate=True).then_inc(neg_max_ready, 1)

            def max_low(s, bank):
                dve.wait_ge(nm_hi_ready, s + 1)
                nc.vector.tensor_tensor(nm_lo[:, :], ps_side[0:HG * RT, bank, 0:P], nm_hi[:, :].bitcast(F32),
                                        ALU.subtract).then_inc(side_read, 1)

            dve.wait_ge(const_ready, 1)
            for m in range(HG * RT):
                take_max(0, m, m % 2, m + 1, None)
            negate(0, 0, HG * RT)
            max_low(0, (HG * RT) % 2)

            def finalize(i, ls):
                s = step_no(i, ls)
                dve.wait_ge(probs_used, slot_no(i, ls + 1))
                dve.wait_ge(side_read, read_no(i, ls, 1))
                dve.wait_ge(later_n_ready, s + 1)
                if positive(s):
                    dve.wait_ge(att_hi_ready, s)
                nc.vector.tensor_tensor(top[:, :], ps_top[:, :], later_v[:, :], ALU.add)
                nc.vector.tensor_tensor(bottom[:, :], ps_bottom[:, :], later_n[:, :], ALU.add).then_inc(sums_read, 1)
                dve.wait_ge(sums_read, s + 1)
                nc.vector.reciprocal(inverse[:, :], bottom[:, :]).then_inc(inverse_ready, 1)

            def body(i):
                for ls in range(STEPS_):
                    s, c = step_no(i, ls), ls % TC
                    more = not (is_last(i, N) and ls == STEPS_ - 1)
                    if not (isinstance(i, int) and i == 0 and ls == 0):
                        finalize(i + (ls - 1) // STEPS_, (ls - 1) % STEPS_)
                    dve.wait_ge(side_ready, use_no(i, ls, 2))
                    dve.wait_ge(weight0_ready, s + 1)
                    nc.vector.tensor_tensor(later_v[:, :], ps_side[:, side_bank(ls, 1)], weight0[:, :], ALU.mult)\
                        .then_inc(side_read, 1)
                    if not more:
                        continue
                    for m in range(NEXT_TILES[ls]):
                        take_max((c + 1) % TC, m, side_bank(ls, 2 + m), use_no(i, ls, 3 + m), None)
                    negate((c + 1) % TC, s + 1, read_no(i, ls, 1 + NEXT_TILES[ls]))
                    max_low(s + 1, side_bank(ls, 2 + NEXT_TILES[ls]))

            peeled(dve, body, N)
            finalize(N - 1, STEPS_ - 1)

        @block.scalar
        def _(act):
            def exps(i, ls, j):
                c, J = ls % TC, slot_no(i, ls, j)
                w0 = max(0, P * (j - RT * c))
                if positive(J - 1):
                    act.wait_ge(probs_used, J - 1)
                for pair in range(2):
                    act.wait_ge(scores_ready, 2 * J + pair + 1)
                    nc.scalar.activation(probs[:, (SLOTS_BEFORE[ls] + j) % 2, 2 * pair:2 * pair + 2, w0:CH],
                                         ps_scores[:, pair, :, w0:CH], ACT.Exp, scale=SCALE).then_inc(probs_ready, 1)

            def max_high(s, ready, bank):
                act.wait_ge(side_ready, ready)
                if positive(32 * s):
                    act.wait_ge(nm_stored, 32 * s)
                nc.scalar.activation(nm_hi[:, :], ps_side[0:HG * RT, bank, 0:P], ACT.Copy).then_inc(nm_hi_ready, 1)

            max_high(0, FIRST, (FIRST - 1) % 2)

            def body(i):
                for ls in range(STEPS_):
                    s, c = step_no(i, ls), ls % TC
                    more = not (is_last(i, N) and ls == STEPS_ - 1)
                    for j in range(STEP_SLOTS[ls]):
                        exps(i, ls, j)
                        if j == 1:
                            act.wait_ge(side_ready, use_no(i, ls, 1))
                            if positive(s):
                                act.wait_ge(later_n_ready, s)
                            if positive(s):
                                act.wait_ge(side_read, read_no(i, ls) - NEXT_TILES[(ls - 1) % STEPS_] - 1)
                            nc.scalar.activation(weight0[:, :], ps_side[:, side_bank(ls, 0)], ACT.Exp, scale=SCALE)\
                                .then_inc(weight0_ready, 1)
                        if more and j == turn_slot(c) + 1:
                            max_high(s + 1, use_no(i, ls + 1), side_bank(ls, 2 + NEXT_TILES[ls]))

            peeled(act, body, N)

        @block.tensor
        def _(pe):
            def take_scores(i, ls, j, pairs=range(2)):
                c, par, J = ls % TC, ls // TC % 2, slot_no(i, ls, j)
                w0 = max(0, P * (j - RT * c))
                for pair in pairs:
                    if positive(2 * (J - 1) + pair + 1):
                        pe.wait_ge(probs_ready, 2 * (J - 1) + pair + 1)
                    for k in range(2):
                        h = 2 * pair + k
                        masked = j >= RT * c
                        last = nc.tensor.matmul(ps_scores[:, pair, k, w0:CH], k_stack[0:STACK, par, h, j * P:(j + 1) * P],
                                                q_stack[0:STACK, c, h, w0:CH], start=True, stop=not masked)
                        if masked:
                            last = nc.tensor.matmul(ps_scores[:, pair, k, w0:w0 + P], ident_b[:, :], mask_kq[:, :],
                                                    start=False, stop=True)
                    last.then_inc(scores_ready, 1)

            def max_tile(ls, m, bank, count_by):
                c, par = ls % TC, ls // TC % 2
                h, tb, sc, width, masked = tile(c, m)
                last = nc.tensor.matmul(ps_side[:, bank, 0:width], q_stack[0:QK_ROWS, c, h, tb * P:(tb + 1) * P],
                                        k_stack[0:QK_ROWS, par, h, sc * CH:sc * CH + width], start=True, stop=not masked)
                if masked:
                    last = nc.tensor.matmul(ps_side[:, bank, width - P:width], ident_b[:, :], mask_qk[:, :],
                                            start=False, stop=True)
                last.then_inc(side_ready, 1)

            def turn_max(s, bank):
                pe.wait_ge(neg_max_ready, s + 1)
                nc.tensor.transpose(ps_side[0:HG * RT, bank, 0:P], neg_max[:, :, :].rearrange("p h b -> p (h b)"),
                                    ident[:, :]).then_inc(side_ready, 1)

            def loaded(i, ls):
                pe.wait_ge(step_loaded[ls % TC], 96 * (2 * i + ls // TC + 1))

            def spread(i, ls):
                pe.wait_ge(side_read, read_no(i, ls) - 1)
                for h in range(HG):
                    last = nc.tensor.matmul(ps_side[:, side_bank(ls, 0)], pick[0:STACK, h, :],
                                            q_stack[0:STACK, ls % TC, h, :], start=(h == 0), stop=(h == HG - 1))
                last.then_inc(side_ready, 1)

            def behind(i, ls):
                c, par = ls % TC, ls // TC
                pe.wait_ge(side_read, read_no(i, ls))
                pe.wait_ge(v_loaded[par], 16 * (i + 1))
                pe.wait_ge(v_later_ready, (SB - 2) * (2 * i + par + 1))
                for tb in range(RT):
                    k = RT * c + tb
                    out = ps_side[:, side_bank(ls, 1), tb * P:(tb + 1) * P]
                    last = nc.tensor.matmul(out, v_in[:, par, k], later[:, :], start=True, stop=(k == SB - 1))
                    if k < SB - 1:
                        rest = v_in[:, par, SB - 1] if k == SB - 2 else v_later[:, par, k]
                        last = nc.tensor.matmul(out, rest, ones[:, :], start=False, stop=True)
                last.then_inc(side_ready, 1)

            def products(i, ls, j, what):
                c, par, J = ls % TC, ls // TC % 2, slot_no(i, ls, j)
                w0 = max(0, P * (j - RT * c))
                first, stop = j == 0, j == STEP_SLOTS[ls] - 1
                if first and what == 0 and positive(step_no(i, ls)):
                    pe.wait_ge(sums_read, step_no(i, ls))
                for h in range(HG):
                    if what == 0 and h % 2 == 0:
                        pe.wait_ge(probs_ready, 2 * J + h // 2 + 1)
                    rows = slice(h * DH, (h + 1) * DH)
                    out, lhsT = ((ps_top, v_in[:, par, j, rows]), (ps_bottom, ones[:, 0:DH]))[what]
                    last = nc.tensor.matmul(out[rows, w0:CH], lhsT, probs[:, (SLOTS_BEFORE[ls] + j) % 2, h, w0:CH],
                                            start=first, stop=stop)
                if what == 1:
                    last.then_inc(probs_used, 1)

            pe.wait_ge(const_ready, 1)
            loaded(0, 0)
            for m in range(HG * RT):
                if m >= 2:
                    pe.wait_ge(side_read, m - 1)
                max_tile(0, m, m % 2, None)
            pe.wait_ge(side_read, HG * RT - 1)
            turn_max(0, (HG * RT) % 2)
            pe.wait_ge(nm_stored, 32)
            take_scores(0, 0, 0)

            def body(i):
                for ls in range(STEPS_):
                    s, c = step_no(i, ls), ls % TC
                    more = not (is_last(i, N) and ls == STEPS_ - 1)
                    after = (i, ls + 1) if ls + 1 < STEPS_ else (i + 1, 0)
                    for j in range(STEP_SLOTS[ls]):
                        tiles = list(share(c, j)) if more else []

                        def some_tiles(part):
                            for m in tiles[len(tiles) * part // 4:len(tiles) * (part + 1) // 4]:
                                if m == 0:
                                    pe.wait_ge(weight0_ready, s + 1)
                                else:
                                    pe.wait_ge(side_read, read_no(i, ls, m))
                                max_tile(after[1], m, side_bank(ls, 2 + m), None)

                        for pair in range(2):
                            if j + 1 < STEP_SLOTS[ls]:
                                take_scores(i, ls, j + 1, [pair])
                            elif more:
                                if pair == 0:
                                    pe.wait_ge(nm_stored, 32 * (s + 2))
                                take_scores(*after, 0, [pair])
                            if j == 0:
                                (spread, behind)[pair](i, ls)
                                if pair == 1 and more:
                                    loaded(*after)
                            if pair == 1 and j == 0:
                                some_tiles(0)
                            if pair == 1 or j > 0:
                                some_tiles(pair)
                        products(i, ls, j, 0)
                        some_tiles(2)
                        products(i, ls, j, 1)
                        some_tiles(3)
                        if more and j == turn_slot(c):
                            pe.wait_ge(side_read, read_no(i, ls, NEXT_TILES[ls]))
                            turn_max(s + 1, side_bank(ls, 2 + NEXT_TILES[ls]))

            peeled(pe, body, N)


def conclude(nc, x, att_scr, Wo, agg_w, agg_b, in_gamma, in_beta, pn_gamma, pn_beta, d1_w, d1_b, d2_w, d2_b,
             bc_w, bc_b, gate_w, gate_b, out_gamma, out_beta, out):
    outer = ExitStack()
    with outer:
        osb = lambda name, shape, dt=F32: outer.enter_context(nc.sbuf_tensor(name, shape, dt))
        wg_hi = osb("wg_hi", [P, 2, KC, D], F32R)
        wg_lo = osb("wg_lo", [P, 2, KC, D], F32R)
        ident = osb("ident3", [P, P])
        bc_scr = nc.dram_tensor("bc_scr", [B, D], F32, kind="Internal").ap()
        think(nc, x, att_scr, Wo, agg_w, agg_b, in_gamma, in_beta, pn_gamma, pn_beta, d1_w, d1_b, d2_w, d2_b,
              bc_w, bc_b, gate_w, wg_hi, wg_lo, ident, bc_scr)
        gate_all(nc, x, att_scr, gate_b, out_gamma, out_beta, out, wg_hi, wg_lo, ident, bc_scr)


def think(nc, x, att_scr, Wo, agg_w, agg_b, in_gamma, in_beta, pn_gamma, pn_beta, d1_w, d1_b, d2_w, d2_b,
          bc_w, bc_b, gate_w, wg_hi, wg_lo, ident, bc_scr):
    ctx = ExitStack()
    sb = lambda name, shape, dt=F32: ctx.enter_context(nc.sbuf_tensor(name, shape, dt))
    pb = lambda name, shape: ctx.enter_context(nc.psum_tensor(name, shape, F32))
    sem = lambda name: ctx.enter_context(nc.semaphore(name))
    Q = 32
    NQ = P // Q
    with ctx:
        wg_raw = sb("wg_raw", [P, 2, KC, D])
        agg_sb = sb("agg_sb", [P, KC, D])
        bc_sb = sb("bc_sb", [P, KC, D])
        d1_sb = sb("d1_sb", [P, KC, HF])
        d2_sb = sb("d2_sb", [P, HC, D])
        vectors = sb("vectors", [B, 7, D])
        d1_bias = sb("d1_bias", [P, D])
        attT = sb("attT", [P, 2, KC, B], F32R)
        x_last = sb("x_last", [B, D])
        row = sb("row", [B, D])
        normed_row = sb("normed_row", [B, D])
        thought = sb("thought", [B, D])
        partly = sb("partly", [B, D])
        mean_var = sb("mean_var", [B, 2])
        stats = sb("stats3", [B, 6])
        var_eps = sb("var_eps3", [B, 1])
        rstd = sb("rstd3", [B, 1])
        minus_half = sb("minus_half3", [B, 1])
        rowT = sb("rowT", [P, KC, Q])
        hidden = sb("hidden", [P, D])
        hiddenT = sb("hiddenT", [P, KC, P])
        parts = sb("parts", [P, D])
        fold = sb("fold", [P, B])
        bc_row = sb("bc_row", [B, D])
        ps_row = pb("ps_row", [P, D])
        ps_turn = pb("ps_turn", [P, KC, P])
        ps_hidden = pb("ps_hidden", [P, D])
        ps_parts = pb("ps_parts", [P, D])

        const_ready, const_step = sem("const_ready3"), sem("const_step3")
        w_loaded, att_loaded, rows_loaded = sem("w_loaded3"), sem("att_loaded3"), sem("rows_loaded3")
        agg_loaded, bc_loaded, d1_loaded, d2_loaded = (sem(n) for n in ("agg_ld", "bc_ld", "d1_ld", "d2_ld"))
        w_hi_ready, w_lo_ready = sem("w_hi_ready3"), sem("w_lo_ready3")
        link = sem("link3")
        product_ready = sem("product_ready3")
        moments_ready, eps_ready, rstd_ready = sem("moments_ready3"), sem("eps_ready3"), sem("rstd_ready3")
        row_ready, turned, rowT_ready = sem("row_ready3"), sem("turned3"), sem("rowT_ready3")
        hidden_summed, biased, gelu_ready = sem("hidden_summed3"), sem("biased3"), sem("gelu_ready3")
        hidden_turned, hiddenT_ready = sem("hidden_turned3"), sem("hiddenT_ready3")
        parts_summed, parts_ready = sem("parts_summed3"), sem("parts_ready3")
        bc_row_ready, bc_stored = sem("bc_row_ready3"), sem("bc_stored3")
        block = ctx.enter_context(nc.Block())

        @block.sync
        def _(sp):
            sp.dma_start(wg_raw[:, 0], Wo.rearrange("(k p) n -> p k n", p=P)).then_inc(w_loaded, 16)
            last = att_scr.rearrange("w (k p) (b t) -> w p k b t", p=P, b=B)
            for w in range(2):
                for b in range(B):
                    sp.dma_start(attT[:, w, :, b:b + 1].bitcast(F32), last[w, :, :, b, T - 1:T],
                                 allow_slow_non_contiguous=True).then_inc(att_loaded, 16)
            sp.dma_start(x_last[:, :], x[:, T - 1, :]).then_inc(rows_loaded, 16)
            for n, vec in enumerate((in_gamma, in_beta, pn_gamma, pn_beta, agg_b, d2_b, bc_b)):
                sp.dma_start(vectors[:, n], vec.partition_broadcast(B)).then_inc(rows_loaded, 16)
            sp.wait_ge(const_ready, 1)
            for q in range(NQ):
                sp.dma_start(d1_bias[q * Q:q * Q + B, :], d1_b[q * D:(q + 1) * D].partition_broadcast(B))\
                    .then_inc(rows_loaded, 16)
            sp.dma_start(agg_sb[:, :, :], agg_w.rearrange("(k p) n -> p k n", p=P)).then_inc(agg_loaded, 16)
            sp.dma_start(d1_sb[:, :, :], d1_w.rearrange("(k p) n -> p k n", p=P)).then_inc(d1_loaded, 16)
            sp.dma_start(d2_sb[:, :, :], d2_w.rearrange("(k p) n -> p k n", p=P)).then_inc(d2_loaded, 16)
            sp.dma_start(bc_sb[:, :, :], bc_w.rearrange("(k p) n -> p k n", p=P)).then_inc(bc_loaded, 16)
            sp.dma_start(wg_raw[:, 1], gate_w.rearrange("(k p) n -> p k n", p=P)).then_inc(bc_loaded, 16)
            sp.wait_ge(bc_row_ready, 1)
            sp.dma_start(bc_scr, bc_row[:, :]).then_inc(bc_stored, 16)
            sp.wait_ge(bc_stored, 16)

        @block.gpsimd
        def _(pool):
            pool.memset(d1_bias[:, :], 0.0).then_inc(const_step, 1)
            pool.wait_ge(const_step, 1)
            pool.memset(minus_half[:, :], -0.5).then_inc(const_ready, 1)
            pool.memset(ident[:, :], 0.0).then_inc(const_step, 1)
            pool.memset(rowT[:, :, :], 0.0).then_inc(const_step, 1)
            pool.wait_ge(const_step, 3)
            pool.affine_select(out=ident[:, :], in_=ident[:, :], compare_op=ALU.not_equal, fill=1.0,
                               base=0, pattern=[[-1, P]], channel_multiplier=1).then_inc(const_ready, 1)
            for n in range(2 + STEPS):
                pool.wait_ge(moments_ready, n + 1)
                pool.tensor_scalar(var_eps[:, :], mean_var[:, 1:2], LN_EPS if n == 0 else FFN_EPS, None, ALU.add)\
                    .then_inc(eps_ready, 1)
                pool.wait_ge(eps_ready, n + 1)
                pool.tensor_tensor(rstd[:, :], var_eps[:, :], minus_half[:, :], ALU.pow).then_inc(rstd_ready, 1)

        @block.vector
        def _(dve):
            links = [0]

            def linked(instruction):
                instruction.then_inc(link, 1)
                links[0] += 1
                dve.wait_ge(link, links[0])

            def norm(n, src, dst, gamma=None, beta=None):
                linked(nc.vector.bn_stats(stats[:, :], src))
                nc.vector.bn_aggr(mean_var[:, :], stats[:, :]).then_inc(moments_ready, 1)
                dve.wait_ge(moments_ready, n + 1)
                dve.wait_ge(rstd_ready, n + 1)
                linked(nc.vector.tensor_scalar(dst, src, mean_var[:, 0:1], rstd[:, 0:1], ALU.subtract, ALU.mult))
                if gamma is not None:
                    linked(nc.vector.tensor_tensor(dst, dst, vectors[:, gamma], ALU.mult))
                    nc.vector.tensor_tensor(dst, dst, vectors[:, beta], ALU.add).then_inc(row_ready, 1)
                    dve.wait_ge(row_ready, n)

            def copy_rowT(n):
                dve.wait_ge(turned, n)
                nc.vector.tensor_copy(rowT[:, :, 0:B], ps_turn[:, :, 0:B]).then_inc(rowT_ready, 1)

            dve.wait_ge(const_ready, 2)
            linked(nc.vector.tensor_reduce(fold[:, :], ident[:, :].rearrange("p (q b) -> p b q", q=NQ)[:, 0:B],
                                           AX.X, ALU.add))
            dve.wait_ge(w_hi_ready, 1)
            nc.vector.tensor_tensor(wg_lo[:, 0], wg_raw[:, 0], wg_hi[:, 0].bitcast(F32), ALU.subtract)\
                .then_inc(w_lo_ready, 1)
            dve.wait_ge(rows_loaded, 16 * (8 + NQ))
            dve.wait_ge(product_ready, 1)
            linked(nc.vector.tensor_tensor(row[:, :], ps_row[0:B, :], x_last[:, :], ALU.add))
            norm(0, row[:, :], row[:, :])
            norm(1, row[:, :], normed_row[:, :], 0, 1)
            copy_rowT(1)
            dve.wait_ge(product_ready, 2)
            linked(nc.vector.tensor_tensor(thought[:, :], ps_row[0:B, :], vectors[:, 4], ALU.add))
            for k in range(STEPS):
                norm(2 + k, thought[:, :], normed_row[:, :], 2, 3)
                copy_rowT(2 + k)
                linked(nc.vector.tensor_tensor(partly[:, :], thought[:, :], vectors[:, 5], ALU.add))
                dve.wait_ge(hidden_summed, k + 1)
                nc.vector.tensor_tensor(hidden[:, :], ps_hidden[:, :], d1_bias[:, :], ALU.add).then_inc(biased, 1)
                dve.wait_ge(hidden_turned, k + 1)
                nc.vector.tensor_copy(hiddenT[:, :, :], ps_turn[:, :, :]).then_inc(hiddenT_ready, 1)
                dve.wait_ge(product_ready, 3 + k)
                done = nc.vector.tensor_tensor(thought[:, :], ps_row[0:B, :], partly[:, :], ALU.add)
                if k < STEPS - 1:
                    linked(done)
                else:
                    done.then_inc(row_ready, 1)
            copy_rowT(2 + STEPS)
            dve.wait_ge(product_ready, 3 + STEPS)
            nc.vector.tensor_tensor(bc_row[:, :], ps_row[0:B, :], vectors[:, 6], ALU.add).then_inc(bc_row_ready, 1)
            dve.wait_ge(w_hi_ready, 2)
            nc.vector.tensor_tensor(wg_lo[:, 1], wg_raw[:, 1], wg_hi[:, 1].bitcast(F32), ALU.subtract)\
                .then_inc(w_lo_ready, 1)

        @block.scalar
        def _(act):
            act.wait_ge(w_loaded, 16)
            nc.scalar.activation(wg_hi[:, 0], wg_raw[:, 0], ACT.Copy).then_inc(w_hi_ready, 1)
            for k in range(STEPS):
                act.wait_ge(biased, k + 1)
                nc.scalar.activation(hidden[:, :], hidden[:, :], ACT.Gelu).then_inc(gelu_ready, 1)
                act.wait_ge(parts_summed, k + 1)
                nc.scalar.activation(parts[:, :], ps_parts[:, :], ACT.Copy).then_inc(parts_ready, 1)
            act.wait_ge(bc_loaded, 32)
            nc.scalar.activation(wg_hi[:, 1], wg_raw[:, 1], ACT.Copy).then_inc(w_hi_ready, 1)

        @block.tensor
        def _(pe):
            def turn_row(n, src):
                pe.wait_ge(row_ready, n)
                if n >= 2:
                    pe.wait_ge(rowT_ready, n - 1)
                if n >= 3:
                    pe.wait_ge(hiddenT_ready, n - 2)
                for c in range(KC):
                    last = nc.tensor.transpose(ps_turn[:, c, 0:B], src[:, c * P:(c + 1) * P], ident[0:B, 0:B])
                last.then_inc(turned, 1)
                pe.wait_ge(rowT_ready, n)

            def row_product(w):
                for c in range(KC):
                    last = nc.tensor.matmul(ps_row[0:B, :], rowT[:, c, 0:B], w[:, c], start=(c == 0), stop=(c == KC - 1))
                last.then_inc(product_ready, 1)

            pe.wait_ge(att_loaded, 32 * B)
            pe.wait_ge(w_lo_ready, 1)
            for c in range(KC):
                for t, (a, w) in enumerate(((0, wg_hi), (0, wg_lo), (1, wg_hi))):
                    last = nc.tensor.matmul(ps_row[0:B, :], attT[:, a, c, :], w[:, 0, c], start=(c == 0 and t == 0),
                                            stop=(c == KC - 1 and t == 2))
            last.then_inc(product_ready, 1)
            turn_row(1, normed_row)
            pe.wait_ge(agg_loaded, 16)
            row_product(agg_sb)
            for k in range(STEPS):
                turn_row(2 + k, normed_row)
                pe.wait_ge(d1_loaded, 16)
                for c in range(KC):
                    for q in range(NQ):
                        last = nc.tensor.matmul(ps_hidden[q * Q:(q + 1) * Q, :], rowT[:, c, :],
                                                d1_sb[:, c, q * D:(q + 1) * D], start=(c == 0), stop=(c == KC - 1))
                last.then_inc(hidden_summed, 1)
                pe.wait_ge(gelu_ready, k + 1)
                for c in range(KC):
                    last = nc.tensor.transpose(ps_turn[:, c, :], hidden[:, c * P:(c + 1) * P], ident[:, :])
                last.then_inc(hidden_turned, 1)
                pe.wait_ge(hiddenT_ready, k + 1)
                pe.wait_ge(d2_loaded, 16)
                if k:
                    pe.wait_ge(parts_ready, k)
                for c in range(KC):
                    for q in range(NQ):
                        last = nc.tensor.matmul(ps_parts[q * Q:(q + 1) * Q, :], hiddenT[:, c, q * Q:(q + 1) * Q],
                                                d2_sb[:, KC * q + c], start=(c == 0), stop=(c == KC - 1))
                last.then_inc(parts_summed, 1)
                pe.wait_ge(parts_ready, k + 1)
                nc.tensor.matmul(ps_row[0:B, :], fold[:, :], parts[:, :], start=True, stop=True).then_inc(product_ready, 1)
            turn_row(2 + STEPS, thought)
            pe.wait_ge(bc_loaded, 32)
            row_product(bc_sb)


def gate_all(nc, x, att_scr, gate_b, out_gamma, out_beta, out, wg_hi, wg_lo, ident, bc_scr):
    ctx = ExitStack()
    sb = lambda name, shape, dt=F32: ctx.enter_context(nc.sbuf_tensor(name, shape, dt))
    pb = lambda name, shape: ctx.enter_context(nc.psum_tensor(name, shape, F32))
    sem = lambda name: ctx.enter_context(nc.semaphore(name))
    N = CHUNKS // 2
    R = 2 * RT
    TILES = N * R
    LAG1, LAG2, LAG3 = 1, 2, 3
    with ctx:
        attT = sb("attT4", [P, 2, 2, KC, CH], F32R)
        x_in = sb("x_in4", [P, 2, RT, D])
        gate_bias = sb("gate_bias", [P, D])
        gamma = sb("gamma4", [P, D])
        beta = sb("beta4", [P, D])
        x1 = sb("x1", [P, 4, D])
        x1_beta = sb("x1_beta", [P, 4, D])
        x2 = sb("x2", [P, 4, D])
        x2T_hi = sb("x2T_hi", [P, 2, KC, P], F32R)
        x2T_lo = sb("x2T_lo", [P, 2, KC, P], F32R)
        gate = sb("gate4", [P, 2, D])
        gated = sb("gated4", [P, 2, D])
        normed = sb("normed4", [P, 2, D])
        result = sb("result4", [P, 4, D])
        stats = sb("stats4", [P, 2, 6])
        mom = sb("mom4", [P, 4, 2, 2])
        eps_var = sb("eps_var4", [P, 4, 2])
        rstd = sb("rstd4", [P, 4, 2])
        minus_half = sb("minus_half4", [P, 1])
        eps = sb("eps4", [P, 2])
        bc_in = sb("bc_in4", [P, 2, D])
        ps_y = pb("ps_y", [P, 2, D])
        ps_t = pb("ps_t4", [P, 2, KC, P])
        ps_g = pb("ps_g", [P, 2, D])

        const_ready = sem("const_ready4")
        loaded = [sem(f"loaded4{p}") for p in range(2)]
        vec_loaded = sem("vec_loaded4")
        y_ready, x1_ready, x1_beta_ready = sem("y_ready4"), sem("x1_ready4"), sem("x1_beta_ready4")
        stats_ready = [sem(f"stats_ready4{w}") for w in range(2)]
        mom_ready = [sem(f"mom_ready4{w}") for w in range(2)]
        eps_ready = [sem(f"eps_ready4{w}") for w in range(2)]
        rstd_ready = [sem(f"rstd_ready4{w}") for w in range(2)]
        x2_ready, turned, hi_ready, lo_ready = sem("x2_ready4"), sem("turned4"), sem("hi_ready4"), sem("lo_ready4")
        g_ready, biased, gate_ready, gated_ready = (sem(n) for n in ("g_ready4", "biased4", "gate_ready4", "gated_ready4"))
        sum_ready, normed_ready = sem("sum_ready4"), sem("normed_ready4")
        scaled_ready, result_ready = sem("scaled_ready4"), sem("result_ready4")
        stored = [sem(f"stored4{p}") for p in range(4)]
        block = ctx.enter_context(nc.Block())

        x_rows = x.rearrange("b (r p) d -> p (b r) d", p=P)
        out_rows = out.rearrange("b (r p) d -> p (b r) d", p=P)

        @block.sync
        def _(sp):
            for dst, vec in ((gate_bias, gate_b), (gamma, out_gamma), (beta, out_beta)):
                sp.dma_start(dst[:, :], vec.partition_broadcast(P)).then_inc(vec_loaded, 16)

            def load(i, par):
                n = 2 * i + par
                if positive(RT * (n - 1)):
                    sp.wait_ge(x1_ready, RT * (n - 1))
                    sp.wait_ge(gated_ready, RT * (n - 1))
                src = att_scr.rearrange("w (k p) t -> w p k t", p=P)
                for w in range(2):
                    sp.dma_start(attT[:, par, w].bitcast(F32), src[w, :, :, bass.ds(n * CH, CH)]).then_inc(loaded[par], 16)
                sp.dma_start(x_in[:, par], x_rows[:, bass.ds(n * RT, RT), :]).then_inc(loaded[par], 16)
                b = i // 2
                sp.dma_start(bc_in[:, par], bc_scr[bass.ds(b, 1), :].rearrange("o d -> (o d)").partition_broadcast(P))\
                    .then_inc(loaded[par], 16)

            def body(i):
                for r in range(R):
                    m = R * i + r
                    if r % RT == 0 and not (is_last(i, N) and r == RT):
                        load(i + (r // RT + 1) // 2, (r // RT + 1) % 2)
                    sp.wait_ge(result_ready, m + 1)
                    sp.dma_start(out_rows[:, bass.ds(m, 1), :].rearrange("p o d -> p (o d)"), result[:, r % 4])\
                        .then_inc(stored[r % 4], 16)

            load(0, 0)
            peeled(sp, body, N)
            for s in stored:
                sp.wait_ge(s, 16 * TILES // 4)

        def staged(stages):
            def body(i):
                for r in range(R):
                    for lag, stage in stages:
                        if positive(R * i + r - lag + 1):
                            stage(i + (r - lag) // R, (r - lag) % R)
            return body

        def rest(stages):
            for late in range(max(lag for lag, _ in stages)):
                for lag, stage in stages:
                    if lag > late:
                        r = R + late - lag
                        stage(N - 1 + r // R, r % R)

        @block.gpsimd
        def _(pool):
            pool.memset(minus_half[:, :], -0.5).then_inc(const_ready, 1)
            for w, value in enumerate((LN_EPS, FFN_EPS)):
                pool.memset(eps[:, w:w + 1], value).then_inc(const_ready, 1)
            pool.wait_ge(const_ready, 3)
            pool.wait_ge(vec_loaded, 48)

            def invert(w):
                def stage(i, r):
                    m, v = R * i + r, r % 4
                    pool.wait_ge(mom_ready[w], m + 1)
                    if positive(m - 3):
                        pool.wait_ge((x2_ready, normed_ready)[w], m - 3)
                    pool.tensor_tensor(eps_var[:, v, w:w + 1], mom[:, v, w, 1:2], eps[:, w:w + 1], ALU.add)\
                        .then_inc(eps_ready[w], 1)
                    pool.wait_ge(eps_ready[w], m + 1)
                    pool.tensor_tensor(rstd[:, v, w:w + 1], eps_var[:, v, w:w + 1], minus_half[:, :], ALU.pow)\
                        .then_inc(rstd_ready[w], 1)
                return stage

            def add_beta(i, r):
                m, v = R * i + r, r % 4
                pool.wait_ge(x1_ready, m + 1)
                if positive(m - 3):
                    pool.wait_ge(result_ready, m - 3)
                pool.tensor_tensor(x1_beta[:, v], x1[:, v], beta[:, :], ALU.add).then_inc(x1_beta_ready, 1)

            def gate_bc(i, r):
                m, u = R * i + r, r % 2
                pool.wait_ge(gate_ready, m + 1)
                if positive(m - 1):
                    pool.wait_ge(normed_ready, m - 1)
                pool.tensor_tensor(gated[:, u], gate[:, u], bc_in[:, r // RT], ALU.mult).then_inc(gated_ready, 1)

            def scale(i, r):
                m, u = R * i + r, r % 2
                pool.wait_ge(normed_ready, m + 1)
                pool.tensor_tensor(normed[:, u], normed[:, u], gamma[:, :], ALU.mult).then_inc(scaled_ready, 1)

            stages = ((0, invert(0)), (LAG2, invert(1)), (LAG2, scale), (0, add_beta), (LAG1, gate_bc))
            peeled(pool, staged(stages), N)
            rest(stages)

        @block.vector
        def _(dve):
            dve.wait_ge(vec_loaded, 48)

            def first(i, r):
                m, v = R * i + r, r % 4
                dve.wait_ge(loaded[r // RT], 64 * (i + 1))
                dve.wait_ge(y_ready, m + 1)
                if positive(m - 3):
                    dve.wait_ge(x1_beta_ready, m - 3)
                nc.vector.tensor_tensor(x1[:, v], ps_y[:, r % 2], x_in[:, r // RT, r % RT], ALU.add).then_inc(x1_ready, 1)
                dve.wait_ge(x1_ready, m + 1)
                nc.vector.bn_stats(stats[:, 0], x1[:, v]).then_inc(stats_ready[0], 1)

            def moments(w):
                def stage(i, r):
                    m = R * i + r
                    if isinstance(m, int):
                        dve.wait_ge(stats_ready[w], m + 1)
                    nc.vector.bn_aggr(mom[:, r % 4, w], stats[:, w]).then_inc(mom_ready[w], 1)
                return stage

            def normalise(i, r):
                m, v = R * i + r, r % 4
                dve.wait_ge(mom_ready[0], m + 1)
                dve.wait_ge(rstd_ready[0], m + 1)
                nc.vector.tensor_scalar(x2[:, v], x1[:, v], mom[:, v, 0, 0:1], rstd[:, v, 0:1], ALU.subtract, ALU.mult)\
                    .then_inc(x2_ready, 1)

            def low(i, r):
                m, u = R * i + r, r % 2
                dve.wait_ge(hi_ready, m + 1)
                nc.vector.tensor_tensor(x2T_lo[:, u], ps_t[:, u], x2T_hi[:, u].bitcast(F32), ALU.subtract).then_inc(lo_ready, 1)

            def bias(i, r):
                m, u = R * i + r, r % 2
                dve.wait_ge(g_ready, m + 1)
                if positive(m - 1):
                    dve.wait_ge(gated_ready, m - 1)
                nc.vector.tensor_tensor(gate[:, u], ps_g[:, u], gate_bias[:, :], ALU.add).then_inc(biased, 1)

            def add_x2(i, r):
                m, v, u = R * i + r, r % 4, r % 2
                if not isinstance(m, int):
                    dve.wait_ge(stats_ready[0], m + LAG2 + 1)
                    dve.wait_ge(rstd_ready[0], m + LAG2 - 3)
                dve.wait_ge(gated_ready, m + 1)
                nc.vector.tensor_tensor(gated[:, u], gated[:, u], x2[:, v], ALU.add).then_inc(sum_ready, 1)
                dve.wait_ge(sum_ready, m + 1)
                nc.vector.bn_stats(stats[:, 1], gated[:, u]).then_inc(stats_ready[1], 1)

            def normalise2(i, r):
                m, v, u = R * i + r, r % 4, r % 2
                dve.wait_ge(mom_ready[1], m + 1)
                dve.wait_ge(rstd_ready[1], m + 1)
                if positive(m - 1):
                    dve.wait_ge(result_ready, m - 1)
                nc.vector.tensor_scalar(normed[:, u], gated[:, u], mom[:, v, 1, 0:1], rstd[:, v, 1:2],
                                        ALU.subtract, ALU.mult).then_inc(normed_ready, 1)

            def add_up(i, r):
                m, v, u = R * i + r, r % 4, r % 2
                if not isinstance(m, int):
                    dve.wait_ge(stats_ready[1], m + LAG3 - LAG2 + 1)
                    dve.wait_ge(rstd_ready[1], m + LAG3 - LAG2 - 3)
                dve.wait_ge(scaled_ready, m + 1)
                dve.wait_ge(x1_beta_ready, m + 1)
                if positive(m - 3):
                    dve.wait_ge(stored[v], 16 * (2 * i + r // 4))
                nc.vector.tensor_tensor(result[:, v], normed[:, u], x1_beta[:, v], ALU.add).then_inc(result_ready, 1)

            stages = ((LAG1, low), (0, first), (LAG2, add_x2), (0, moments(0)), (LAG3, add_up), (LAG2, moments(1)),
                      (0, normalise), (LAG2, normalise2), (LAG1, bias))
            peeled(dve, staged(stages), N)
            rest(stages)

        @block.scalar
        def _(act):
            def high(i, r):
                m, u = R * i + r, r % 2
                act.wait_ge(turned, m + 1)
                if positive(m - 1):
                    act.wait_ge(g_ready, m - 1)
                nc.scalar.activation(x2T_hi[:, u], ps_t[:, u], ACT.Copy).then_inc(hi_ready, 1)

            def sigmoid(i, r):
                m, u = R * i + r, r % 2
                act.wait_ge(biased, m + 1)
                nc.scalar.activation(gate[:, u], gate[:, u], ACT.Sigmoid).then_inc(gate_ready, 1)

            stages = ((LAG1, sigmoid), (0, high))
            peeled(act, staged(stages), N)
            rest(stages)

        @block.tensor
        def _(pe):
            def project(i, r):
                m, par = R * i + r, r // RT
                pe.wait_ge(loaded[par], 64 * (i + 1))
                if positive(m - 1):
                    pe.wait_ge(x1_ready, m - 1)
                for c in range(KC):
                    for t, (a, w) in enumerate(((0, wg_hi), (0, wg_lo), (1, wg_hi))):
                        last = nc.tensor.matmul(ps_y[:, r % 2], attT[:, par, a, c, (r % RT) * P:(r % RT + 1) * P], w[:, 0, c],
                                                start=(c == 0 and t == 0), stop=(c == KC - 1 and t == 2))
                last.then_inc(y_ready, 1)

            def turn(i, r):
                m, u, v = R * i + r, r % 2, r % 4
                pe.wait_ge(x2_ready, m + 1)
                if positive(m - 1):
                    pe.wait_ge(lo_ready, m - 1)
                for c in range(KC):
                    last = nc.tensor.transpose(ps_t[:, u, c], x2[:, v, c * P:(c + 1) * P], ident[:, :])
                last.then_inc(turned, 1)

            def gates(i, r):
                m, u = R * i + r, r % 2
                pe.wait_ge(lo_ready, m + 1)
                if positive(m - 1):
                    pe.wait_ge(biased, m - 1)
                for c in range(KC):
                    for t, (xT, w) in enumerate(((x2T_hi, wg_hi), (x2T_hi, wg_lo), (x2T_lo, wg_hi))):
                        last = nc.tensor.matmul(ps_g[:, u], xT[:, u, c], w[:, 1, c],
                                                start=(c == 0 and t == 0), stop=(c == KC - 1 and t == 2))
                last.then_inc(g_ready, 1)

            stages = ((0, project), (LAG1, gates), (0, turn))
            peeled(pe, staged(stages), N)
            rest(stages)


def build(nc, x, Wq, Wk, Wv, Wo, in_gamma, in_beta, agg_w, agg_b, pn_gamma, pn_beta, d1_w, d1_b, d2_w, d2_b,
          bc_w, bc_b, gate_w, gate_b, out_gamma, out_beta, out):
    qk_scr = nc.dram_tensor("qk_scr", [2, 2, D, B * T], F32, kind="Internal").ap()
    v_scr = nc.dram_tensor("v_scr", [B * T, D], F32, kind="Internal").ap()
    att_scr = nc.dram_tensor("att_scr", [2, D, B * T], F32, kind="Internal").ap()
    project(nc, x, Wq, Wk, Wv, qk_scr, v_scr)
    attend(nc, qk_scr, v_scr, att_scr)
    conclude(nc, x, att_scr, Wo, agg_w, agg_b, in_gamma, in_beta, pn_gamma, pn_beta, d1_w, d1_b, d2_w, d2_b,
             bc_w, bc_b, gate_w, gate_b, out_gamma, out_beta, out)


_INS = ["L0_attn_x", "L0_attn_Wq", "L0_attn_Wk", "L0_attn_Wv", "L0_attn_Wo", "L0_ffn_in_gamma", "L0_ffn_in_beta",
        "L0_ffn_agg_w", "L0_ffn_agg_b", "L0_ffn_pn_gamma", "L0_ffn_pn_beta", "L0_ffn_d1_w", "L0_ffn_d1_b",
        "L0_ffn_d2_w", "L0_ffn_d2_b", "L0_ffn_bc_w", "L0_ffn_bc_b", "L0_ffn_gate_w", "L0_ffn_gate_b",
        "L0_ffn_out_gamma", "L0_ffn_out_beta"]


def kernel(**inputs):
    import numpy as _np
    import concourse.bacc as _bacc
    from concourse import mybir as _mybir
    from concourse.bass_utils import run_bass_kernel_spmd as _run

    nc = _bacc.Bacc("TRN2", target_bir_lowering=False, num_devices=1)
    arrays, args = {}, []
    for name in _INS:
        a = _np.ascontiguousarray(inputs[name])
        arrays[f"in_{name}"] = a
        args.append(nc.dram_tensor(f"in_{name}", a.shape, _mybir.dt.from_np(a.dtype), kind="ExternalInput").ap())
    args.append(nc.dram_tensor("out_x", (B, T, D), _mybir.dt.float32, kind="ExternalOutput").ap())
    build(nc, *args)
    r = _run(nc, [arrays], core_ids=[0])
    return r.results[0]["out_x"]
```

```python
import concourse.bass as bass
from concourse import mybir
from concourse.alu_op_type import AluOpType as ALU
from contextlib import ExitStack

ACT = mybir.ActivationFunctionType
AX = mybir.AxisListType
F32 = mybir.dt.float32
F32R = mybir.dt.float32r
BF16 = mybir.dt.bfloat16

P = 128
B, T, D = 4, 2048, 512
HEADS = 16
DH = D // HEADS
HG = P // DH
GROUPS = HEADS // HG
KC = D // P
CH = 512
RT = CH // P
CHUNKS = B * T // CH
TC = T // CH
SB = T // P
HF = 2048
HC = HF // P
STEPS = 4
LN_EPS, FFN_EPS = 1e-5, 1e-6
SCALE = float(T) ** -0.5


def positive(value):
    return not isinstance(value, int) or value > 0


def peeled(eng, body, n):
    body(0)
    with eng.Fori(1, n - 1) as i:
        body(i)
    body(n - 1)


def is_last(i, n):
    return isinstance(i, int) and i == n - 1


def project(nc, x, Wq, Wk, Wv, qk_scr, v_scr):
    ctx = ExitStack()
    sb = lambda name, shape, dt=F32: ctx.enter_context(nc.sbuf_tensor(name, shape, dt))
    pb = lambda name, shape: ctx.enter_context(nc.psum_tensor(name, shape, F32))
    sem = lambda name: ctx.enter_context(nc.semaphore(name))
    QK_TILES, V_TILES = 2 * GROUPS, RT
    BANKS = 6
    with ctx:
        w_raw = sb("w_raw", [P, 3, KC, D])
        w_hi = sb("w_hi", [P, 3, KC, D], F32R)
        w_lo = sb("w_lo", [P, 3, KC, D], F32R)
        x_in = sb("x_in", [P, 2, RT, D])
        xT_hi = sb("xT_hi", [P, 2, KC, CH], F32R)
        xT_lo = sb("xT_lo", [P, 2, KC, CH], F32R)
        qk_out = sb("qk_out", [P, QK_TILES, 2, CH], F32R)
        v_out = sb("v_out", [P, V_TILES, D])
        stats = sb("stats", [P, 2, RT, 6])
        moments = sb("moments", [P, 2, RT, 2])
        var_eps = sb("var_eps", [P, 2, RT])
        rstd = sb("rstd", [P, 2, RT])
        minus_half = sb("minus_half", [P, RT])
        eps = sb("eps", [P, RT])
        ident = sb("ident", [P, P])
        ps_t = pb("ps_t", [P, 2, CH])
        ps_mm = pb("ps_mm", [P, BANKS, CH])

        w_loaded = sem("w_loaded")
        w_hi_ready, w_lo_ready = sem("w_hi_ready"), sem("w_lo_ready")
        x_loaded = [sem(f"x_loaded{p}") for p in range(2)]
        const_ready = sem("const_ready")
        stats_ready, moments_ready = sem("stats_ready"), sem("moments_ready")
        eps_ready, rstd_ready = sem("eps_ready"), sem("rstd_ready")
        norm_ready = sem("norm_ready")
        transposed = sem("transposed")
        xT_hi_ready, xT_lo_ready = sem("xT_hi_ready"), sem("xT_lo_ready")
        product_ready = sem("product_ready")
        qk_hi_ready, qk_lo_ready, v_ready = sem("qk_hi_ready"), sem("qk_lo_ready"), sem("v_ready")
        qk_stored = [sem(f"qk_stored{k}") for k in range(QK_TILES)]
        v_stored = [sem(f"v_stored{r}") for r in range(V_TILES)]

        block = ctx.enter_context(nc.Block())
        N = CHUNKS // 2

        x_rows = x.rearrange("b (r p) d -> p (b r) d", p=P)
        qk_cols = qk_scr.rearrange("w s (g p) t -> w g p s t", p=P)

        @block.sync
        def _(sp):
            for w, W in enumerate((Wq, Wk, Wv)):
                sp.dma_start(w_raw[:, w], W.rearrange("(k p) n -> p k n", p=P)).then_inc(w_loaded, 16)

            def load(i, par):
                n = 2 * i + par
                if positive(KC * (n - 1)):
                    sp.wait_ge(transposed, KC * (n - 1))
                sp.dma_start(x_in[:, par], x_rows[:, bass.ds(n * RT, RT), :]).then_inc(x_loaded[par], 16)

            def store(i, par):
                n = 2 * i + par
                for k in range(QK_TILES):
                    sp.wait_ge(qk_lo_ready, QK_TILES * n + k + 1)
                    sp.dma_start(qk_cols[k // GROUPS, k % GROUPS, :, :, bass.ds(n * CH, CH)],
                                 qk_out[:, k].bitcast(F32)).then_inc(qk_stored[k], 16)
                for r in range(V_TILES):
                    sp.wait_ge(v_ready, V_TILES * n + r + 1)
                    sp.dma_start(v_scr[bass.ds(n * CH + r * P, P), :], v_out[:, r]).then_inc(v_stored[r], 16)

            def pair(i):
                for par in range(2):
                    store(i, par)
                    if not is_last(i, N):
                        load(i + 1, par)

            load(0, 0)
            load(0, 1)
            peeled(sp, pair, N)
            for s in qk_stored + v_stored:
                sp.wait_ge(s, 16 * CHUNKS)

        @block.gpsimd
        def _(pool):
            pool.memset(minus_half[:, :], -0.5).then_inc(const_ready, 1)
            pool.memset(eps[:, :], LN_EPS).then_inc(const_ready, 1)
            pool.memset(ident[:, :], 0.0).then_inc(const_ready, 1)
            pool.wait_ge(const_ready, 3)
            pool.affine_select(out=ident[:, :], in_=ident[:, :], compare_op=ALU.not_equal, fill=1.0,
                               base=0, pattern=[[-1, P]], channel_multiplier=1).then_inc(const_ready, 1)

            def pair(i):
                for par in range(2):
                    n = 2 * i + par
                    pool.wait_ge(moments_ready, RT * (n + 1))
                    if positive(RT * (n - 1)):
                        pool.wait_ge(norm_ready, RT * (n - 1))
                    pool.tensor_tensor(var_eps[:, par], moments[:, par, :, 1], eps[:, :], ALU.add).then_inc(eps_ready, 1)
                    pool.wait_ge(eps_ready, n + 1)
                    pool.tensor_tensor(rstd[:, par], var_eps[:, par], minus_half[:, :],
                                       ALU.pow).then_inc(rstd_ready, 1)

            peeled(pool, pair, N)

        @block.vector
        def _(dve):
            def chunk_stats(n, par, first=False):
                dve.wait_ge(x_loaded[par], (n // 2 + 1) * 16 if isinstance(n, int) else (n - par) * 8 + 16)
                if positive(n - 1):
                    dve.wait_ge(rstd_ready, n - 1)
                for r in range(RT):
                    nc.vector.bn_stats(stats[:, par, r], x_in[:, par, r]).then_inc(stats_ready, 1)

            def chunk_moments(n, par):
                for r in range(RT):
                    nc.vector.bn_aggr(moments[:, par, r], stats[:, par, r]).then_inc(moments_ready, 1)

            def chunk_norm(n, par):
                dve.wait_ge(rstd_ready, n + 1)
                dve.wait_ge(moments_ready, RT * (n + 1))
                for r in range(RT):
                    nc.vector.tensor_scalar(x_in[:, par, r], x_in[:, par, r], moments[:, par, r, 0:1],
                                            rstd[:, par, r:r + 1], ALU.subtract, ALU.mult).then_inc(norm_ready, 1)

            def xT_low(n, par, c):
                dve.wait_ge(xT_hi_ready, KC * n + c + 1)
                nc.vector.tensor_tensor(xT_lo[:, par, c], ps_t[:, c % 2], xT_hi[:, par, c].bitcast(F32),
                                        ALU.subtract).then_inc(xT_lo_ready, 1)

            def qk_low(n, k, stats_too=False):
                if stats_too:
                    dve.wait_ge(stats_ready, RT * (n + 2))
                dve.wait_ge(qk_hi_ready, QK_TILES * n + k + 1)
                nc.vector.tensor_tensor(qk_out[:, k, 1], ps_mm[:, k % BANKS], qk_out[:, k, 0].bitcast(F32),
                                        ALU.subtract).then_inc(qk_lo_ready, 1)

            chunk_stats(0, 0)
            dve.wait_ge(stats_ready, RT)
            chunk_moments(0, 0)
            chunk_norm(0, 0)
            dve.wait_ge(w_loaded, 48)
            for w in range(3):
                dve.wait_ge(w_hi_ready, w + 1)
                nc.vector.tensor_tensor(w_lo[:, w], w_raw[:, w], w_hi[:, w].bitcast(F32),
                                        ALU.subtract).then_inc(w_lo_ready, 1)
            for c in range(KC):
                xT_low(0, 0, c)

            def pair(i):
                for par in range(2):
                    n = 2 * i + par
                    more = not (is_last(i, N) and par == 1)
                    if more:
                        chunk_stats(n + 1, 1 - par)
                    for k in range(4):
                        qk_low(n, k, stats_too=more and k == 0)
                        if more and k == 0:
                            chunk_moments(n + 1, 1 - par)
                    if more:
                        chunk_norm(n + 1, 1 - par)
                    for k in range(4, QK_TILES):
                        qk_low(n, k)
                        if more and k >= 5:
                            for c in ((0, 1), (2,), (3,))[k - 5]:
                                xT_low(n + 1, 1 - par, c)

            peeled(dve, pair, N)

        @block.scalar
        def _(act):
            act.wait_ge(w_loaded, 48)
            for w in range(3):
                nc.scalar.activation(w_hi[:, w], w_raw[:, w], ACT.Copy).then_inc(w_hi_ready, 1)

            def xT_high(n, par, c):
                act.wait_ge(transposed, KC * n + c + 1)
                if positive((QK_TILES + V_TILES) * (n - 1)):
                    act.wait_ge(product_ready, (QK_TILES + V_TILES) * (n - 1))
                nc.scalar.activation(xT_hi[:, par, c], ps_t[:, c % 2], ACT.Copy).then_inc(xT_hi_ready, 1)

            for c in range(KC):
                xT_high(0, 0, c)

            def pair(i):
                for par in range(2):
                    n = 2 * i + par
                    more = not (is_last(i, N) and par == 1)
                    for k in range(QK_TILES):
                        act.wait_ge(product_ready, (QK_TILES + V_TILES) * n + k + 1)
                        if positive(16 * n):
                            act.wait_ge(qk_stored[k], 16 * n)
                        nc.scalar.activation(qk_out[:, k, 0], ps_mm[:, k % BANKS], ACT.Copy).then_inc(qk_hi_ready, 1)
                        if more and k >= 5:
                            for c in ((0, 1), (2,), (3,))[k - 5]:
                                xT_high(n + 1, 1 - par, c)
                    for r in range(V_TILES):
                        act.wait_ge(product_ready, (QK_TILES + V_TILES) * n + QK_TILES + r + 1)
                        if positive(16 * n):
                            act.wait_ge(v_stored[r], 16 * n)
                        nc.scalar.activation(v_out[:, r], ps_mm[:, (QK_TILES + r) % BANKS], ACT.Copy).then_inc(v_ready, 1)

            peeled(act, pair, N)

        @block.tensor
        def _(pe):
            def transposes(n, par, c):
                if c == 0:
                    pe.wait_ge(norm_ready, RT * (n + 1))
                if positive(KC * n + c - 1):
                    pe.wait_ge(xT_lo_ready, KC * n + c - 1)
                for r in range(RT):
                    last = nc.tensor.transpose(ps_t[:, c % 2, r * P:(r + 1) * P], x_in[:, par, r, c * P:(c + 1) * P],
                                               ident[:, :])
                last.then_inc(transposed, 1)

            def bank_free(n, k):
                if k >= BANKS:
                    pe.wait_ge(qk_lo_ready, QK_TILES * n + k - BANKS + 1)
                elif k + BANKS < QK_TILES:
                    if positive(n):
                        pe.wait_ge(qk_lo_ready, QK_TILES * (n - 1) + k + BANKS + 1)
                elif positive(n):
                    pe.wait_ge(v_ready, V_TILES * (n - 1) + k + BANKS - QK_TILES + 1)

            def product(n, par, k):
                bank_free(n, k)
                terms = ((w_hi, xT_hi), (w_hi, xT_lo), (w_lo, xT_hi))
                for c in range(KC):
                    for t, (w, xT) in enumerate(terms):
                        if k < QK_TILES:
                            g = k % GROUPS
                            lhsT, rhs = w[:, k // GROUPS, c, g * P:(g + 1) * P], xT[:, par, c]
                        else:
                            r = k - QK_TILES
                            lhsT, rhs = xT[:, par, c, r * P:(r + 1) * P], w[:, 2, c]
                        last = nc.tensor.matmul(ps_mm[:, k % BANKS], lhsT, rhs, start=(c == 0 and t == 0),
                                                stop=(c == KC - 1 and t == 2))
                last.then_inc(product_ready, 1)

            pe.wait_ge(const_ready, 4)
            for c in range(KC):
                transposes(0, 0, c)
            pe.wait_ge(w_lo_ready, 3)

            def pair(i):
                for par in range(2):
                    n = 2 * i + par
                    more = not (is_last(i, N) and par == 1)
                    pe.wait_ge(xT_lo_ready, KC * (n + 1))
                    for k in range(QK_TILES + V_TILES):
                        product(n, par, k)
                        if more and 5 <= k < 8:
                            for c in ((0, 1), (2,), (3,))[k - 5]:
                                transposes(n + 1, 1 - par, c)

            peeled(pe, pair, N)


class Side:
    def __init__(self, kind, number, reads, step, tile=0):
        self.kind, self.number, self.reads, self.step, self.tile = kind, number, reads, step, tile
        self.bank = number % 2


def side_plan():
    slots = [(c, j) for c in range(TC) for j in range(RT * (c + 1))]
    tiles = [HG * RT * (c + 1) for c in range(TC)]
    weights = [{0: 2.0, 1: 3.0, 2: 2.5, 3: 4.0}.get(j, 4.6) for c, j in slots]
    before = lambda p: sum(weights[:p])
    third_done, last_done = sum(slots.index((c, 0)) for c in (2,)) - 3, slots.index((TC - 1, 0)) - 3
    total = sum(tiles)
    lead = total - int(total * before(last_done) / before(len(slots)))

    def pace(marks):
        out = []
        for (p0, n0), (p1, n1) in zip(marks, marks[1:]):
            out += [n0 + int((n1 - n0) * (before(p) - before(p0)) / (before(p1) - before(p0))) for p in range(p0, p1)]
        return out + [marks[-1][1]]

    first = pace([(0, sum(tiles[:1]) + 16), (2, sum(tiles[:2])), (third_done, sum(tiles[:3])), (last_done, total),
                  (len(slots), total + lead)])
    steady = pace([(0, lead), (len(slots), total + lead)])

    counts = [0, 0]

    def use(kind, step, tile=0):
        u = Side(kind, counts[0], counts[1], step, tile)
        counts[0] += 1
        counts[1] += kind != "spread"
        return u

    def tile_use(group, x):
        group, x = (group + 1, x - total) if x >= total else (group, x)
        c = 0
        while x >= tiles[c]:
            x, c = x - tiles[c], c + 1
        return use("tile", TC * group + c, x)

    start = [tile_use(0, x) for x in range(tiles[0] + 2)]
    start.append(use("turn", 0))
    start += [tile_use(0, x) for x in range(tiles[0] + 2, first[0])]

    turns, plan, edges = [], [], []
    for group in range(B * GROUPS):
        marks = first if group == 0 else steady
        for p, (c, j) in enumerate(slots):
            edges.append(tuple(counts))
            quarters = [[], [], [], []]
            if j == 0:
                quarters[0].append(use("spread", TC * group + c))
                quarters[1].append(use("behind", TC * group + c))
                free = [2, 3]
            elif turns:
                quarters[0].append(use("turn", turns.pop(0)))
                free = [1, 2, 3]
            else:
                free = [0, 1, 2, 3]
            last_tile = total if group == B * GROUPS - 1 else total + lead
            xs = list(range(min(marks[p], last_tile), min(marks[p + 1], last_tile)))
            for n, q in enumerate(free):
                for x in xs[len(xs) * n // len(free):len(xs) * (n + 1) // len(free)]:
                    u = tile_use(group, x)
                    quarters[q].append(u)
                    if u.tile == tiles[u.step % TC] - 1:
                        turns.append(u.step)
            plan.append(quarters)
    edges.append(tuple(counts))
    return start, plan, edges


def attend(nc, qk_scr, v_scr, att_scr):
    ctx = ExitStack()
    sb = lambda name, shape, dt=F32: ctx.enter_context(nc.sbuf_tensor(name, shape, dt))
    pb = lambda name, shape: ctx.enter_context(nc.psum_tensor(name, shape, F32))
    sem = lambda name: ctx.enter_context(nc.semaphore(name))

    QK_ROWS, STACK = 3 * DH, 3 * DH + 2
    FAR = -float(2 ** 100)
    STEPS_ = 2 * TC
    N = B * GROUPS // 2
    STEP_SLOTS = [RT * (ls % TC + 1) for ls in range(STEPS_)]
    SLOTS_BEFORE = [sum(STEP_SLOTS[:ls]) for ls in range(STEPS_ + 1)]
    BODY_SLOTS = SLOTS_BEFORE[STEPS_]
    GROUP_SLOTS = BODY_SLOTS // 2
    PROBS = 5
    PIECES = {(1, 3): 0, (2, 1): 1, (2, 3): 2, (3, 1): 3}

    start_uses, plan, edges = side_plan()
    BODY_USES, BODY_READS = [edges[2 * BODY_SLOTS][x] - edges[BODY_SLOTS][x] for x in range(2)]
    assert BODY_USES % 2 == 0 and BODY_SLOTS % PROBS == 0

    def step_no(i, ls):
        return STEPS_ * i + ls

    def slot_no(i, ls, j=0):
        return BODY_SLOTS * i + SLOTS_BEFORE[ls] + j

    def pair_no(i, ls, k=0):
        return BODY_SLOTS // 2 * i + SLOTS_BEFORE[ls] // 2 + k

    def kind(i):
        return i if isinstance(i, int) else 1

    def uses(i, ls, j, quarter):
        return plan[slot_no(kind(i), ls, j)][quarter]

    def at(i, value, per_body):
        return value if isinstance(i, int) else value - per_body + per_body * i

    def use_no(i, u):
        return at(i, u.number, BODY_USES)

    def read_no(i, u):
        return at(i, u.reads, BODY_READS)

    def step_of(i, u):
        return at(i, u.step, STEPS_)

    ALL_USES = {u.number: u for quarters in plan for quarter in quarters for u in quarter}
    ALL_USES.update({u.number: u for u in start_uses})

    def find(i, ls, what, steps=0):
        n = step_no(kind(i), ls) + steps
        return plan[slot_no(n // STEPS_, n % STEPS_)][{"spread": 0, "behind": 1}[what]][0]

    def next_slot(i, ls, j):
        if j + 1 < STEP_SLOTS[ls]:
            return i, ls, j + 1
        return (i, ls + 1, 0) if ls + 1 < STEPS_ else (i + 1, 0, 0)

    def ends(i, ls, j):
        return is_last(i, N) and ls == STEPS_ - 1 and j == STEP_SLOTS[ls] - 1

    def probs_buffer(ls, j):
        return (SLOTS_BEFORE[ls] + j) % PROBS

    def tile(u):
        c = u.step % TC
        h, rest = divmod(u.tile, RT * (c + 1))
        tb, sc = divmod(rest, c + 1)
        return h, tb, sc, P * (tb + 1) if sc == c else CH, sc == c

    with ctx:
        k_stack = sb("k_stack", [P, 2, HG, T], F32R)
        q_stack = sb("q_stack", [P, TC, HG, CH], F32R)
        v_in = sb("v_in", [P, 2, SB, P])
        v_later = sb("v_later", [P, 2, SB - 2, P])
        probs = sb("probs", [P, PROBS, HG, CH])
        weight0 = sb("weight0", [P, CH])
        later_v = sb("later_v", [P, CH])
        later_n = sb("later_n", [P, CH])
        count = sb("count", [P, T])
        top = sb("top", [P, 2, CH])
        bottom = sb("bottom", [P, CH])
        inverse = sb("inverse", [P, CH])
        att = sb("att", [P, CH])
        att_out = sb("att_out", [P, 2, 2, CH], F32R)
        maxima = sb("maxima", [P, TC, HG, RT, TC + 1])
        neg_max = sb("neg_max", [P, HG, RT])
        nm_hi = sb("nm_hi", [HG * RT, P], F32R)
        nm_lo = sb("nm_lo", [HG * RT, P], F32R)
        pick = sb("pick", [P, HG, P], F32R)
        ones = sb("ones", [P, P])
        ident = sb("ident2", [P, P])
        later = sb("later", [P, P])
        ident_b = sb("ident_b", [P, P], BF16)
        mask_qk = sb("mask_qk", [P, P], BF16)
        mask_kq = sb("mask_kq", [P, P], BF16)

        ps_scores = pb("ps_scores", [P, 2, 2, CH])
        ps_top = pb("ps_top", [P, CH])
        ps_bottom = pb("ps_bottom", [P, CH])
        ps_side = pb("ps_side", [P, 2, CH])

        const_ready, const_step = sem("const_ready"), sem("const_step")
        step_loaded = [sem(f"step_loaded{c}") for c in range(TC)]
        v_loaded = [sem(f"v_loaded{p}") for p in range(2)]
        scores_ready, probs_ready = sem("scores_ready"), sem("probs_ready")
        tops_done, pair_summed, bottoms_done = sem("tops_done"), sem("pair_summed"), sem("bottoms_done")
        side_ready, side_read, weight0_ready = sem("side_ready"), sem("side_read"), sem("weight0_ready")
        neg_max_ready, nm_hi_ready, nm_stored = sem("neg_max_ready"), sem("nm_hi_ready"), sem("nm_stored")
        v_later_ready = sem("v_later_ready")
        later_n_ready = sem("later_n_ready")
        top_read, bottom_read, inverse_ready = sem("top_read"), sem("bottom_read"), sem("inverse_ready")
        att_ready, att_hi_ready, att_lo_ready = sem("att_ready"), sem("att_hi_ready"), sem("att_lo_ready")
        att_stored = [sem(f"att_stored{p}") for p in range(2)]

        block = ctx.enter_context(nc.Block())

        @block.sync
        def _(sp):
            def load(i, ls):
                s, c, par = step_no(i, ls), ls % TC, ls // TC % 2
                b, g = i // 2, (i % 2) * 2 + par
                slots = slot_no(i + (ls - TC + 1) // STEPS_, (ls - TC + 1) % STEPS_)
                if positive(slots):
                    sp.wait_ge(scores_ready, 2 * slots)
                for w, stack, parts in ((0, q_stack[:, c], (0, 0, 1)),
                                        (1, k_stack[:, par, :, c * CH:(c + 1) * CH], (0, 1, 0))):
                    for r, part in enumerate(parts):
                        src = qk_scr[w, part, bass.ds(g * P, P), bass.ds(b * T + c * CH, CH)]
                        sp.dma_start(stack[r * DH:(r + 1) * DH].bitcast(F32),
                                     src.rearrange("(h d) t -> d h t", d=DH)).then_inc(step_loaded[c], 16)
                if c == 0:
                    if positive(slot_no(i, ls) - GROUP_SLOTS):
                        sp.wait_ge(tops_done, slot_no(i, ls) - GROUP_SLOTS)
                    src = v_scr[bass.ds(b * T, T), bass.ds(g * P, P)]
                    sp.dma_start(v_in[:, par], src.rearrange("(k p) n -> p k n", p=P)).then_inc(v_loaded[par], 16)

            def store(i, ls):
                s, c, par = step_no(i, ls), ls % TC, ls // TC % 2
                b, g = i // 2, (i % 2) * 2 + par
                sp.wait_ge(att_lo_ready, s + 1)
                dst = att_scr[:, bass.ds(g * P, P), bass.ds(b * T + c * CH, CH)]
                sp.dma_start(dst.rearrange("w p t -> p w t"), att_out[:, ls % 2].bitcast(F32)).then_inc(att_stored[ls % 2], 16)

            def max_rows(i, u):
                sp.wait_ge(side_read, read_no(i, u) + 1)
                for r, nm in enumerate((nm_hi, nm_lo)):
                    row = q_stack[QK_ROWS + r:QK_ROWS + r + 1, u.step % TC].rearrange("o h (b t) -> o (h b) t", t=P)
                    sp.dma_start(row.bitcast(F32), nm[:, :].bitcast(F32)).then_inc(nm_stored, 16)

            def after(i, ls, n):
                return i + (ls + n) // STEPS_, (ls + n) % STEPS_

            def turned(i, ls, slots):
                for j in slots:
                    for u in uses(i, ls, j, 0):
                        if u.kind == "turn":
                            max_rows(i, u)

            def body(i):
                for ls in range(STEPS_):
                    if not (is_last(i, N) and ls + 3 >= STEPS_):
                        load(*after(i, ls, 3))
                    turned(i, ls, range(RT))
                    if not (isinstance(i, int) and i == 0 and ls == 0):
                        store(*after(i, ls, -1))
                    turned(i, ls, range(RT, STEP_SLOTS[ls]))

            for ls in range(3):
                load(0, ls)
            for u in start_uses:
                if u.kind == "turn":
                    max_rows(0, u)
            peeled(sp, body, N)
            store(N - 1, STEPS_ - 1)
            for s in att_stored:
                sp.wait_ge(s, 16 * STEPS_ * N // 2)

        @block.gpsimd
        def _(pool):
            steps = [0]

            def step(instruction):
                instruction.then_inc(const_step, 1)
                steps[0] += 1
                pool.wait_ge(const_step, steps[0])

            step(pool.memset(ones[:, :], 1.0))
            step(pool.memset(ident[:, :], 0.0))
            step(pool.affine_select(out=ident[:, :], in_=ident[:, :], compare_op=ALU.not_equal, fill=1.0,
                                    base=0, pattern=[[-1, P]], channel_multiplier=1))
            step(pool.tensor_copy(ident_b[:, :], ident[:, :]))
            step(pool.affine_select(out=later[:, :], in_=ones[:, :], compare_op=ALU.is_gt, fill=0.0,
                                    base=0, pattern=[[-1, P]], channel_multiplier=1))
            step(pool.memset(mask_qk[:, :], 0.0))
            step(pool.memset(mask_kq[:, :], 0.0))
            step(pool.affine_select(out=mask_qk[:, :], in_=mask_qk[:, :], compare_op=ALU.is_ge, fill=FAR,
                                    base=0, pattern=[[-1, P]], channel_multiplier=1))
            step(pool.affine_select(out=mask_kq[:, :], in_=mask_kq[:, :], compare_op=ALU.is_ge, fill=FAR,
                                    base=0, pattern=[[1, P]], channel_multiplier=-1))
            count_i = probs[:, 0].bitcast(mybir.dt.int32).rearrange("p h t -> p (h t)")
            step(pool.iota(count_i, pattern=[[-1, T]], base=T - 1, channel_multiplier=0))
            step(pool.tensor_copy(count[:, :], count_i))
            step(pool.memset(maxima[:, :, :, :, :], 0.0))
            last_query = maxima[:, TC - 1, :, RT - 1, 0]
            step(pool.affine_select(out=last_query, in_=last_query, compare_op=ALU.is_gt, fill=FAR,
                                    base=P - 1, pattern=[[0, HG]], channel_multiplier=-1))
            step(pool.memset(k_stack[QK_ROWS:STACK, :, :, :].bitcast(F32), 1.0))
            step(pool.memset(pick[:, :, :].bitcast(F32), 0.0))
            for h in range(HG - 1):
                step(pool.memset(pick[QK_ROWS:STACK, h, h * DH:(h + 1) * DH].bitcast(F32), 1.0))
            pool.memset(pick[QK_ROWS:STACK, HG - 1, (HG - 1) * DH:P].bitcast(F32), 1.0).then_inc(const_ready, 1)
            pool.wait_ge(const_ready, 1)

            def sum_later(i, par, ks):
                n = SB - 2
                g = 2 * i + par
                for k in ks:
                    if k == n - 1:
                        pool.wait_ge(v_loaded[par], 16 * (i + 1))
                        if positive(slot_no(i, TC * par) - GROUP_SLOTS):
                            pool.wait_ge(tops_done, slot_no(i, TC * par) - GROUP_SLOTS)
                    else:
                        pool.wait_ge(v_later_ready, n * g + n - 1 - k)
                    behind = v_in[:, par, SB - 1] if k == n - 1 else v_later[:, par, k + 1]
                    pool.tensor_tensor(v_later[:, par, k], v_in[:, par, k + 1], behind, ALU.add)\
                        .then_inc(v_later_ready, 1)

            def add_pair(i, ls, k):
                c, j = ls % TC, 2 * k + 1
                w0 = max(0, P * (j - RT * c))
                one, other = probs_buffer(ls, j - 1), probs_buffer(ls, j)
                pool.wait_ge(tops_done, slot_no(i, ls, j) + 1)
                pool.tensor_tensor(probs[:, one, :, w0:CH], probs[:, one, :, w0:CH], probs[:, other, :, w0:CH],
                                   ALU.add).then_inc(pair_summed, 1)

            def finish(i, ls):
                s, w = step_no(i, ls), ls % 2
                pool.wait_ge(inverse_ready, len(PIECES) * (s + 1))
                if positive(s):
                    pool.wait_ge(att_lo_ready, s)
                pool.tensor_tensor(att[:, :], top[:, w], inverse[:, :], ALU.mult).then_inc(att_ready, 1)
                pool.wait_ge(att_ready, s + 1)
                if positive(4 * i + ls // 2):
                    pool.wait_ge(att_stored[w], 16 * (4 * i + ls // 2))
                pool.tensor_tensor(att_out[:, w, 0], top[:, w], inverse[:, :], ALU.mult).then_inc(att_hi_ready, 1)
                pool.wait_ge(att_hi_ready, s + 1)
                pool.tensor_tensor(att_out[:, w, 1], att[:, :], att_out[:, w, 0].bitcast(F32), ALU.subtract)\
                    .then_inc(att_lo_ready, 1)

            def body(i):
                for ls in range(STEPS_):
                    s, c = step_no(i, ls), ls % TC
                    for k in range(STEP_SLOTS[ls] // 2):
                        add_pair(i, ls, k)
                        if k == 0:
                            pool.wait_ge(weight0_ready, s + 1)
                            if positive(s):
                                pool.wait_ge(bottom_read, s)
                            pool.tensor_tensor(later_n[:, :], weight0[:, :], count[:, c * CH:(c + 1) * CH], ALU.mult)\
                                .then_inc(later_n_ready, 1)
                            if not (isinstance(i, int) and i == 0 and ls == 0):
                                finish(i + (ls - 1) // STEPS_, (ls - 1) % STEPS_)
                        elif c == TC - 1 and not (is_last(i, N) and ls >= TC):
                            sum_later(i + (ls + TC) // STEPS_, (ls // TC + 1) % 2,
                                      range(SB - 1 - 2 * k, SB - 3 - 2 * k, -1))

            sum_later(0, 0, range(SB - 3, -1, -1))
            peeled(pool, body, N)
            finish(N - 1, STEPS_ - 1)

        @block.vector
        def _(dve):
            def take_max(i, u):
                h, tb, sc, width, _ = tile(u)
                dve.wait_ge(side_ready, use_no(i, u) + 1)
                nc.vector.tensor_reduce(maxima[:, u.step % TC, h, tb, sc + 1:sc + 2], ps_side[:, u.bank, 0:width],
                                        AX.X, ALU.max).then_inc(side_read, 1)

            def negate(i, u):
                s, c = step_of(i, u), u.step % TC
                dve.wait_ge(side_read, read_no(i, u) + 1)
                if positive(s):
                    dve.wait_ge(nm_hi_ready, s)
                nc.vector.tensor_reduce(neg_max[:, :, :], maxima[:, c, :, :, 0:c + 2], AX.X, ALU.max,
                                        negate=True).then_inc(neg_max_ready, 1)

            def max_low(i, u):
                dve.wait_ge(nm_hi_ready, step_of(i, u) + 1)
                nc.vector.tensor_tensor(nm_lo[:, :], ps_side[0:HG * RT, u.bank, 0:P], nm_hi[:, :].bitcast(F32),
                                        ALU.subtract).then_inc(side_read, 1)

            def weigh_later(i, u):
                s = step_of(i, u)
                dve.wait_ge(side_ready, use_no(i, u) + 1)
                dve.wait_ge(weight0_ready, s + 1)
                if positive(s):
                    dve.wait_ge(top_read, s)
                nc.vector.tensor_tensor(later_v[:, :], ps_side[:, u.bank], weight0[:, :], ALU.mult)\
                    .then_inc(side_read, 1)

            def read_side(i, u):
                if u.kind == "tile":
                    take_max(i, u)
                    if u.tile == HG * RT * (u.step % TC + 1) - 1:
                        negate(i, u)
                elif u.kind == "turn":
                    max_low(i, u)
                elif u.kind == "behind":
                    weigh_later(i, u)

            def read_top(i, ls):
                s = step_no(i, ls)
                dve.wait_ge(tops_done, slot_no(i, ls + 1))
                dve.wait_ge(side_read, read_no(i, find(i, ls, "behind")) + 1)
                if positive(s - 1):
                    dve.wait_ge(att_hi_ready, s - 1)
                nc.vector.tensor_tensor(top[:, ls % 2], ps_top[:, :], later_v[:, :], ALU.add).then_inc(top_read, 1)

            def read_bottom(i, ls):
                s = step_no(i, ls)
                dve.wait_ge(bottoms_done, pair_no(i, ls + 1))
                dve.wait_ge(later_n_ready, s + 1)
                if positive(s):
                    dve.wait_ge(inverse_ready, len(PIECES) * s)
                nc.vector.tensor_tensor(bottom[:, :], ps_bottom[:, :], later_n[:, :], ALU.add).then_inc(bottom_read, 1)

            def invert(i, ls, piece):
                s = step_no(i, ls)
                cols = slice(P * piece, P * (piece + 1))
                if piece == 0:
                    dve.wait_ge(bottom_read, s + 1)
                    if positive(s):
                        dve.wait_ge(att_hi_ready, s)
                nc.vector.reciprocal(inverse[:, cols], bottom[:, cols]).then_inc(inverse_ready, 1)

            dve.wait_ge(const_ready, 1)
            for u in start_uses:
                read_side(0, u)

            def body(i):
                for ls in range(STEPS_):
                    before = (i + (ls - 1) // STEPS_, (ls - 1) % STEPS_)
                    has_before = not (isinstance(i, int) and i == 0 and ls == 0)
                    for j in range(STEP_SLOTS[ls]):
                        for quarter in range(4):
                            if has_before and (j, quarter) == (0, 0):
                                read_top(*before)
                            if has_before and (j, quarter) == (1, 3):
                                read_bottom(*before)
                            for u in uses(i, ls, j, quarter):
                                read_side(i, u)
                            if has_before and (j, quarter) in PIECES:
                                invert(*before, PIECES[j, quarter])

            peeled(dve, body, N)
            read_top(N - 1, STEPS_ - 1)
            read_bottom(N - 1, STEPS_ - 1)
            for piece in range(len(PIECES)):
                invert(N - 1, STEPS_ - 1, piece)

        @block.scalar
        def _(act):
            def exps(i, ls, j, pair):
                c, J = ls % TC, slot_no(i, ls, j)
                w0 = max(0, P * (j - RT * c))
                if j % 2 == 1 and pair == 0 and positive(pair_no(i, ls, j // 2) - 1):
                    act.wait_ge(bottoms_done, pair_no(i, ls, j // 2) - 1)
                act.wait_ge(scores_ready, 2 * J + pair + 1)
                nc.scalar.activation(probs[:, probs_buffer(ls, j), 2 * pair:2 * pair + 2, w0:CH],
                                     ps_scores[:, pair, :, w0:CH], ACT.Exp, scale=SCALE).then_inc(probs_ready, 1)

            def max_high(i, u):
                s = step_of(i, u)
                act.wait_ge(side_ready, use_no(i, u) + 1)
                if positive(s):
                    act.wait_ge(nm_stored, 32 * s)
                nc.scalar.activation(nm_hi[:, :], ps_side[0:HG * RT, u.bank, 0:P], ACT.Copy).then_inc(nm_hi_ready, 1)

            def weight(i, ls):
                s, u = step_no(i, ls), find(i, ls, "spread")
                act.wait_ge(side_ready, use_no(i, u) + 1)
                if positive(s):
                    act.wait_ge(later_n_ready, s)
                    act.wait_ge(side_read, at(i, find(kind(i), ls, "behind", -1).reads, BODY_READS) + 1)
                nc.scalar.activation(weight0[:, :], ps_side[:, u.bank], ACT.Exp, scale=SCALE)\
                    .then_inc(weight0_ready, 1)

            for u in start_uses:
                if u.kind == "turn":
                    max_high(0, u)
            for pair in range(2):
                exps(0, 0, 0, pair)

            def body(i):
                for ls in range(STEPS_):
                    for j in range(STEP_SLOTS[ls]):
                        if not ends(i, ls, j):
                            exps(*next_slot(i, ls, j), 0)
                        if j == 0:
                            weight(i, ls)
                        for u in uses(i, ls, j, 0):
                            if u.kind == "turn":
                                max_high(i, u)
                        if not ends(i, ls, j):
                            exps(*next_slot(i, ls, j), 1)

            peeled(act, body, N)

        @block.tensor
        def _(pe):
            def take_scores(i, ls, j, pair):
                c, par, J = ls % TC, ls // TC % 2, slot_no(i, ls, j)
                w0 = max(0, P * (j - RT * c))
                masked = j >= RT * c
                if j == 0 and pair == 0:
                    pe.wait_ge(nm_stored, 32 * (step_no(i, ls) + 1))
                if positive(J):
                    pe.wait_ge(probs_ready, 2 * J + pair - 1)
                for k in range(2):
                    h = 2 * pair + k
                    last = nc.tensor.matmul(ps_scores[:, pair, k, w0:CH], k_stack[0:STACK, par, h, j * P:(j + 1) * P],
                                            q_stack[0:STACK, c, h, w0:CH], start=True, stop=not masked)
                    if masked:
                        last = nc.tensor.matmul(ps_scores[:, pair, k, w0:w0 + P], ident_b[:, :], mask_kq[:, :],
                                                start=False, stop=True)
                last.then_inc(scores_ready, 1)

            def wait_bank(i, u):
                before = ALL_USES[u.number - 2]
                if before.kind == "spread":
                    pe.wait_ge(weight0_ready, step_of(i, before) + 1)
                else:
                    pe.wait_ge(side_read, at(i, before.reads, BODY_READS) + 1)

            def max_tile(i, u):
                c, par = u.step % TC, u.step // TC % 2
                h, tb, sc, width, masked = tile(u)
                if u.tile == 0:
                    pe.wait_ge(step_loaded[c], 96 * (at(i, u.step // TC, 2) + 1))
                last = nc.tensor.matmul(ps_side[:, u.bank, 0:width], q_stack[0:QK_ROWS, c, h, tb * P:(tb + 1) * P],
                                        k_stack[0:QK_ROWS, par, h, sc * CH:sc * CH + width], start=True, stop=not masked)
                if masked:
                    last = nc.tensor.matmul(ps_side[:, u.bank, width - P:width], ident_b[:, :], mask_qk[:, :],
                                            start=False, stop=True)
                last.then_inc(side_ready, 1)

            def turn_max(i, u):
                pe.wait_ge(neg_max_ready, step_of(i, u) + 1)
                nc.tensor.transpose(ps_side[0:HG * RT, u.bank, 0:P], neg_max[:, :, :].rearrange("p h b -> p (h b)"),
                                    ident[:, :]).then_inc(side_ready, 1)

            def spread(i, u):
                for h in range(HG):
                    last = nc.tensor.matmul(ps_side[:, u.bank], pick[0:STACK, h, :],
                                            q_stack[0:STACK, u.step % TC, h, :], start=(h == 0), stop=(h == HG - 1))
                last.then_inc(side_ready, 1)

            def behind(i, u):
                c, par = u.step % TC, u.step // TC % 2
                pe.wait_ge(v_loaded[par], 16 * (i + 1))
                pe.wait_ge(v_later_ready, (SB - 2) * (2 * i + par + 1))
                for tb in range(RT):
                    k = RT * c + tb
                    out = ps_side[:, u.bank, tb * P:(tb + 1) * P]
                    last = nc.tensor.matmul(out, v_in[:, par, k], later[:, :], start=True, stop=(k == SB - 1))
                    if k < SB - 1:
                        rest = v_in[:, par, SB - 1] if k == SB - 2 else v_later[:, par, k]
                        last = nc.tensor.matmul(out, rest, ones[:, :], start=False, stop=True)
                last.then_inc(side_ready, 1)

            def use_side(i, u):
                if u.number >= 2:
                    wait_bank(i, u)
                {"tile": max_tile, "turn": turn_max, "spread": spread, "behind": behind}[u.kind](i, u)

            def tops(i, ls, j):
                c, par, J = ls % TC, ls // TC % 2, slot_no(i, ls, j)
                w0 = max(0, P * (j - RT * c))
                if j == 0 and positive(step_no(i, ls)):
                    pe.wait_ge(top_read, step_no(i, ls))
                pe.wait_ge(probs_ready, 2 * J + 2)
                for h in range(HG):
                    rows = slice(h * DH, (h + 1) * DH)
                    last = nc.tensor.matmul(ps_top[rows, w0:CH], v_in[:, par, j, rows],
                                            probs[:, probs_buffer(ls, j), h, w0:CH],
                                            start=(j == 0), stop=(j == STEP_SLOTS[ls] - 1))
                last.then_inc(tops_done, 1)

            def bottoms(i, ls, k):
                c, j, n = ls % TC, 2 * k, pair_no(i, ls, k)
                w0 = max(0, P * (j - RT * c))
                if k == 0 and positive(step_no(i, ls)):
                    pe.wait_ge(bottom_read, step_no(i, ls))
                pe.wait_ge(pair_summed, n + 1)
                for h in range(HG):
                    rows = slice(h * DH, (h + 1) * DH)
                    last = nc.tensor.matmul(ps_bottom[rows, w0:CH], ones[:, 0:DH], probs[:, probs_buffer(ls, j), h, w0:CH],
                                            start=(k == 0), stop=(k == STEP_SLOTS[ls] // 2 - 1))
                last.then_inc(bottoms_done, 1)

            pe.wait_ge(const_ready, 1)
            for u in start_uses:
                use_side(0, u)
            for pair in range(2):
                take_scores(0, 0, 0, pair)

            def body(i):
                for ls in range(STEPS_):
                    for j in range(STEP_SLOTS[ls]):
                        for pair in range(2):
                            if not ends(i, ls, j):
                                take_scores(*next_slot(i, ls, j), pair)
                            for u in uses(i, ls, j, pair):
                                use_side(i, u)
                        tops(i, ls, j)
                        for u in uses(i, ls, j, 2):
                            use_side(i, u)
                        if j >= 3 and j % 2 == 1:
                            bottoms(i, ls, j // 2 - 1)
                        elif j == 1 and not (isinstance(i, int) and i == 0 and ls == 0):
                            bottoms(i + (ls - 1) // STEPS_, (ls - 1) % STEPS_, STEP_SLOTS[(ls - 1) % STEPS_] // 2 - 1)
                        for u in uses(i, ls, j, 3):
                            use_side(i, u)

            peeled(pe, body, N)
            bottoms(N - 1, STEPS_ - 1, STEP_SLOTS[-1] // 2 - 1)


def conclude(nc, x, att_scr, Wo, agg_w, agg_b, in_gamma, in_beta, pn_gamma, pn_beta, d1_w, d1_b, d2_w, d2_b,
             bc_w, bc_b, gate_w, gate_b, out_gamma, out_beta, out):
    outer = ExitStack()
    with outer:
        osb = lambda name, shape, dt=F32: outer.enter_context(nc.sbuf_tensor(name, shape, dt))
        wg_hi = osb("wg_hi", [P, 2, KC, D], F32R)
        wg_lo = osb("wg_lo", [P, 2, KC, D], F32R)
        ident = osb("ident3", [P, P])
        bc_scr = nc.dram_tensor("bc_scr", [B, D], F32, kind="Internal").ap()
        think(nc, x, att_scr, Wo, agg_w, agg_b, in_gamma, in_beta, pn_gamma, pn_beta, d1_w, d1_b, d2_w, d2_b,
              bc_w, bc_b, gate_w, wg_hi, wg_lo, ident, bc_scr)
        gate_all(nc, x, att_scr, gate_b, out_gamma, out_beta, out, wg_hi, wg_lo, ident, bc_scr)


def think(nc, x, att_scr, Wo, agg_w, agg_b, in_gamma, in_beta, pn_gamma, pn_beta, d1_w, d1_b, d2_w, d2_b,
          bc_w, bc_b, gate_w, wg_hi, wg_lo, ident, bc_scr):
    ctx = ExitStack()
    sb = lambda name, shape, dt=F32: ctx.enter_context(nc.sbuf_tensor(name, shape, dt))
    pb = lambda name, shape: ctx.enter_context(nc.psum_tensor(name, shape, F32))
    sem = lambda name: ctx.enter_context(nc.semaphore(name))
    Q = 32
    NQ = P // Q
    with ctx:
        wg_raw = sb("wg_raw", [P, 2, KC, D])
        agg_sb = sb("agg_sb", [P, KC, D])
        bc_sb = sb("bc_sb", [P, KC, D])
        d1_sb = sb("d1_sb", [P, KC, HF])
        d2_sb = sb("d2_sb", [P, HC, D])
        vectors = sb("vectors", [B, 7, D])
        d1_bias = sb("d1_bias", [P, D])
        attT = sb("attT", [P, 2, KC, B], F32R)
        x_last = sb("x_last", [B, D])
        row = sb("row", [B, D])
        normed_row = sb("normed_row", [B, D])
        thought = sb("thought", [B, D])
        partly = sb("partly", [B, D])
        mean_var = sb("mean_var", [B, 2])
        stats = sb("stats3", [B, 6])
        var_eps = sb("var_eps3", [B, 1])
        rstd = sb("rstd3", [B, 1])
        minus_half = sb("minus_half3", [B, 1])
        rowT = sb("rowT", [P, KC, Q])
        hidden = sb("hidden", [P, D])
        hiddenT = sb("hiddenT", [P, KC, P])
        parts = sb("parts", [P, D])
        fold = sb("fold", [P, B])
        bc_row = sb("bc_row", [B, D])
        ps_row = pb("ps_row", [P, D])
        ps_turn = pb("ps_turn", [P, KC, P])
        ps_hidden = pb("ps_hidden", [P, D])
        ps_parts = pb("ps_parts", [P, D])

        const_ready, const_step = sem("const_ready3"), sem("const_step3")
        w_loaded, att_loaded, rows_loaded = sem("w_loaded3"), sem("att_loaded3"), sem("rows_loaded3")
        agg_loaded, bc_loaded, d1_loaded, d2_loaded = (sem(n) for n in ("agg_ld", "bc_ld", "d1_ld", "d2_ld"))
        w_hi_ready, w_lo_ready = sem("w_hi_ready3"), sem("w_lo_ready3")
        link = sem("link3")
        product_ready = sem("product_ready3")
        moments_ready, eps_ready, rstd_ready = sem("moments_ready3"), sem("eps_ready3"), sem("rstd_ready3")
        row_ready, turned, rowT_ready = sem("row_ready3"), sem("turned3"), sem("rowT_ready3")
        hidden_summed, biased, gelu_ready = sem("hidden_summed3"), sem("biased3"), sem("gelu_ready3")
        hidden_turned, hiddenT_ready = sem("hidden_turned3"), sem("hiddenT_ready3")
        parts_summed, parts_ready = sem("parts_summed3"), sem("parts_ready3")
        bc_row_ready, bc_stored = sem("bc_row_ready3"), sem("bc_stored3")
        block = ctx.enter_context(nc.Block())

        @block.sync
        def _(sp):
            sp.dma_start(wg_raw[:, 0], Wo.rearrange("(k p) n -> p k n", p=P)).then_inc(w_loaded, 16)
            last = att_scr.rearrange("w (k p) (b t) -> w p k b t", p=P, b=B)
            for w in range(2):
                for b in range(B):
                    sp.dma_start(attT[:, w, :, b:b + 1].bitcast(F32), last[w, :, :, b, T - 1:T],
                                 allow_slow_non_contiguous=True).then_inc(att_loaded, 16)
            sp.dma_start(x_last[:, :], x[:, T - 1, :]).then_inc(rows_loaded, 16)
            for n, vec in enumerate((in_gamma, in_beta, pn_gamma, pn_beta, agg_b, d2_b, bc_b)):
                sp.dma_start(vectors[:, n], vec.partition_broadcast(B)).then_inc(rows_loaded, 16)
            sp.wait_ge(const_ready, 1)
            for q in range(NQ):
                sp.dma_start(d1_bias[q * Q:q * Q + B, :], d1_b[q * D:(q + 1) * D].partition_broadcast(B))\
                    .then_inc(rows_loaded, 16)
            sp.dma_start(agg_sb[:, :, :], agg_w.rearrange("(k p) n -> p k n", p=P)).then_inc(agg_loaded, 16)
            sp.dma_start(d1_sb[:, :, :], d1_w.rearrange("(k p) n -> p k n", p=P)).then_inc(d1_loaded, 16)
            sp.dma_start(d2_sb[:, :, :], d2_w.rearrange("(k p) n -> p k n", p=P)).then_inc(d2_loaded, 16)
            sp.dma_start(bc_sb[:, :, :], bc_w.rearrange("(k p) n -> p k n", p=P)).then_inc(bc_loaded, 16)
            sp.dma_start(wg_raw[:, 1], gate_w.rearrange("(k p) n -> p k n", p=P)).then_inc(bc_loaded, 16)
            sp.wait_ge(bc_row_ready, 1)
            sp.dma_start(bc_scr, bc_row[:, :]).then_inc(bc_stored, 16)
            sp.wait_ge(bc_stored, 16)

        @block.gpsimd
        def _(pool):
            pool.memset(d1_bias[:, :], 0.0).then_inc(const_step, 1)
            pool.wait_ge(const_step, 1)
            pool.memset(minus_half[:, :], -0.5).then_inc(const_ready, 1)
            pool.memset(ident[:, :], 0.0).then_inc(const_step, 1)
            pool.memset(rowT[:, :, :], 0.0).then_inc(const_step, 1)
            pool.wait_ge(const_step, 3)
            pool.affine_select(out=ident[:, :], in_=ident[:, :], compare_op=ALU.not_equal, fill=1.0,
                               base=0, pattern=[[-1, P]], channel_multiplier=1).then_inc(const_ready, 1)
            for n in range(2 + STEPS):
                pool.wait_ge(moments_ready, n + 1)
                pool.tensor_scalar(var_eps[:, :], mean_var[:, 1:2], LN_EPS if n == 0 else FFN_EPS, None, ALU.add)\
                    .then_inc(eps_ready, 1)
                pool.wait_ge(eps_ready, n + 1)
                pool.tensor_tensor(rstd[:, :], var_eps[:, :], minus_half[:, :], ALU.pow).then_inc(rstd_ready, 1)

        @block.vector
        def _(dve):
            links = [0]

            def linked(instruction):
                instruction.then_inc(link, 1)
                links[0] += 1
                dve.wait_ge(link, links[0])

            def norm(n, src, dst, gamma=None, beta=None):
                linked(nc.vector.bn_stats(stats[:, :], src))
                nc.vector.bn_aggr(mean_var[:, :], stats[:, :]).then_inc(moments_ready, 1)
                dve.wait_ge(moments_ready, n + 1)
                dve.wait_ge(rstd_ready, n + 1)
                linked(nc.vector.tensor_scalar(dst, src, mean_var[:, 0:1], rstd[:, 0:1], ALU.subtract, ALU.mult))
                if gamma is not None:
                    linked(nc.vector.tensor_tensor(dst, dst, vectors[:, gamma], ALU.mult))
                    nc.vector.tensor_tensor(dst, dst, vectors[:, beta], ALU.add).then_inc(row_ready, 1)
                    dve.wait_ge(row_ready, n)

            def copy_rowT(n):
                dve.wait_ge(turned, n)
                nc.vector.tensor_copy(rowT[:, :, 0:B], ps_turn[:, :, 0:B]).then_inc(rowT_ready, 1)

            dve.wait_ge(const_ready, 2)
            linked(nc.vector.tensor_reduce(fold[:, :], ident[:, :].rearrange("p (q b) -> p b q", q=NQ)[:, 0:B],
                                           AX.X, ALU.add))
            dve.wait_ge(w_hi_ready, 1)
            nc.vector.tensor_tensor(wg_lo[:, 0], wg_raw[:, 0], wg_hi[:, 0].bitcast(F32), ALU.subtract)\
                .then_inc(w_lo_ready, 1)
            dve.wait_ge(rows_loaded, 16 * (8 + NQ))
            dve.wait_ge(product_ready, 1)
            linked(nc.vector.tensor_tensor(row[:, :], ps_row[0:B, :], x_last[:, :], ALU.add))
            norm(0, row[:, :], row[:, :])
            norm(1, row[:, :], normed_row[:, :], 0, 1)
            copy_rowT(1)
            dve.wait_ge(product_ready, 2)
            linked(nc.vector.tensor_tensor(thought[:, :], ps_row[0:B, :], vectors[:, 4], ALU.add))
            for k in range(STEPS):
                norm(2 + k, thought[:, :], normed_row[:, :], 2, 3)
                copy_rowT(2 + k)
                linked(nc.vector.tensor_tensor(partly[:, :], thought[:, :], vectors[:, 5], ALU.add))
                dve.wait_ge(hidden_summed, k + 1)
                nc.vector.tensor_tensor(hidden[:, :], ps_hidden[:, :], d1_bias[:, :], ALU.add).then_inc(biased, 1)
                dve.wait_ge(hidden_turned, k + 1)
                nc.vector.tensor_copy(hiddenT[:, :, :], ps_turn[:, :, :]).then_inc(hiddenT_ready, 1)
                dve.wait_ge(product_ready, 3 + k)
                done = nc.vector.tensor_tensor(thought[:, :], ps_row[0:B, :], partly[:, :], ALU.add)
                if k < STEPS - 1:
                    linked(done)
                else:
                    done.then_inc(row_ready, 1)
            copy_rowT(2 + STEPS)
            dve.wait_ge(product_ready, 3 + STEPS)
            nc.vector.tensor_tensor(bc_row[:, :], ps_row[0:B, :], vectors[:, 6], ALU.add).then_inc(bc_row_ready, 1)
            dve.wait_ge(w_hi_ready, 2)
            nc.vector.tensor_tensor(wg_lo[:, 1], wg_raw[:, 1], wg_hi[:, 1].bitcast(F32), ALU.subtract)\
                .then_inc(w_lo_ready, 1)

        @block.scalar
        def _(act):
            act.wait_ge(w_loaded, 16)
            nc.scalar.activation(wg_hi[:, 0], wg_raw[:, 0], ACT.Copy).then_inc(w_hi_ready, 1)
            for k in range(STEPS):
                act.wait_ge(biased, k + 1)
                nc.scalar.activation(hidden[:, :], hidden[:, :], ACT.Gelu).then_inc(gelu_ready, 1)
                act.wait_ge(parts_summed, k + 1)
                nc.scalar.activation(parts[:, :], ps_parts[:, :], ACT.Copy).then_inc(parts_ready, 1)
            act.wait_ge(bc_loaded, 32)
            nc.scalar.activation(wg_hi[:, 1], wg_raw[:, 1], ACT.Copy).then_inc(w_hi_ready, 1)

        @block.tensor
        def _(pe):
            def turn_row(n, src):
                pe.wait_ge(row_ready, n)
                if n >= 2:
                    pe.wait_ge(rowT_ready, n - 1)
                if n >= 3:
                    pe.wait_ge(hiddenT_ready, n - 2)
                for c in range(KC):
                    last = nc.tensor.transpose(ps_turn[:, c, 0:B], src[:, c * P:(c + 1) * P], ident[0:B, 0:B])
                last.then_inc(turned, 1)
                pe.wait_ge(rowT_ready, n)

            def row_product(w):
                for c in range(KC):
                    last = nc.tensor.matmul(ps_row[0:B, :], rowT[:, c, 0:B], w[:, c], start=(c == 0), stop=(c == KC - 1))
                last.then_inc(product_ready, 1)

            pe.wait_ge(att_loaded, 32 * B)
            pe.wait_ge(w_lo_ready, 1)
            for c in range(KC):
                for t, (a, w) in enumerate(((0, wg_hi), (0, wg_lo), (1, wg_hi))):
                    last = nc.tensor.matmul(ps_row[0:B, :], attT[:, a, c, :], w[:, 0, c], start=(c == 0 and t == 0),
                                            stop=(c == KC - 1 and t == 2))
            last.then_inc(product_ready, 1)
            turn_row(1, normed_row)
            pe.wait_ge(agg_loaded, 16)
            row_product(agg_sb)
            for k in range(STEPS):
                turn_row(2 + k, normed_row)
                pe.wait_ge(d1_loaded, 16)
                for c in range(KC):
                    for q in range(NQ):
                        last = nc.tensor.matmul(ps_hidden[q * Q:(q + 1) * Q, :], rowT[:, c, :],
                                                d1_sb[:, c, q * D:(q + 1) * D], start=(c == 0), stop=(c == KC - 1))
                last.then_inc(hidden_summed, 1)
                pe.wait_ge(gelu_ready, k + 1)
                for c in range(KC):
                    last = nc.tensor.transpose(ps_turn[:, c, :], hidden[:, c * P:(c + 1) * P], ident[:, :])
                last.then_inc(hidden_turned, 1)
                pe.wait_ge(hiddenT_ready, k + 1)
                pe.wait_ge(d2_loaded, 16)
                if k:
                    pe.wait_ge(parts_ready, k)
                for c in range(KC):
                    for q in range(NQ):
                        last = nc.tensor.matmul(ps_parts[q * Q:(q + 1) * Q, :], hiddenT[:, c, q * Q:(q + 1) * Q],
                                                d2_sb[:, KC * q + c], start=(c == 0), stop=(c == KC - 1))
                last.then_inc(parts_summed, 1)
                pe.wait_ge(parts_ready, k + 1)
                nc.tensor.matmul(ps_row[0:B, :], fold[:, :], parts[:, :], start=True, stop=True).then_inc(product_ready, 1)
            turn_row(2 + STEPS, thought)
            pe.wait_ge(bc_loaded, 32)
            row_product(bc_sb)


def gate_all(nc, x, att_scr, gate_b, out_gamma, out_beta, out, wg_hi, wg_lo, ident, bc_scr):
    ctx = ExitStack()
    sb = lambda name, shape, dt=F32: ctx.enter_context(nc.sbuf_tensor(name, shape, dt))
    pb = lambda name, shape: ctx.enter_context(nc.psum_tensor(name, shape, F32))
    sem = lambda name: ctx.enter_context(nc.semaphore(name))
    N = CHUNKS // 2
    R = 2 * RT
    TILES = N * R
    LAG1, LAG2, LAG3 = 1, 2, 3
    with ctx:
        attT = sb("attT4", [P, 2, 2, KC, CH], F32R)
        x_in = sb("x_in4", [P, 2, RT, D])
        gate_bias = sb("gate_bias", [P, D])
        gamma = sb("gamma4", [P, D])
        beta = sb("beta4", [P, D])
        x1 = sb("x1", [P, 4, D])
        x1_beta = sb("x1_beta", [P, 4, D])
        x2 = sb("x2", [P, 4, D])
        x2T_hi = sb("x2T_hi", [P, 2, KC, P], F32R)
        x2T_lo = sb("x2T_lo", [P, 2, KC, P], F32R)
        gate = sb("gate4", [P, 2, D])
        gated = sb("gated4", [P, 2, D])
        normed = sb("normed4", [P, 2, D])
        result = sb("result4", [P, 4, D])
        stats = sb("stats4", [P, 2, 6])
        mom = sb("mom4", [P, 4, 2, 2])
        eps_var = sb("eps_var4", [P, 4, 2])
        rstd = sb("rstd4", [P, 4, 2])
        minus_half = sb("minus_half4", [P, 1])
        eps = sb("eps4", [P, 2])
        bc_in = sb("bc_in4", [P, 2, D])
        ps_y = pb("ps_y", [P, 2, D])
        ps_t = pb("ps_t4", [P, 2, KC, P])
        ps_g = pb("ps_g", [P, 2, D])

        const_ready = sem("const_ready4")
        loaded = [sem(f"loaded4{p}") for p in range(2)]
        vec_loaded = sem("vec_loaded4")
        y_ready, x1_ready, x1_beta_ready = sem("y_ready4"), sem("x1_ready4"), sem("x1_beta_ready4")
        stats_ready = [sem(f"stats_ready4{w}") for w in range(2)]
        mom_ready = [sem(f"mom_ready4{w}") for w in range(2)]
        eps_ready = [sem(f"eps_ready4{w}") for w in range(2)]
        rstd_ready = [sem(f"rstd_ready4{w}") for w in range(2)]
        x2_ready, turned, hi_ready, lo_ready = sem("x2_ready4"), sem("turned4"), sem("hi_ready4"), sem("lo_ready4")
        g_ready, biased, gate_ready, gated_ready = (sem(n) for n in ("g_ready4", "biased4", "gate_ready4", "gated_ready4"))
        sum_ready, normed_ready = sem("sum_ready4"), sem("normed_ready4")
        scaled_ready, result_ready = sem("scaled_ready4"), sem("result_ready4")
        stored = [sem(f"stored4{p}") for p in range(4)]
        block = ctx.enter_context(nc.Block())

        x_rows = x.rearrange("b (r p) d -> p (b r) d", p=P)
        out_rows = out.rearrange("b (r p) d -> p (b r) d", p=P)

        @block.sync
        def _(sp):
            for dst, vec in ((gate_bias, gate_b), (gamma, out_gamma), (beta, out_beta)):
                sp.dma_start(dst[:, :], vec.partition_broadcast(P)).then_inc(vec_loaded, 16)

            def load(i, par):
                n = 2 * i + par
                if positive(RT * (n - 1)):
                    sp.wait_ge(x1_ready, RT * (n - 1))
                    sp.wait_ge(gated_ready, RT * (n - 1))
                src = att_scr.rearrange("w (k p) t -> w p k t", p=P)
                for w in range(2):
                    sp.dma_start(attT[:, par, w].bitcast(F32), src[w, :, :, bass.ds(n * CH, CH)]).then_inc(loaded[par], 16)
                sp.dma_start(x_in[:, par], x_rows[:, bass.ds(n * RT, RT), :]).then_inc(loaded[par], 16)
                b = i // 2
                sp.dma_start(bc_in[:, par], bc_scr[bass.ds(b, 1), :].rearrange("o d -> (o d)").partition_broadcast(P))\
                    .then_inc(loaded[par], 16)

            def body(i):
                for r in range(R):
                    m = R * i + r
                    if r % RT == 0 and not (is_last(i, N) and r == RT):
                        load(i + (r // RT + 1) // 2, (r // RT + 1) % 2)
                    sp.wait_ge(result_ready, m + 1)
                    sp.dma_start(out_rows[:, bass.ds(m, 1), :].rearrange("p o d -> p (o d)"), result[:, r % 4])\
                        .then_inc(stored[r % 4], 16)

            load(0, 0)
            peeled(sp, body, N)
            for s in stored:
                sp.wait_ge(s, 16 * TILES // 4)

        def staged(stages):
            def body(i):
                for r in range(R):
                    for lag, stage in stages:
                        if positive(R * i + r - lag + 1):
                            stage(i + (r - lag) // R, (r - lag) % R)
            return body

        def rest(stages):
            for late in range(max(lag for lag, _ in stages)):
                for lag, stage in stages:
                    if lag > late:
                        r = R + late - lag
                        stage(N - 1 + r // R, r % R)

        @block.gpsimd
        def _(pool):
            pool.memset(minus_half[:, :], -0.5).then_inc(const_ready, 1)
            for w, value in enumerate((LN_EPS, FFN_EPS)):
                pool.memset(eps[:, w:w + 1], value).then_inc(const_ready, 1)
            pool.wait_ge(const_ready, 3)
            pool.wait_ge(vec_loaded, 48)

            def invert(w):
                def stage(i, r):
                    m, v = R * i + r, r % 4
                    pool.wait_ge(mom_ready[w], m + 1)
                    if positive(m - 3):
                        pool.wait_ge((x2_ready, normed_ready)[w], m - 3)
                    pool.tensor_tensor(eps_var[:, v, w:w + 1], mom[:, v, w, 1:2], eps[:, w:w + 1], ALU.add)\
                        .then_inc(eps_ready[w], 1)
                    pool.wait_ge(eps_ready[w], m + 1)
                    pool.tensor_tensor(rstd[:, v, w:w + 1], eps_var[:, v, w:w + 1], minus_half[:, :], ALU.pow)\
                        .then_inc(rstd_ready[w], 1)
                return stage

            def add_beta(i, r):
                m, v = R * i + r, r % 4
                pool.wait_ge(x1_ready, m + 1)
                if positive(m - 3):
                    pool.wait_ge(result_ready, m - 3)
                pool.tensor_tensor(x1_beta[:, v], x1[:, v], beta[:, :], ALU.add).then_inc(x1_beta_ready, 1)

            def gate_bc(i, r):
                m, u = R * i + r, r % 2
                pool.wait_ge(gate_ready, m + 1)
                if positive(m - 1):
                    pool.wait_ge(normed_ready, m - 1)
                pool.tensor_tensor(gated[:, u], gate[:, u], bc_in[:, r // RT], ALU.mult).then_inc(gated_ready, 1)

            def scale(i, r):
                m, u = R * i + r, r % 2
                pool.wait_ge(normed_ready, m + 1)
                pool.tensor_tensor(normed[:, u], normed[:, u], gamma[:, :], ALU.mult).then_inc(scaled_ready, 1)

            stages = ((0, invert(0)), (LAG2, invert(1)), (LAG2, scale), (0, add_beta), (LAG1, gate_bc))
            peeled(pool, staged(stages), N)
            rest(stages)

        @block.vector
        def _(dve):
            dve.wait_ge(vec_loaded, 48)

            def first(i, r):
                m, v = R * i + r, r % 4
                dve.wait_ge(loaded[r // RT], 64 * (i + 1))
                dve.wait_ge(y_ready, m + 1)
                if positive(m - 3):
                    dve.wait_ge(x1_beta_ready, m - 3)
                nc.vector.tensor_tensor(x1[:, v], ps_y[:, r % 2], x_in[:, r // RT, r % RT], ALU.add).then_inc(x1_ready, 1)
                dve.wait_ge(x1_ready, m + 1)
                nc.vector.bn_stats(stats[:, 0], x1[:, v]).then_inc(stats_ready[0], 1)

            def moments(w):
                def stage(i, r):
                    m = R * i + r
                    if isinstance(m, int):
                        dve.wait_ge(stats_ready[w], m + 1)
                    nc.vector.bn_aggr(mom[:, r % 4, w], stats[:, w]).then_inc(mom_ready[w], 1)
                return stage

            def normalise(i, r):
                m, v = R * i + r, r % 4
                dve.wait_ge(mom_ready[0], m + 1)
                dve.wait_ge(rstd_ready[0], m + 1)
                nc.vector.tensor_scalar(x2[:, v], x1[:, v], mom[:, v, 0, 0:1], rstd[:, v, 0:1], ALU.subtract, ALU.mult)\
                    .then_inc(x2_ready, 1)

            def low(i, r):
                m, u = R * i + r, r % 2
                dve.wait_ge(hi_ready, m + 1)
                nc.vector.tensor_tensor(x2T_lo[:, u], ps_t[:, u], x2T_hi[:, u].bitcast(F32), ALU.subtract).then_inc(lo_ready, 1)

            def bias(i, r):
                m, u = R * i + r, r % 2
                dve.wait_ge(g_ready, m + 1)
                if positive(m - 1):
                    dve.wait_ge(gated_ready, m - 1)
                nc.vector.tensor_tensor(gate[:, u], ps_g[:, u], gate_bias[:, :], ALU.add).then_inc(biased, 1)

            def add_x2(i, r):
                m, v, u = R * i + r, r % 4, r % 2
                if not isinstance(m, int):
                    dve.wait_ge(stats_ready[0], m + LAG2 + 1)
                    dve.wait_ge(rstd_ready[0], m + LAG2 - 3)
                dve.wait_ge(gated_ready, m + 1)
                nc.vector.tensor_tensor(gated[:, u], gated[:, u], x2[:, v], ALU.add).then_inc(sum_ready, 1)
                dve.wait_ge(sum_ready, m + 1)
                nc.vector.bn_stats(stats[:, 1], gated[:, u]).then_inc(stats_ready[1], 1)

            def normalise2(i, r):
                m, v, u = R * i + r, r % 4, r % 2
                dve.wait_ge(mom_ready[1], m + 1)
                dve.wait_ge(rstd_ready[1], m + 1)
                if positive(m - 1):
                    dve.wait_ge(result_ready, m - 1)
                nc.vector.tensor_scalar(normed[:, u], gated[:, u], mom[:, v, 1, 0:1], rstd[:, v, 1:2],
                                        ALU.subtract, ALU.mult).then_inc(normed_ready, 1)

            def add_up(i, r):
                m, v, u = R * i + r, r % 4, r % 2
                if not isinstance(m, int):
                    dve.wait_ge(stats_ready[1], m + LAG3 - LAG2 + 1)
                    dve.wait_ge(rstd_ready[1], m + LAG3 - LAG2 - 3)
                dve.wait_ge(scaled_ready, m + 1)
                dve.wait_ge(x1_beta_ready, m + 1)
                if positive(m - 3):
                    dve.wait_ge(stored[v], 16 * (2 * i + r // 4))
                nc.vector.tensor_tensor(result[:, v], normed[:, u], x1_beta[:, v], ALU.add).then_inc(result_ready, 1)

            stages = ((LAG1, low), (0, first), (LAG2, add_x2), (0, moments(0)), (LAG3, add_up), (LAG2, moments(1)),
                      (0, normalise), (LAG2, normalise2), (LAG1, bias))
            peeled(dve, staged(stages), N)
            rest(stages)

        @block.scalar
        def _(act):
            def high(i, r):
                m, u = R * i + r, r % 2
                act.wait_ge(turned, m + 1)
                if positive(m - 1):
                    act.wait_ge(g_ready, m - 1)
                nc.scalar.activation(x2T_hi[:, u], ps_t[:, u], ACT.Copy).then_inc(hi_ready, 1)

            def sigmoid(i, r):
                m, u = R * i + r, r % 2
                act.wait_ge(biased, m + 1)
                nc.scalar.activation(gate[:, u], gate[:, u], ACT.Sigmoid).then_inc(gate_ready, 1)

            stages = ((LAG1, sigmoid), (0, high))
            peeled(act, staged(stages), N)
            rest(stages)

        @block.tensor
        def _(pe):
            def project(i, r):
                m, par = R * i + r, r // RT
                pe.wait_ge(loaded[par], 64 * (i + 1))
                if positive(m - 1):
                    pe.wait_ge(x1_ready, m - 1)
                for c in range(KC):
                    for t, (a, w) in enumerate(((0, wg_hi), (0, wg_lo), (1, wg_hi))):
                        last = nc.tensor.matmul(ps_y[:, r % 2], attT[:, par, a, c, (r % RT) * P:(r % RT + 1) * P], w[:, 0, c],
                                                start=(c == 0 and t == 0), stop=(c == KC - 1 and t == 2))
                last.then_inc(y_ready, 1)

            def turn(i, r):
                m, u, v = R * i + r, r % 2, r % 4
                pe.wait_ge(x2_ready, m + 1)
                if positive(m - 1):
                    pe.wait_ge(lo_ready, m - 1)
                for c in range(KC):
                    last = nc.tensor.transpose(ps_t[:, u, c], x2[:, v, c * P:(c + 1) * P], ident[:, :])
                last.then_inc(turned, 1)

            def gates(i, r):
                m, u = R * i + r, r % 2
                pe.wait_ge(lo_ready, m + 1)
                if positive(m - 1):
                    pe.wait_ge(biased, m - 1)
                for c in range(KC):
                    for t, (xT, w) in enumerate(((x2T_hi, wg_hi), (x2T_hi, wg_lo), (x2T_lo, wg_hi))):
                        last = nc.tensor.matmul(ps_g[:, u], xT[:, u, c], w[:, 1, c],
                                                start=(c == 0 and t == 0), stop=(c == KC - 1 and t == 2))
                last.then_inc(g_ready, 1)

            stages = ((0, project), (LAG1, gates), (0, turn))
            peeled(pe, staged(stages), N)
            rest(stages)


def build(nc, x, Wq, Wk, Wv, Wo, in_gamma, in_beta, agg_w, agg_b, pn_gamma, pn_beta, d1_w, d1_b, d2_w, d2_b,
          bc_w, bc_b, gate_w, gate_b, out_gamma, out_beta, out):
    qk_scr = nc.dram_tensor("qk_scr", [2, 2, D, B * T], F32, kind="Internal").ap()
    v_scr = nc.dram_tensor("v_scr", [B * T, D], F32, kind="Internal").ap()
    att_scr = nc.dram_tensor("att_scr", [2, D, B * T], F32, kind="Internal").ap()
    project(nc, x, Wq, Wk, Wv, qk_scr, v_scr)
    attend(nc, qk_scr, v_scr, att_scr)
    conclude(nc, x, att_scr, Wo, agg_w, agg_b, in_gamma, in_beta, pn_gamma, pn_beta, d1_w, d1_b, d2_w, d2_b,
             bc_w, bc_b, gate_w, gate_b, out_gamma, out_beta, out)


_INS = ["L0_attn_x", "L0_attn_Wq", "L0_attn_Wk", "L0_attn_Wv", "L0_attn_Wo", "L0_ffn_in_gamma", "L0_ffn_in_beta",
        "L0_ffn_agg_w", "L0_ffn_agg_b", "L0_ffn_pn_gamma", "L0_ffn_pn_beta", "L0_ffn_d1_w", "L0_ffn_d1_b",
        "L0_ffn_d2_w", "L0_ffn_d2_b", "L0_ffn_bc_w", "L0_ffn_bc_b", "L0_ffn_gate_w", "L0_ffn_gate_b",
        "L0_ffn_out_gamma", "L0_ffn_out_beta"]


def kernel(**inputs):
    import numpy as _np
    import concourse.bacc as _bacc
    from concourse import mybir as _mybir
    from concourse.bass_utils import run_bass_kernel_spmd as _run

    nc = _bacc.Bacc("TRN2", target_bir_lowering=False, num_devices=1)
    arrays, args = {}, []
    for name in _INS:
        a = _np.ascontiguousarray(inputs[name])
        arrays[f"in_{name}"] = a
        args.append(nc.dram_tensor(f"in_{name}", a.shape, _mybir.dt.from_np(a.dtype), kind="ExternalInput").ap())
    args.append(nc.dram_tensor("out_x", (B, T, D), _mybir.dt.float32, kind="ExternalOutput").ap())
    build(nc, *args)
    r = _run(nc, [arrays], core_ids=[0])
    return r.results[0]["out_x"]
```

```python
import concourse.bass as bass
from concourse import mybir
from concourse.alu_op_type import AluOpType as ALU
from contextlib import ExitStack

ACT = mybir.ActivationFunctionType
AX = mybir.AxisListType
F32 = mybir.dt.float32
F32R = mybir.dt.float32r
BF16 = mybir.dt.bfloat16

P = 128
B, T, D = 4, 2048, 512
HEADS = 16
DH = D // HEADS
HG = P // DH
GROUPS = HEADS // HG
KC = D // P
CH = 512
RT = CH // P
CHUNKS = B * T // CH
TC = T // CH
SB = T // P
HF = 2048
HC = HF // P
STEPS = 4
LN_EPS, FFN_EPS = 1e-5, 1e-6
SCALE = float(T) ** -0.5


def positive(value):
    return not isinstance(value, int) or value > 0


def peeled(eng, body, n):
    body(0)
    with eng.Fori(1, n - 1) as i:
        body(i)
    body(n - 1)


def is_last(i, n):
    return isinstance(i, int) and i == n - 1


def project(nc, x, Wq, Wk, Wv, qk_scr, v_scr):
    ctx = ExitStack()
    sb = lambda name, shape, dt=F32: ctx.enter_context(nc.sbuf_tensor(name, shape, dt))
    pb = lambda name, shape: ctx.enter_context(nc.psum_tensor(name, shape, F32))
    sem = lambda name: ctx.enter_context(nc.semaphore(name))
    QK_TILES, V_TILES = 2 * GROUPS, RT
    BANKS = 6
    with ctx:
        w_raw = sb("w_raw", [P, 3, KC, D])
        w_hi = sb("w_hi", [P, 3, KC, D], F32R)
        w_lo = sb("w_lo", [P, 3, KC, D], F32R)
        x_in = sb("x_in", [P, 2, RT, D])
        xT_hi = sb("xT_hi", [P, 2, KC, CH], F32R)
        xT_lo = sb("xT_lo", [P, 2, KC, CH], F32R)
        qk_out = sb("qk_out", [P, QK_TILES, 2, CH], F32R)
        v_out = sb("v_out", [P, V_TILES, D])
        stats = sb("stats", [P, 2, RT, 6])
        moments = sb("moments", [P, 2, RT, 2])
        var_eps = sb("var_eps", [P, 2, RT])
        rstd = sb("rstd", [P, 2, RT])
        minus_half = sb("minus_half", [P, RT])
        eps = sb("eps", [P, RT])
        ident = sb("ident", [P, P])
        ps_t = pb("ps_t", [P, 2, CH])
        ps_mm = pb("ps_mm", [P, BANKS, CH])

        w_loaded = [sem(f"w_loaded{w}") for w in range(3)]
        w_hi_ready, w_lo_ready = sem("w_hi_ready"), sem("w_lo_ready")
        x_loaded = [sem(f"x_loaded{p}") for p in range(2)]
        const_ready = sem("const_ready")
        stats_ready, moments_ready = sem("stats_ready"), sem("moments_ready")
        eps_ready, rstd_ready = sem("eps_ready"), sem("rstd_ready")
        norm_ready = sem("norm_ready")
        transposed = sem("transposed")
        xT_hi_ready, xT_lo_ready = sem("xT_hi_ready"), sem("xT_lo_ready")
        product_ready = sem("product_ready")
        qk_hi_ready, qk_lo_ready, v_ready = sem("qk_hi_ready"), sem("qk_lo_ready"), sem("v_ready")
        qk_stored = [sem(f"qk_stored{k}") for k in range(QK_TILES)]
        v_stored = [sem(f"v_stored{r}") for r in range(V_TILES)]

        block = ctx.enter_context(nc.Block())
        N = CHUNKS // 2

        x_rows = x.rearrange("b (r p) d -> p (b r) d", p=P)
        qk_cols = qk_scr.rearrange("w s (g p) t -> w g p s t", p=P)

        @block.sync
        def _(sp):
            def load(i, par):
                n = 2 * i + par
                if positive(KC * (n - 1)):
                    sp.wait_ge(transposed, KC * (n - 1))
                sp.dma_start(x_in[:, par], x_rows[:, bass.ds(n * RT, RT), :]).then_inc(x_loaded[par], 16)

            def store(i, par):
                n = 2 * i + par
                for k in range(QK_TILES):
                    sp.wait_ge(qk_lo_ready, QK_TILES * n + k + 1)
                    sp.dma_start(qk_cols[k // GROUPS, k % GROUPS, :, :, bass.ds(n * CH, CH)],
                                 qk_out[:, k].bitcast(F32)).then_inc(qk_stored[k], 16)
                for r in range(V_TILES):
                    sp.wait_ge(v_ready, V_TILES * n + r + 1)
                    sp.dma_start(v_scr[bass.ds(n * CH + r * P, P), :], v_out[:, r]).then_inc(v_stored[r], 16)

            def pair(i):
                for par in range(2):
                    store(i, par)
                    if not is_last(i, N):
                        load(i + 1, par)

            load(0, 0)
            for w, W in enumerate((Wq, Wk, Wv)):
                sp.dma_start(w_raw[:, w], W.rearrange("(k p) n -> p k n", p=P)).then_inc(w_loaded[w], 16)
            load(0, 1)
            peeled(sp, pair, N)
            for s in qk_stored + v_stored:
                sp.wait_ge(s, 16 * CHUNKS)

        @block.gpsimd
        def _(pool):
            pool.memset(minus_half[:, :], -0.5).then_inc(const_ready, 1)
            pool.memset(eps[:, :], LN_EPS).then_inc(const_ready, 1)
            pool.memset(ident[:, :], 0.0).then_inc(const_ready, 1)
            pool.wait_ge(const_ready, 3)
            pool.affine_select(out=ident[:, :], in_=ident[:, :], compare_op=ALU.not_equal, fill=1.0,
                               base=0, pattern=[[-1, P]], channel_multiplier=1).then_inc(const_ready, 1)

            def pair(i):
                for par in range(2):
                    n = 2 * i + par
                    pool.wait_ge(moments_ready, RT * (n + 1))
                    if positive(RT * (n - 1)):
                        pool.wait_ge(norm_ready, RT * (n - 1))
                    pool.tensor_tensor(var_eps[:, par], moments[:, par, :, 1], eps[:, :], ALU.add).then_inc(eps_ready, 1)
                    pool.wait_ge(eps_ready, n + 1)
                    pool.tensor_tensor(rstd[:, par], var_eps[:, par], minus_half[:, :],
                                       ALU.pow).then_inc(rstd_ready, 1)

            peeled(pool, pair, N)

        @block.vector
        def _(dve):
            def chunk_stats(n, par):
                dve.wait_ge(x_loaded[par], (n // 2 + 1) * 16 if isinstance(n, int) else (n - par) * 8 + 16)
                if positive(n - 1):
                    dve.wait_ge(rstd_ready, n - 1)
                for r in range(RT):
                    nc.vector.bn_stats(stats[:, par, r], x_in[:, par, r]).then_inc(stats_ready, 1)

            def chunk_moments(n, par):
                for r in range(RT):
                    nc.vector.bn_aggr(moments[:, par, r], stats[:, par, r]).then_inc(moments_ready, 1)

            def chunk_norm(n, par):
                dve.wait_ge(rstd_ready, n + 1)
                dve.wait_ge(moments_ready, RT * (n + 1))
                for r in range(RT):
                    nc.vector.tensor_scalar(x_in[:, par, r], x_in[:, par, r], moments[:, par, r, 0:1],
                                            rstd[:, par, r:r + 1], ALU.subtract, ALU.mult).then_inc(norm_ready, 1)

            def xT_low(n, par, c):
                dve.wait_ge(xT_hi_ready, KC * n + c + 1)
                nc.vector.tensor_tensor(xT_lo[:, par, c], ps_t[:, c % 2], xT_hi[:, par, c].bitcast(F32),
                                        ALU.subtract).then_inc(xT_lo_ready, 1)

            def qk_low(n, k, stats_too=False):
                if stats_too:
                    dve.wait_ge(stats_ready, RT * (n + 2))
                dve.wait_ge(qk_hi_ready, QK_TILES * n + k + 1)
                nc.vector.tensor_tensor(qk_out[:, k, 1], ps_mm[:, k % BANKS], qk_out[:, k, 0].bitcast(F32),
                                        ALU.subtract).then_inc(qk_lo_ready, 1)

            chunk_stats(0, 0)
            dve.wait_ge(stats_ready, RT)
            chunk_moments(0, 0)
            chunk_norm(0, 0)
            for c in range(KC):
                xT_low(0, 0, c)
            for w in range(3):
                dve.wait_ge(w_loaded[w], 16)
                dve.wait_ge(w_hi_ready, w + 1)
                nc.vector.tensor_tensor(w_lo[:, w], w_raw[:, w], w_hi[:, w].bitcast(F32),
                                        ALU.subtract).then_inc(w_lo_ready, 1)

            def pair(i):
                for par in range(2):
                    n = 2 * i + par
                    more = not (is_last(i, N) and par == 1)
                    if more:
                        chunk_stats(n + 1, 1 - par)
                    for k in range(4):
                        qk_low(n, k, stats_too=more and k == 0)
                        if more and k == 0:
                            chunk_moments(n + 1, 1 - par)
                    if more:
                        chunk_norm(n + 1, 1 - par)
                    for k in range(4, QK_TILES):
                        qk_low(n, k)
                        if more and k >= 5:
                            for c in ((0, 1), (2,), (3,))[k - 5]:
                                xT_low(n + 1, 1 - par, c)

            peeled(dve, pair, N)

        @block.scalar
        def _(act):
            def xT_high(n, par, c):
                act.wait_ge(transposed, KC * n + c + 1)
                if positive((QK_TILES + V_TILES) * (n - 1)):
                    act.wait_ge(product_ready, (QK_TILES + V_TILES) * (n - 1))
                nc.scalar.activation(xT_hi[:, par, c], ps_t[:, c % 2], ACT.Copy).then_inc(xT_hi_ready, 1)

            for c in range(KC):
                xT_high(0, 0, c)
            for w in range(3):
                act.wait_ge(w_loaded[w], 16)
                nc.scalar.activation(w_hi[:, w], w_raw[:, w], ACT.Copy).then_inc(w_hi_ready, 1)

            def pair(i):
                for par in range(2):
                    n = 2 * i + par
                    more = not (is_last(i, N) and par == 1)
                    for k in range(QK_TILES):
                        act.wait_ge(product_ready, (QK_TILES + V_TILES) * n + k + 1)
                        if positive(16 * n):
                            act.wait_ge(qk_stored[k], 16 * n)
                        nc.scalar.activation(qk_out[:, k, 0], ps_mm[:, k % BANKS], ACT.Copy).then_inc(qk_hi_ready, 1)
                        if more and k >= 5:
                            for c in ((0, 1), (2,), (3,))[k - 5]:
                                xT_high(n + 1, 1 - par, c)
                    for r in range(V_TILES):
                        act.wait_ge(product_ready, (QK_TILES + V_TILES) * n + QK_TILES + r + 1)
                        if positive(16 * n):
                            act.wait_ge(v_stored[r], 16 * n)
                        nc.scalar.activation(v_out[:, r], ps_mm[:, (QK_TILES + r) % BANKS], ACT.Copy).then_inc(v_ready, 1)

            peeled(act, pair, N)

        @block.tensor
        def _(pe):
            def transposes(n, par, c):
                if c == 0:
                    pe.wait_ge(norm_ready, RT * (n + 1))
                if positive(KC * n + c - 1):
                    pe.wait_ge(xT_lo_ready, KC * n + c - 1)
                for r in range(RT):
                    last = nc.tensor.transpose(ps_t[:, c % 2, r * P:(r + 1) * P], x_in[:, par, r, c * P:(c + 1) * P],
                                               ident[:, :])
                last.then_inc(transposed, 1)

            def bank_free(n, k):
                if k >= BANKS:
                    pe.wait_ge(qk_lo_ready, QK_TILES * n + k - BANKS + 1)
                elif k + BANKS < QK_TILES:
                    if positive(n):
                        pe.wait_ge(qk_lo_ready, QK_TILES * (n - 1) + k + BANKS + 1)
                elif positive(n):
                    pe.wait_ge(v_ready, V_TILES * (n - 1) + k + BANKS - QK_TILES + 1)

            def product(n, par, k):
                bank_free(n, k)
                terms = ((w_hi, xT_hi), (w_hi, xT_lo), (w_lo, xT_hi))
                for c in range(KC):
                    for t, (w, xT) in enumerate(terms):
                        if k < QK_TILES:
                            g = k % GROUPS
                            lhsT, rhs = w[:, k // GROUPS, c, g * P:(g + 1) * P], xT[:, par, c]
                        else:
                            r = k - QK_TILES
                            lhsT, rhs = xT[:, par, c, r * P:(r + 1) * P], w[:, 2, c]
                        last = nc.tensor.matmul(ps_mm[:, k % BANKS], lhsT, rhs, start=(c == 0 and t == 0),
                                                stop=(c == KC - 1 and t == 2))
                last.then_inc(product_ready, 1)

            pe.wait_ge(const_ready, 4)
            for c in range(KC):
                transposes(0, 0, c)
            def pair(i):
                for par in range(2):
                    n = 2 * i + par
                    more = not (is_last(i, N) and par == 1)
                    pe.wait_ge(xT_lo_ready, KC * (n + 1))
                    for k in range(QK_TILES + V_TILES):
                        if isinstance(n, int) and n == 0 and k % GROUPS == 0:
                            pe.wait_ge(w_lo_ready, k // GROUPS + 1)
                        product(n, par, k)
                        if more and 5 <= k < 8:
                            for c in ((0, 1), (2,), (3,))[k - 5]:
                                transposes(n + 1, 1 - par, c)

            peeled(pe, pair, N)


PIECES = {(1, 3): 0, (2, 1): 1, (2, 3): 2, (3, 1): 3}


class Side:
    def __init__(self, kind, number, reads, step, tile=0):
        self.kind, self.number, self.reads, self.step, self.tile = kind, number, reads, step, tile
        self.bank = number % 2


def side_plan():
    slots = [(c, j) for c in range(TC) for j in range(RT * (c + 1))]
    tiles = [HG * RT * (c + 1) for c in range(TC)]
    total = sum(tiles)
    arrivals = [(2, 3), (6, TC), (14, TC + 1), (26, TC + 2)]
    third_due, last_due = slots.index((2, 0)) - 3, slots.index((TC - 1, 0)) - 3
    SMALL = 0.1
    SIGNAL, BACK = 0.2, 0.25

    def step_tile(x):
        c = 0
        while x >= tiles[c % TC]:
            x, c = x - tiles[c % TC], c + 1
        return c, x

    def width(x):
        c, m = step_tile(x)
        tb, sc = divmod(m % (RT * (c % TC + 1)), c % TC + 1)
        return (tb + 1) / RT if sc == c % TC else 1

    def bank_share(c, j):
        return min(1.0, 1 - (j - RT * c) / RT)

    def place(x, end, patience, due):
        pe = dve = act = 0.0
        read = [0.0, 0.0]
        negated, out = [], []
        for p, (c, j) in enumerate(slots):
            c1, j1 = slots[(p + 1) % len(slots)]
            pair = (c, j - 3) if j >= 3 else ((c - 1) % TC, RT * ((c - 1) % TC + 1) - 2)
            known = [n for slot, n in arrivals if p >= slot]
            cap = min(end, sum(tiles[n % TC] for n in range((known[-1] if known else 2) + 1)))
            out.append([[], [], [], []])
            for quarter in range(4):
                scores = 0.43 * bank_share(c1, j1) + (0.21 if j1 >= RT * c1 else 0.0)
                top, bottom = (0.17 + 0.85 * bank_share(*block) for block in ((c, j), pair))
                pe += (scores, scores, top, bottom if j % 2 else 0.0)[quarter] + SMALL
                if quarter < 2:
                    act = max(act, pe + SIGNAL) + 0.9 * bank_share(c1, j1)
                if (j, quarter) == (0, 0):
                    dve = max(dve, pe - scores) + 0.6
                    pe = max(pe, read[-2]) + 0.22
                    act = max(act, pe + SIGNAL) + 0.48
                    read = [read[-1], act + SIGNAL]
                elif (j, quarter) == (0, 1):
                    pe = max(pe, read[-2]) + 1.5
                    dve = max(dve, pe + SIGNAL) + 0.6
                    read = [read[-1], dve + BACK]
                elif (j, quarter) == (1, 3):
                    dve = max(dve, pe + SIGNAL) + 0.6
                elif quarter >= 2 and negated and (max(negated[0], read[-2]) <= pe or p + 2 == slots.index((1, 0))):
                    negated.pop(0)
                    out[-1][quarter].append("turn")
                    pe += 0.11
                    act = max(act, pe + SIGNAL) + 0.16
                    dve = max(dve, act + SIGNAL) + 0.2
                    read = [read[-1], dve + BACK]
                while x < cap and (len(out[-1][quarter]) < 2 and read[-2] <= pe + patience or
                                   quarter == 3 and x < due[p + 1]):
                    out[-1][quarter].append(x)
                    pe = max(pe, read[-2]) + 0.216 * width(x) + (0.05 if width(x) < 1 else 0)
                    dve = max(dve, pe + SIGNAL) + 0.07 + 0.53 * width(x)
                    read = [read[-1], dve + BACK]
                    x += 1
                    if step_tile(x)[1] == 0:
                        dve += 0.2
                        negated.append(dve + SIGNAL)
                if (j, quarter) in PIECES:
                    dve += 0.85
        return x, out, len(negated)

    def taken(out, p):
        return sum(isinstance(x, int) for quarters in out[:p] for q in quarters for x in q)

    def climb(marks):
        return [n0 + (n1 - n0) * (p - p0) // (p1 - p0) for (p0, n0), (p1, n1) in zip(marks, marks[1:])
                for p in range(p0, p1)] + [marks[-1][1]]

    none_due = [0] * (len(slots) + 1)
    for patience in [0.01 * n for n in range(200)]:
        lead = (total - tiles[0]) // 2 + 4
        for _ in range(4):
            x, steady, pending = place(lead, total + lead, patience, none_due)
            lead = max(lead, total - taken(steady, last_due))
        if x == total + lead and lead + taken(steady, last_due) >= total and not pending:
            break
    else:
        raise AssertionError("no plan")
    due = climb([(0, 2 * tiles[0]), (2, sum(tiles[:2])), (third_due, sum(tiles[:3])), (last_due, total),
                 (len(slots), total + lead)])
    x, first, pending = place(2 * tiles[0], total + lead, patience, due)
    assert x == total + lead and not pending

    counts = [0, 0]

    def use(kind, step, tile=0):
        u = Side(kind, counts[0], counts[1], step, tile)
        counts[0] += 1
        counts[1] += kind != "spread"
        return u

    def tile_use(group, x):
        c, m = step_tile(x)
        return use("tile", TC * group + c, m)

    start = [tile_use(0, x) for x in range(tiles[0] + 2)]
    start.append(use("turn", 0))
    start += [tile_use(0, x) for x in range(tiles[0] + 2, 2 * tiles[0])]
    plan, edges, turned = [], [], 1
    last_step = B * GROUPS * TC - 1
    for group in range(B * GROUPS):
        for (c, j), placed in zip(slots, first if group == 0 else steady):
            edges.append(tuple(counts))
            plan.append([[], [], [], []])
            for quarter, xs in enumerate(placed):
                if j == 0 and quarter < 2:
                    plan[-1][quarter].append(use(("spread", "behind")[quarter], TC * group + c))
                for x in xs:
                    if x == "turn":
                        if turned <= last_step:
                            plan[-1][quarter].append(use("turn", turned))
                        turned += 1
                    elif TC * group + step_tile(x)[0] <= last_step:
                        plan[-1][quarter].append(tile_use(group, x))
    edges.append(tuple(counts))
    return start, plan, edges


def attend(nc, qk_scr, v_scr, att_scr):
    ctx = ExitStack()
    sb = lambda name, shape, dt=F32: ctx.enter_context(nc.sbuf_tensor(name, shape, dt))
    pb = lambda name, shape: ctx.enter_context(nc.psum_tensor(name, shape, F32))
    sem = lambda name: ctx.enter_context(nc.semaphore(name))

    QK_ROWS, STACK = 3 * DH, 3 * DH + 2
    FAR = -float(2 ** 100)
    STEPS_ = 2 * TC
    N = B * GROUPS // 2
    STEP_SLOTS = [RT * (ls % TC + 1) for ls in range(STEPS_)]
    SLOTS_BEFORE = [sum(STEP_SLOTS[:ls]) for ls in range(STEPS_ + 1)]
    BODY_SLOTS = SLOTS_BEFORE[STEPS_]
    GROUP_SLOTS = BODY_SLOTS // 2
    PROBS = 5

    start_uses, plan, edges = side_plan()
    BODY_USES, BODY_READS = [edges[2 * BODY_SLOTS][x] - edges[BODY_SLOTS][x] for x in range(2)]
    assert BODY_USES % 2 == 0 and BODY_SLOTS % PROBS == 0

    def step_no(i, ls):
        return STEPS_ * i + ls

    def slot_no(i, ls, j=0):
        return BODY_SLOTS * i + SLOTS_BEFORE[ls] + j

    def pair_no(i, ls, k=0):
        return BODY_SLOTS // 2 * i + SLOTS_BEFORE[ls] // 2 + k

    def kind(i):
        return i if isinstance(i, int) else 1

    def uses(i, ls, j, quarter):
        return plan[slot_no(kind(i), ls, j)][quarter]

    def at(i, value, per_body):
        return value if isinstance(i, int) else value - per_body + per_body * i

    def use_no(i, u):
        return at(i, u.number, BODY_USES)

    def read_no(i, u):
        return at(i, u.reads, BODY_READS)

    def step_of(i, u):
        return at(i, u.step, STEPS_)

    USES = start_uses + [u for quarters in plan for quarter in quarters for u in quarter]

    def find(i, ls, what, steps=0):
        n = step_no(kind(i), ls) + steps
        return plan[slot_no(n // STEPS_, n % STEPS_)][{"spread": 0, "behind": 1}[what]][0]

    def next_slot(i, ls, j):
        if j + 1 < STEP_SLOTS[ls]:
            return i, ls, j + 1
        return (i, ls + 1, 0) if ls + 1 < STEPS_ else (i + 1, 0, 0)

    def ends(i, ls, j):
        return is_last(i, N) and ls == STEPS_ - 1 and j == STEP_SLOTS[ls] - 1

    def probs_buffer(ls, j):
        return (SLOTS_BEFORE[ls] + j) % PROBS

    def tile(u):
        c = u.step % TC
        h, rest = divmod(u.tile, RT * (c + 1))
        tb, sc = divmod(rest, c + 1)
        return h, tb, sc, P * (tb + 1) if sc == c else CH, sc == c

    with ctx:
        k_stack = sb("k_stack", [P, 2, HG, T], F32R)
        q_stack = sb("q_stack", [P, TC, HG, CH], F32R)
        v_in = sb("v_in", [P, 2, SB, P])
        v_later = sb("v_later", [P, 2, SB - 2, P])
        probs = sb("probs", [P, PROBS, HG, CH])
        weight0 = sb("weight0", [P, CH])
        later_v = sb("later_v", [P, CH])
        later_n = sb("later_n", [P, CH])
        count = sb("count", [P, T])
        top = sb("top", [P, 2, CH])
        bottom = sb("bottom", [P, CH])
        inverse = sb("inverse", [P, CH])
        att = sb("att", [P, CH])
        att_out = sb("att_out", [P, 2, 2, CH], F32R)
        maxima = sb("maxima", [P, TC, HG, RT, TC + 1])
        neg_max = sb("neg_max", [P, HG, RT])
        nm_hi = sb("nm_hi", [HG * RT, P], F32R)
        nm_lo = sb("nm_lo", [HG * RT, P], F32R)
        nm_rows = sb("nm_rows", [P, 2, CH], F32R)
        pick = sb("pick", [P, P], F32R)
        ones = sb("ones", [P, P])
        ident = sb("ident2", [P, P])
        later = sb("later", [P, P])
        ident_b = sb("ident_b", [P, P], BF16)
        mask_qk = sb("mask_qk", [P, P], BF16)
        mask_kq = sb("mask_kq", [P, P], BF16)

        ps_scores = pb("ps_scores", [P, 2, 2, CH])
        ps_top = pb("ps_top", [P, CH])
        ps_bottom = pb("ps_bottom", [P, CH])
        ps_side = pb("ps_side", [P, 2, CH])

        const_ready, const_step = sem("const_ready"), sem("const_step")
        step_loaded = [sem(f"step_loaded{c}") for c in range(TC)]
        v_loaded = [sem(f"v_loaded{p}") for p in range(2)]
        scores_ready, probs_ready = sem("scores_ready"), sem("probs_ready")
        tops_done, pair_summed, bottoms_done = sem("tops_done"), sem("pair_summed"), sem("bottoms_done")
        side_ready, side_read, weight0_ready = sem("side_ready"), sem("side_read"), sem("weight0_ready")
        neg_max_ready, nm_hi_ready, nm_stored = sem("neg_max_ready"), sem("nm_hi_ready"), sem("nm_stored")
        v_later_ready = sem("v_later_ready")
        later_n_ready = sem("later_n_ready")
        top_read, bottom_read, inverse_ready = sem("top_read"), sem("bottom_read"), sem("inverse_ready")
        att_ready, att_hi_ready, att_lo_ready = sem("att_ready"), sem("att_hi_ready"), sem("att_lo_ready")
        att_stored = [sem(f"att_stored{p}") for p in range(2)]

        block = ctx.enter_context(nc.Block())

        @block.sync
        def _(sp):
            def load(i, ls):
                s, c, par = step_no(i, ls), ls % TC, ls // TC % 2
                b, g = i // 2, (i % 2) * 2 + par
                slots = slot_no(i + (ls - TC + 1) // STEPS_, (ls - TC + 1) % STEPS_)
                if positive(slots):
                    sp.wait_ge(scores_ready, 2 * slots)
                for w, stack, parts in ((0, q_stack[:, c], (0, 0, 1)),
                                        (1, k_stack[:, par, :, c * CH:(c + 1) * CH], (0, 1, 0))):
                    for r, part in enumerate(parts):
                        src = qk_scr[w, part, bass.ds(g * P, P), bass.ds(b * T + c * CH, CH)]
                        sp.dma_start(stack[r * DH:(r + 1) * DH].bitcast(F32),
                                     src.rearrange("(h d) t -> d h t", d=DH)).then_inc(step_loaded[c], 16)
                if c == 0:
                    if positive(slot_no(i, ls) - GROUP_SLOTS):
                        sp.wait_ge(tops_done, slot_no(i, ls) - GROUP_SLOTS)
                    src = v_scr[bass.ds(b * T, T), bass.ds(g * P, P)]
                    sp.dma_start(v_in[:, par], src.rearrange("(k p) n -> p k n", p=P)).then_inc(v_loaded[par], 16)

            def store(i, ls):
                s, c, par = step_no(i, ls), ls % TC, ls // TC % 2
                b, g = i // 2, (i % 2) * 2 + par
                sp.wait_ge(att_lo_ready, s + 1)
                dst = att_scr[:, bass.ds(g * P, P), bass.ds(b * T + c * CH, CH)]
                sp.dma_start(dst.rearrange("w p t -> p w t"), att_out[:, ls % 2].bitcast(F32)).then_inc(att_stored[ls % 2], 16)

            def max_rows(i, u):
                sp.wait_ge(side_read, read_no(i, u) + 1)
                for r, nm in enumerate((nm_hi, nm_lo)):
                    row = q_stack[QK_ROWS + r:QK_ROWS + r + 1, u.step % TC].rearrange("o h (b t) -> o (h b) t", t=P)
                    sp.dma_start(row.bitcast(F32), nm[:, :].bitcast(F32)).then_inc(nm_stored, 16)
                    sp.dma_start(nm_rows[DH * r:DH * r + HG, u.step % 2].rearrange("h (b t) -> h b t", t=P).bitcast(F32),
                                 nm[:, :].bitcast(F32)).then_inc(nm_stored, 16)

            def after(i, ls, n):
                return i + (ls + n) // STEPS_, (ls + n) % STEPS_

            def turned(i, ls, slots):
                for j in slots:
                    for quarter in range(4):
                        for u in uses(i, ls, j, quarter):
                            if u.kind == "turn":
                                max_rows(i, u)

            def body(i):
                for ls in range(STEPS_):
                    if not (is_last(i, N) and ls + 3 >= STEPS_):
                        load(*after(i, ls, 3))
                    turned(i, ls, range(RT))
                    if not (isinstance(i, int) and i == 0 and ls == 0):
                        store(*after(i, ls, -1))
                    turned(i, ls, range(RT, STEP_SLOTS[ls]))

            for ls in range(3):
                load(0, ls)
            for u in start_uses:
                if u.kind == "turn":
                    max_rows(0, u)
            peeled(sp, body, N)
            store(N - 1, STEPS_ - 1)
            for s in att_stored:
                sp.wait_ge(s, 16 * STEPS_ * N // 2)

        @block.gpsimd
        def _(pool):
            steps = [0]

            def step(instruction):
                instruction.then_inc(const_step, 1)
                steps[0] += 1
                pool.wait_ge(const_step, steps[0])

            step(pool.memset(nm_rows[:, :, :].bitcast(F32), 0.0))
            step(pool.memset(mask_qk[:, :], 0.0))
            step(pool.affine_select(out=mask_qk[:, :], in_=mask_qk[:, :], compare_op=ALU.is_ge, fill=FAR,
                                    base=0, pattern=[[-1, P]], channel_multiplier=1))
            step(pool.memset(ident[:, :], 0.0))
            step(pool.affine_select(out=ident[:, :], in_=ident[:, :], compare_op=ALU.not_equal, fill=1.0,
                                    base=0, pattern=[[-1, P]], channel_multiplier=1))
            step(pool.tensor_copy(ident_b[:, :], ident[:, :]))
            step(pool.memset(maxima[:, :, :, :, :], 0.0))
            last_query = maxima[:, TC - 1, :, RT - 1, 0]
            pool.affine_select(out=last_query, in_=last_query, compare_op=ALU.is_gt, fill=FAR,
                               base=P - 1, pattern=[[0, HG]], channel_multiplier=-1).then_inc(const_ready, 1)
            pool.wait_ge(const_ready, 1)
            step(pool.memset(k_stack[QK_ROWS:STACK, 0, :, :].bitcast(F32), 1.0))
            step(pool.memset(mask_kq[:, :], 0.0))
            step(pool.affine_select(out=mask_kq[:, :], in_=mask_kq[:, :], compare_op=ALU.is_ge, fill=FAR,
                                    base=0, pattern=[[1, P]], channel_multiplier=-1))
            picked = later
            step(pool.memset(picked[:, :], 0.0))
            step(pool.memset(picked[0:2 * DH, :], 1.0))
            for r in range(2):
                part = picked[DH * r:DH * (r + 1), :]
                step(pool.affine_select(out=part, in_=part, compare_op=ALU.is_ge, fill=0.0,
                                        base=0, pattern=[[1, P]], channel_multiplier=-DH))
                step(pool.affine_select(out=part, in_=part, compare_op=ALU.is_ge, fill=0.0,
                                        base=DH - 1, pattern=[[-1, P]], channel_multiplier=DH))
            step(pool.tensor_copy(pick[:, :], picked[:, :]))
            step(pool.memset(ones[:, :], 1.0))
            pool.affine_select(out=later[:, :], in_=ones[:, :], compare_op=ALU.is_gt, fill=0.0,
                               base=0, pattern=[[-1, P]], channel_multiplier=1).then_inc(const_ready, 1)
            pool.wait_ge(const_ready, 2)
            step(pool.memset(k_stack[QK_ROWS:STACK, 1, :, :].bitcast(F32), 1.0))
            count_i = bottom[:, :].bitcast(mybir.dt.int32)
            for c in range(TC):
                step(pool.iota(count_i, pattern=[[-1, CH]], base=T - 1 - CH * c, channel_multiplier=0))
                step(pool.tensor_copy(count[:, c * CH:(c + 1) * CH], count_i))

            def sum_later(i, par, ks):
                n = SB - 2
                g = 2 * i + par
                for k in ks:
                    if k == n - 1:
                        pool.wait_ge(v_loaded[par], 16 * (i + 1))
                        if positive(slot_no(i, TC * par) - GROUP_SLOTS):
                            pool.wait_ge(tops_done, slot_no(i, TC * par) - GROUP_SLOTS)
                    else:
                        pool.wait_ge(v_later_ready, n * g + n - 1 - k)
                    behind = v_in[:, par, SB - 1] if k == n - 1 else v_later[:, par, k + 1]
                    pool.tensor_tensor(v_later[:, par, k], v_in[:, par, k + 1], behind, ALU.add)\
                        .then_inc(v_later_ready, 1)

            def add_pair(i, ls, k):
                c, j = ls % TC, 2 * k + 1
                w0 = max(0, P * (j - RT * c))
                one, other = probs_buffer(ls, j - 1), probs_buffer(ls, j)
                pool.wait_ge(tops_done, slot_no(i, ls, j) + 1)
                pool.tensor_tensor(probs[:, one, :, w0:CH], probs[:, one, :, w0:CH], probs[:, other, :, w0:CH],
                                   ALU.add).then_inc(pair_summed, 1)

            def divide(i, ls):
                s, w = step_no(i, ls), ls % 2
                pool.wait_ge(inverse_ready, len(PIECES) * (s + 1))
                if positive(s):
                    pool.wait_ge(att_lo_ready, s)
                pool.tensor_tensor(att[:, :], top[:, w], inverse[:, :], ALU.mult).then_inc(att_ready, 1)

            def att_low(i, ls):
                s, w = step_no(i, ls), ls % 2
                pool.wait_ge(att_hi_ready, s + 1)
                pool.tensor_tensor(att_out[:, w, 1], att[:, :], att_out[:, w, 0].bitcast(F32), ALU.subtract)\
                    .then_inc(att_lo_ready, 1)

            def body(i):
                for ls in range(STEPS_):
                    s, c = step_no(i, ls), ls % TC
                    before = (i + (ls - 1) // STEPS_, (ls - 1) % STEPS_)
                    has_before = not (isinstance(i, int) and i == 0 and ls == 0)
                    for k in range(STEP_SLOTS[ls] // 2):
                        add_pair(i, ls, k)
                        if k == 0:
                            pool.wait_ge(weight0_ready, s + 1)
                            if positive(s):
                                pool.wait_ge(bottom_read, s)
                            pool.tensor_tensor(later_n[:, :], weight0[:, :], count[:, c * CH:(c + 1) * CH], ALU.mult)\
                                .then_inc(later_n_ready, 1)
                            if has_before:
                                divide(*before)
                        if k == 1 and has_before:
                            att_low(*before)
                        if k > 0 and c == TC - 1 and not (is_last(i, N) and ls >= TC):
                            sum_later(i + (ls + TC) // STEPS_, (ls // TC + 1) % 2,
                                      range(SB - 1 - 2 * k, SB - 3 - 2 * k, -1))

            sum_later(0, 0, range(SB - 3, -1, -1))
            peeled(pool, body, N)
            divide(N - 1, STEPS_ - 1)
            att_low(N - 1, STEPS_ - 1)

        @block.vector
        def _(dve):
            def take_max(i, u):
                h, tb, sc, width, _ = tile(u)
                dve.wait_ge(side_ready, use_no(i, u) + 1)
                nc.vector.tensor_reduce(maxima[:, u.step % TC, h, tb, sc + 1:sc + 2], ps_side[:, u.bank, 0:width],
                                        AX.X, ALU.max).then_inc(side_read, 1)

            def negate(i, u):
                s, c = step_of(i, u), u.step % TC
                dve.wait_ge(side_read, read_no(i, u) + 1)
                if positive(s):
                    dve.wait_ge(nm_hi_ready, s)
                nc.vector.tensor_reduce(neg_max[:, :, :], maxima[:, c, :, :, 0:c + 2], AX.X, ALU.max,
                                        negate=True).then_inc(neg_max_ready, 1)

            def max_low(i, u):
                dve.wait_ge(nm_hi_ready, step_of(i, u) + 1)
                nc.vector.tensor_tensor(nm_lo[:, :], ps_side[0:HG * RT, u.bank, 0:P], nm_hi[:, :].bitcast(F32),
                                        ALU.subtract).then_inc(side_read, 1)

            def weigh_later(i, u):
                s = step_of(i, u)
                dve.wait_ge(side_ready, use_no(i, u) + 1)
                dve.wait_ge(weight0_ready, s + 1)
                if positive(s):
                    dve.wait_ge(top_read, s)
                nc.vector.tensor_tensor(later_v[:, :], ps_side[:, u.bank], weight0[:, :], ALU.mult)\
                    .then_inc(side_read, 1)

            def read_side(i, u):
                if u.kind == "tile":
                    take_max(i, u)
                    if u.tile == HG * RT * (u.step % TC + 1) - 1:
                        negate(i, u)
                elif u.kind == "turn":
                    max_low(i, u)
                elif u.kind == "behind":
                    weigh_later(i, u)

            def read_top(i, ls):
                s = step_no(i, ls)
                dve.wait_ge(tops_done, slot_no(i, ls + 1))
                dve.wait_ge(side_read, read_no(i, find(i, ls, "behind")) + 1)
                if positive(s - 1):
                    dve.wait_ge(att_ready, s - 1)
                nc.vector.tensor_tensor(top[:, ls % 2], ps_top[:, :], later_v[:, :], ALU.add).then_inc(top_read, 1)

            def read_bottom(i, ls):
                s = step_no(i, ls)
                dve.wait_ge(bottoms_done, pair_no(i, ls + 1))
                dve.wait_ge(later_n_ready, s + 1)
                if positive(s):
                    dve.wait_ge(inverse_ready, len(PIECES) * s)
                nc.vector.tensor_tensor(bottom[:, :], ps_bottom[:, :], later_n[:, :], ALU.add).then_inc(bottom_read, 1)

            def invert(i, ls, piece):
                s = step_no(i, ls)
                cols = slice(P * piece, P * (piece + 1))
                if piece == 0:
                    dve.wait_ge(bottom_read, s + 1)
                    if positive(s):
                        dve.wait_ge(att_ready, s)
                nc.vector.reciprocal(inverse[:, cols], bottom[:, cols]).then_inc(inverse_ready, 1)

            dve.wait_ge(const_ready, 1)
            for u in start_uses:
                read_side(0, u)

            def body(i):
                for ls in range(STEPS_):
                    before = (i + (ls - 1) // STEPS_, (ls - 1) % STEPS_)
                    has_before = not (isinstance(i, int) and i == 0 and ls == 0)
                    for j in range(STEP_SLOTS[ls]):
                        for quarter in range(4):
                            if has_before and (j, quarter) == (0, 0):
                                read_top(*before)
                            if has_before and (j, quarter) == (1, 3):
                                read_bottom(*before)
                            for u in uses(i, ls, j, quarter):
                                read_side(i, u)
                            if has_before and (j, quarter) in PIECES:
                                invert(*before, PIECES[j, quarter])

            peeled(dve, body, N)
            read_top(N - 1, STEPS_ - 1)
            read_bottom(N - 1, STEPS_ - 1)
            for piece in range(len(PIECES)):
                invert(N - 1, STEPS_ - 1, piece)

        @block.scalar
        def _(act):
            def exps(i, ls, j, pair):
                c, J = ls % TC, slot_no(i, ls, j)
                w0 = max(0, P * (j - RT * c))
                if j % 2 == 1 and pair == 0 and positive(pair_no(i, ls, j // 2) - 1):
                    act.wait_ge(bottoms_done, pair_no(i, ls, j // 2) - 1)
                act.wait_ge(scores_ready, 2 * J + pair + 1)
                nc.scalar.activation(probs[:, probs_buffer(ls, j), 2 * pair:2 * pair + 2, w0:CH],
                                     ps_scores[:, pair, :, w0:CH], ACT.Exp, scale=SCALE).then_inc(probs_ready, 1)

            def max_high(i, u):
                s = step_of(i, u)
                act.wait_ge(side_ready, use_no(i, u) + 1)
                if positive(s):
                    act.wait_ge(nm_stored, 64 * s)
                nc.scalar.activation(nm_hi[:, :], ps_side[0:HG * RT, u.bank, 0:P], ACT.Copy).then_inc(nm_hi_ready, 1)

            def weight(i, ls):
                s, u = step_no(i, ls), find(i, ls, "spread")
                act.wait_ge(side_ready, use_no(i, u) + 1)
                if positive(s):
                    act.wait_ge(later_n_ready, s)
                    act.wait_ge(side_read, at(i, find(kind(i), ls, "behind", -1).reads, BODY_READS) + 1)
                nc.scalar.activation(weight0[:, :], ps_side[:, u.bank], ACT.Exp, scale=SCALE)\
                    .then_inc(weight0_ready, 1)

            def att_high(i, ls):
                s, w = step_no(i, ls), ls % 2
                act.wait_ge(att_ready, s + 1)
                if positive(4 * i + ls // 2):
                    act.wait_ge(att_stored[w], 16 * (4 * i + ls // 2))
                nc.scalar.activation(att_out[:, w, 0], att[:, :], ACT.Copy).then_inc(att_hi_ready, 1)

            for u in start_uses:
                if u.kind == "turn":
                    max_high(0, u)
            for pair in range(2):
                exps(0, 0, 0, pair)

            def body(i):
                for ls in range(STEPS_):
                    for j in range(STEP_SLOTS[ls]):
                        if not ends(i, ls, j):
                            exps(*next_slot(i, ls, j), 0)
                        if j == 0:
                            weight(i, ls)
                        for quarter in range(4):
                            if quarter == 1 and not ends(i, ls, j):
                                exps(*next_slot(i, ls, j), 1)
                            for u in uses(i, ls, j, quarter):
                                if u.kind == "turn":
                                    max_high(i, u)
                        if j == 3 and ls % TC > 0:
                            att_high(i, ls - 1)
                        elif j == 0 and ls % TC == 1 and not (isinstance(i, int) and i == 0 and ls == 1):
                            att_high(i + (ls - 2) // STEPS_, (ls - 2) % STEPS_)

            peeled(act, body, N)
            att_high(N - 1, STEPS_ - 1)

        @block.tensor
        def _(pe):
            def take_scores(i, ls, j, pair):
                c, par, J = ls % TC, ls // TC % 2, slot_no(i, ls, j)
                w0 = max(0, P * (j - RT * c))
                masked = j >= RT * c
                if j == 0 and pair == 0:
                    pe.wait_ge(nm_stored, 64 * (step_no(i, ls) + 1))
                if positive(J):
                    pe.wait_ge(probs_ready, 2 * J + pair - 1)
                for k in range(2):
                    h = 2 * pair + k
                    last = nc.tensor.matmul(ps_scores[:, pair, k, w0:CH], k_stack[0:STACK, par, h, j * P:(j + 1) * P],
                                            q_stack[0:STACK, c, h, w0:CH], start=True, stop=not masked)
                    if masked:
                        last = nc.tensor.matmul(ps_scores[:, pair, k, w0:w0 + P], ident_b[:, :], mask_kq[:, :],
                                                start=False, stop=True)
                last.then_inc(scores_ready, 1)

            def wait_bank(i, u):
                before = USES[u.number - 2]
                if before.kind == "spread":
                    pe.wait_ge(weight0_ready, step_of(i, before) + 1)
                else:
                    pe.wait_ge(side_read, at(i, before.reads, BODY_READS) + 1)

            def max_tile(i, u):
                c, par = u.step % TC, u.step // TC % 2
                h, tb, sc, width, masked = tile(u)
                if u.tile == 0:
                    pe.wait_ge(step_loaded[c], 96 * (at(i, u.step // TC, 2) + 1))
                last = nc.tensor.matmul(ps_side[:, u.bank, 0:width], q_stack[0:QK_ROWS, c, h, tb * P:(tb + 1) * P],
                                        k_stack[0:QK_ROWS, par, h, sc * CH:sc * CH + width], start=True, stop=not masked)
                if masked:
                    last = nc.tensor.matmul(ps_side[:, u.bank, width - P:width], ident_b[:, :], mask_qk[:, :],
                                            start=False, stop=True)
                last.then_inc(side_ready, 1)

            def turn_max(i, u):
                pe.wait_ge(neg_max_ready, step_of(i, u) + 1)
                nc.tensor.transpose(ps_side[0:HG * RT, u.bank, 0:P], neg_max[:, :, :].rearrange("p h b -> p (h b)"),
                                    ident[:, :]).then_inc(side_ready, 1)

            def spread(i, u):
                pe.wait_ge(nm_stored, 64 * (step_of(i, u) + 1))
                nc.tensor.matmul(ps_side[:, u.bank], pick[:, :], nm_rows[:, u.step % 2], start=True, stop=True)\
                    .then_inc(side_ready, 1)

            def behind(i, u):
                c, par = u.step % TC, u.step // TC % 2
                pe.wait_ge(v_loaded[par], 16 * (i + 1))
                pe.wait_ge(v_later_ready, (SB - 2) * (2 * i + par + 1))
                for tb in range(RT):
                    k = RT * c + tb
                    out = ps_side[:, u.bank, tb * P:(tb + 1) * P]
                    last = nc.tensor.matmul(out, v_in[:, par, k], later[:, :], start=True, stop=(k == SB - 1))
                    if k < SB - 1:
                        rest = v_in[:, par, SB - 1] if k == SB - 2 else v_later[:, par, k]
                        last = nc.tensor.matmul(out, rest, ones[:, :], start=False, stop=True)
                last.then_inc(side_ready, 1)

            def use_side(i, u):
                if u.number >= 2:
                    wait_bank(i, u)
                {"tile": max_tile, "turn": turn_max, "spread": spread, "behind": behind}[u.kind](i, u)

            def tops(i, ls, j):
                c, par, J = ls % TC, ls // TC % 2, slot_no(i, ls, j)
                w0 = max(0, P * (j - RT * c))
                if j == 0 and positive(step_no(i, ls)):
                    pe.wait_ge(top_read, step_no(i, ls))
                pe.wait_ge(probs_ready, 2 * J + 2)
                for h in range(HG):
                    rows = slice(h * DH, (h + 1) * DH)
                    last = nc.tensor.matmul(ps_top[rows, w0:CH], v_in[:, par, j, rows],
                                            probs[:, probs_buffer(ls, j), h, w0:CH],
                                            start=(j == 0), stop=(j == STEP_SLOTS[ls] - 1))
                last.then_inc(tops_done, 1)

            def bottoms(i, ls, k):
                c, j, n = ls % TC, 2 * k, pair_no(i, ls, k)
                w0 = max(0, P * (j - RT * c))
                if k == 0 and positive(step_no(i, ls)):
                    pe.wait_ge(bottom_read, step_no(i, ls))
                pe.wait_ge(pair_summed, n + 1)
                for h in range(HG):
                    rows = slice(h * DH, (h + 1) * DH)
                    last = nc.tensor.matmul(ps_bottom[rows, w0:CH], ones[:, 0:DH], probs[:, probs_buffer(ls, j), h, w0:CH],
                                            start=(k == 0), stop=(k == STEP_SLOTS[ls] // 2 - 1))
                last.then_inc(bottoms_done, 1)

            pe.wait_ge(const_ready, 1)
            for u in start_uses:
                use_side(0, u)
            pe.wait_ge(const_ready, 2)
            for pair in range(2):
                take_scores(0, 0, 0, pair)

            def body(i):
                for ls in range(STEPS_):
                    for j in range(STEP_SLOTS[ls]):
                        for pair in range(2):
                            if not ends(i, ls, j):
                                take_scores(*next_slot(i, ls, j), pair)
                            for u in uses(i, ls, j, pair):
                                use_side(i, u)
                        tops(i, ls, j)
                        for u in uses(i, ls, j, 2):
                            use_side(i, u)
                        if j >= 3 and j % 2 == 1:
                            bottoms(i, ls, j // 2 - 1)
                        elif j == 1 and not (isinstance(i, int) and i == 0 and ls == 0):
                            bottoms(i + (ls - 1) // STEPS_, (ls - 1) % STEPS_, STEP_SLOTS[(ls - 1) % STEPS_] // 2 - 1)
                        for u in uses(i, ls, j, 3):
                            use_side(i, u)

            peeled(pe, body, N)
            bottoms(N - 1, STEPS_ - 1, STEP_SLOTS[-1] // 2 - 1)


def conclude(nc, x, att_scr, Wo, agg_w, agg_b, in_gamma, in_beta, pn_gamma, pn_beta, d1_w, d1_b, d2_w, d2_b,
             bc_w, bc_b, gate_w, gate_b, out_gamma, out_beta, out):
    outer = ExitStack()
    with outer:
        osb = lambda name, shape, dt=F32: outer.enter_context(nc.sbuf_tensor(name, shape, dt))
        wg_hi = osb("wg_hi", [P, 2, KC, D], F32R)
        wg_lo = osb("wg_lo", [P, 2, KC, D], F32R)
        ident = osb("ident3", [P, P])
        bc_scr = nc.dram_tensor("bc_scr", [B, D], F32, kind="Internal").ap()
        attT = osb("attT4", [P, 2, 2, KC, CH], F32R)
        x_in = osb("x_in4", [P, 2, RT, D])
        loaded = [outer.enter_context(nc.semaphore(f"loaded4{p}")) for p in range(2)]
        think(nc, x, att_scr, Wo, agg_w, agg_b, in_gamma, in_beta, pn_gamma, pn_beta, d1_w, d1_b, d2_w, d2_b,
              bc_w, bc_b, gate_w, wg_hi, wg_lo, ident, bc_scr, attT, x_in, loaded)
        gate_all(nc, x, att_scr, gate_b, out_gamma, out_beta, out, wg_hi, wg_lo, ident, bc_scr, attT, x_in, loaded)


def load_chunk(sp, n, par, x, att_scr, attT, x_in, loaded):
    src = att_scr.rearrange("w (k p) t -> w p k t", p=P)
    for w in range(2):
        sp.dma_start(attT[:, par, w].bitcast(F32), src[w, :, :, bass.ds(n * CH, CH)]).then_inc(loaded[par], 16)
    x_rows = x.rearrange("b (r p) d -> p (b r) d", p=P)
    sp.dma_start(x_in[:, par], x_rows[:, bass.ds(n * RT, RT), :]).then_inc(loaded[par], 16)


def think(nc, x, att_scr, Wo, agg_w, agg_b, in_gamma, in_beta, pn_gamma, pn_beta, d1_w, d1_b, d2_w, d2_b,
          bc_w, bc_b, gate_w, wg_hi, wg_lo, ident, bc_scr, attT4, x_in4, loaded):
    ctx = ExitStack()
    sb = lambda name, shape, dt=F32: ctx.enter_context(nc.sbuf_tensor(name, shape, dt))
    pb = lambda name, shape: ctx.enter_context(nc.psum_tensor(name, shape, F32))
    sem = lambda name: ctx.enter_context(nc.semaphore(name))
    Q = 32
    NQ = P // Q
    with ctx:
        wg_raw = sb("wg_raw", [P, KC, D])
        agg_sb = sb("agg_sb", [P, KC, D])
        bc_sb = sb("bc_sb", [P, KC, D])
        d1_sb = sb("d1_sb", [P, KC, HF])
        d2_sb = sb("d2_sb", [P, HC, D])
        vectors = sb("vectors", [B, 7, D])
        d1_bias = sb("d1_bias", [P, D])
        attT = sb("attT", [P, 2, KC, B], F32R)
        x_last = sb("x_last", [B, D])
        row = sb("row", [B, D])
        normed_row = sb("normed_row", [B, D])
        thought = sb("thought", [B, D])
        partly = sb("partly", [B, D])
        mean_var = sb("mean_var", [B, 2])
        stats = sb("stats3", [B, 6])
        var_eps = sb("var_eps3", [B, 1])
        rstd = sb("rstd3", [B, 1])
        minus_half = sb("minus_half3", [B, 1])
        rowT = sb("rowT", [P, KC, Q])
        hidden = sb("hidden", [P, D])
        hiddenT = sb("hiddenT", [P, KC, P])
        parts = sb("parts", [P, D])
        fold = sb("fold", [P, B])
        bc_row = sb("bc_row", [B, D])
        ps_row = pb("ps_row", [P, D])
        ps_turn = pb("ps_turn", [P, KC, P])
        ps_hidden = pb("ps_hidden", [P, D])
        ps_parts = pb("ps_parts", [P, D])

        const_ready, const_step = sem("const_ready3"), sem("const_step3")
        w_loaded, att_loaded, rows_loaded = sem("w_loaded3"), sem("att_loaded3"), sem("rows_loaded3")
        agg_loaded, bc_loaded, d1_loaded, d2_loaded = (sem(n) for n in ("agg_ld", "bc_ld", "d1_ld", "d2_ld"))
        w_hi_ready, w_lo_ready = sem("w_hi_ready3"), sem("w_lo_ready3")
        link = sem("link3")
        product_ready = sem("product_ready3")
        moments_ready, eps_ready, rstd_ready = sem("moments_ready3"), sem("eps_ready3"), sem("rstd_ready3")
        row_ready, turned, rowT_ready = sem("row_ready3"), sem("turned3"), sem("rowT_ready3")
        hidden_summed, biased, gelu_ready = sem("hidden_summed3"), sem("biased3"), sem("gelu_ready3")
        hidden_turned, hiddenT_ready = sem("hidden_turned3"), sem("hiddenT_ready3")
        parts_summed, parts_ready = sem("parts_summed3"), sem("parts_ready3")
        bc_row_ready, bc_stored = sem("bc_row_ready3"), sem("bc_stored3")
        block = ctx.enter_context(nc.Block())

        @block.sync
        def _(sp):
            sp.dma_start(wg_raw[:, :, :], Wo.rearrange("(k p) n -> p k n", p=P)).then_inc(w_loaded, 16)
            last = att_scr.rearrange("w (k p) (b t) -> w p k b t", p=P, b=B)
            for w in range(2):
                for b in range(B):
                    sp.dma_start(attT[:, w, :, b:b + 1].bitcast(F32), last[w, :, :, b, T - 1:T],
                                 allow_slow_non_contiguous=True).then_inc(att_loaded, 16)
            sp.dma_start(x_last[:, :], x[:, T - 1, :]).then_inc(rows_loaded, 16)
            for n, vec in enumerate((in_gamma, in_beta, pn_gamma, pn_beta, agg_b, d2_b, bc_b)):
                sp.dma_start(vectors[:, n], vec.partition_broadcast(B)).then_inc(rows_loaded, 16)
            sp.wait_ge(const_ready, 1)
            for q in range(NQ):
                sp.dma_start(d1_bias[q * Q:q * Q + B, :], d1_b[q * D:(q + 1) * D].partition_broadcast(B))\
                    .then_inc(rows_loaded, 16)
            sp.dma_start(agg_sb[:, :, :], agg_w.rearrange("(k p) n -> p k n", p=P)).then_inc(agg_loaded, 16)
            sp.dma_start(d1_sb[:, :, :], d1_w.rearrange("(k p) n -> p k n", p=P)).then_inc(d1_loaded, 16)
            sp.dma_start(d2_sb[:, :, :], d2_w.rearrange("(k p) n -> p k n", p=P)).then_inc(d2_loaded, 16)
            sp.dma_start(bc_sb[:, :, :], bc_w.rearrange("(k p) n -> p k n", p=P)).then_inc(bc_loaded, 16)
            sp.wait_ge(w_lo_ready, 1)
            sp.dma_start(wg_raw[:, :, :], gate_w.rearrange("(k p) n -> p k n", p=P)).then_inc(bc_loaded, 16)
            load_chunk(sp, 0, 0, x, att_scr, attT4, x_in4, loaded)
            sp.wait_ge(bc_row_ready, 1)
            sp.dma_start(bc_scr, bc_row[:, :]).then_inc(bc_stored, 16)
            sp.wait_ge(bc_stored, 16)

        @block.gpsimd
        def _(pool):
            pool.memset(d1_bias[:, :], 0.0).then_inc(const_step, 1)
            pool.wait_ge(const_step, 1)
            pool.memset(minus_half[:, :], -0.5).then_inc(const_ready, 1)
            pool.memset(ident[:, :], 0.0).then_inc(const_step, 1)
            pool.memset(rowT[:, :, :], 0.0).then_inc(const_step, 1)
            pool.wait_ge(const_step, 3)
            pool.affine_select(out=ident[:, :], in_=ident[:, :], compare_op=ALU.not_equal, fill=1.0,
                               base=0, pattern=[[-1, P]], channel_multiplier=1).then_inc(const_ready, 1)
            for n in range(2 + STEPS):
                pool.wait_ge(moments_ready, n + 1)
                pool.tensor_scalar(var_eps[:, :], mean_var[:, 1:2], LN_EPS if n == 0 else FFN_EPS, None, ALU.add)\
                    .then_inc(eps_ready, 1)
                pool.wait_ge(eps_ready, n + 1)
                pool.tensor_tensor(rstd[:, :], var_eps[:, :], minus_half[:, :], ALU.pow).then_inc(rstd_ready, 1)

        @block.vector
        def _(dve):
            links = [0]

            def linked(instruction):
                instruction.then_inc(link, 1)
                links[0] += 1
                dve.wait_ge(link, links[0])

            def norm(n, src, dst, gamma=None, beta=None):
                linked(nc.vector.bn_stats(stats[:, :], src))
                nc.vector.bn_aggr(mean_var[:, :], stats[:, :]).then_inc(moments_ready, 1)
                dve.wait_ge(moments_ready, n + 1)
                dve.wait_ge(rstd_ready, n + 1)
                linked(nc.vector.tensor_scalar(dst, src, mean_var[:, 0:1], rstd[:, 0:1], ALU.subtract, ALU.mult))
                if gamma is not None:
                    linked(nc.vector.tensor_tensor(dst, dst, vectors[:, gamma], ALU.mult))
                    nc.vector.tensor_tensor(dst, dst, vectors[:, beta], ALU.add).then_inc(row_ready, 1)
                    dve.wait_ge(row_ready, n)

            def copy_rowT(n):
                dve.wait_ge(turned, n)
                nc.vector.tensor_copy(rowT[:, :, 0:B], ps_turn[:, :, 0:B]).then_inc(rowT_ready, 1)

            dve.wait_ge(const_ready, 2)
            linked(nc.vector.tensor_reduce(fold[:, :], ident[:, :].rearrange("p (q b) -> p b q", q=NQ)[:, 0:B],
                                           AX.X, ALU.add))
            dve.wait_ge(w_hi_ready, 1)
            nc.vector.tensor_tensor(wg_lo[:, 0], wg_raw[:, :, :], wg_hi[:, 0].bitcast(F32), ALU.subtract)\
                .then_inc(w_lo_ready, 1)
            dve.wait_ge(rows_loaded, 16 * (8 + NQ))
            dve.wait_ge(product_ready, 1)
            linked(nc.vector.tensor_tensor(row[:, :], ps_row[0:B, :], x_last[:, :], ALU.add))
            norm(0, row[:, :], row[:, :])
            norm(1, row[:, :], normed_row[:, :], 0, 1)
            copy_rowT(1)
            dve.wait_ge(product_ready, 2)
            linked(nc.vector.tensor_tensor(thought[:, :], ps_row[0:B, :], vectors[:, 4], ALU.add))
            for k in range(STEPS):
                norm(2 + k, thought[:, :], normed_row[:, :], 2, 3)
                copy_rowT(2 + k)
                linked(nc.vector.tensor_tensor(partly[:, :], thought[:, :], vectors[:, 5], ALU.add))
                if k == 2:
                    dve.wait_ge(w_hi_ready, 2)
                    nc.vector.tensor_tensor(wg_lo[:, 1], wg_raw[:, :, :], wg_hi[:, 1].bitcast(F32), ALU.subtract)\
                        .then_inc(w_lo_ready, 1)
                dve.wait_ge(hidden_summed, k + 1)
                nc.vector.tensor_tensor(hidden[:, :], ps_hidden[:, :], d1_bias[:, :], ALU.add).then_inc(biased, 1)
                dve.wait_ge(hidden_turned, k + 1)
                nc.vector.tensor_copy(hiddenT[:, :, :], ps_turn[:, :, :]).then_inc(hiddenT_ready, 1)
                dve.wait_ge(product_ready, 3 + k)
                done = nc.vector.tensor_tensor(thought[:, :], ps_row[0:B, :], partly[:, :], ALU.add)
                if k < STEPS - 1:
                    linked(done)
                else:
                    done.then_inc(row_ready, 1)
            copy_rowT(2 + STEPS)
            dve.wait_ge(product_ready, 3 + STEPS)
            nc.vector.tensor_tensor(bc_row[:, :], ps_row[0:B, :], vectors[:, 6], ALU.add).then_inc(bc_row_ready, 1)

        @block.scalar
        def _(act):
            act.wait_ge(w_loaded, 16)
            nc.scalar.activation(wg_hi[:, 0], wg_raw[:, :, :], ACT.Copy).then_inc(w_hi_ready, 1)
            for k in range(STEPS):
                act.wait_ge(biased, k + 1)
                nc.scalar.activation(hidden[:, :], hidden[:, :], ACT.Gelu).then_inc(gelu_ready, 1)
                if k == 1:
                    act.wait_ge(bc_loaded, 32)
                    nc.scalar.activation(wg_hi[:, 1], wg_raw[:, :, :], ACT.Copy).then_inc(w_hi_ready, 1)
                act.wait_ge(parts_summed, k + 1)
                nc.scalar.activation(parts[:, :], ps_parts[:, :], ACT.Copy).then_inc(parts_ready, 1)

        @block.tensor
        def _(pe):
            def turn_row(n, src):
                pe.wait_ge(row_ready, n)
                if n >= 2:
                    pe.wait_ge(rowT_ready, n - 1)
                if n >= 3:
                    pe.wait_ge(hiddenT_ready, n - 2)
                for c in range(KC):
                    last = nc.tensor.transpose(ps_turn[:, c, 0:B], src[:, c * P:(c + 1) * P], ident[0:B, 0:B])
                last.then_inc(turned, 1)
                pe.wait_ge(rowT_ready, n)

            def row_product(w):
                for c in range(KC):
                    last = nc.tensor.matmul(ps_row[0:B, :], rowT[:, c, 0:B], w[:, c], start=(c == 0), stop=(c == KC - 1))
                last.then_inc(product_ready, 1)

            pe.wait_ge(att_loaded, 32 * B)
            pe.wait_ge(w_lo_ready, 1)
            for c in range(KC):
                for t, (a, w) in enumerate(((0, wg_hi), (0, wg_lo), (1, wg_hi))):
                    last = nc.tensor.matmul(ps_row[0:B, :], attT[:, a, c, :], w[:, 0, c], start=(c == 0 and t == 0),
                                            stop=(c == KC - 1 and t == 2))
            last.then_inc(product_ready, 1)
            turn_row(1, normed_row)
            pe.wait_ge(agg_loaded, 16)
            row_product(agg_sb)
            for k in range(STEPS):
                turn_row(2 + k, normed_row)
                pe.wait_ge(d1_loaded, 16)
                for c in range(KC):
                    for q in range(NQ):
                        last = nc.tensor.matmul(ps_hidden[q * Q:(q + 1) * Q, :], rowT[:, c, :],
                                                d1_sb[:, c, q * D:(q + 1) * D], start=(c == 0), stop=(c == KC - 1))
                last.then_inc(hidden_summed, 1)
                pe.wait_ge(gelu_ready, k + 1)
                for c in range(KC):
                    last = nc.tensor.transpose(ps_turn[:, c, :], hidden[:, c * P:(c + 1) * P], ident[:, :])
                last.then_inc(hidden_turned, 1)
                pe.wait_ge(hiddenT_ready, k + 1)
                pe.wait_ge(d2_loaded, 16)
                if k:
                    pe.wait_ge(parts_ready, k)
                for c in range(KC):
                    for q in range(NQ):
                        last = nc.tensor.matmul(ps_parts[q * Q:(q + 1) * Q, :], hiddenT[:, c, q * Q:(q + 1) * Q],
                                                d2_sb[:, KC * q + c], start=(c == 0), stop=(c == KC - 1))
                last.then_inc(parts_summed, 1)
                pe.wait_ge(parts_ready, k + 1)
                nc.tensor.matmul(ps_row[0:B, :], fold[:, :], parts[:, :], start=True, stop=True).then_inc(product_ready, 1)
            turn_row(2 + STEPS, thought)
            pe.wait_ge(bc_loaded, 32)
            row_product(bc_sb)


def gate_all(nc, x, att_scr, gate_b, out_gamma, out_beta, out, wg_hi, wg_lo, ident, bc_scr, attT, x_in, loaded):
    ctx = ExitStack()
    sb = lambda name, shape, dt=F32: ctx.enter_context(nc.sbuf_tensor(name, shape, dt))
    pb = lambda name, shape: ctx.enter_context(nc.psum_tensor(name, shape, F32))
    sem = lambda name: ctx.enter_context(nc.semaphore(name))
    N = CHUNKS // 2
    R = 2 * RT
    TILES = N * R
    TURN, GATE, NORM, OUT = 1, 2, 3, 4
    with ctx:
        gate_bias = sb("gate_bias", [P, D])
        bias_rows = sb("bias_rows", [P, D], F32R)
        pick = sb("pick4", [P, P], F32R)
        gamma = sb("gamma4", [P, D])
        beta = sb("beta4", [P, D])
        x1 = sb("x1", [P, 4, D])
        x1_beta = sb("x1_beta", [P, 4, D])
        x2 = sb("x2", [P, 4, D])
        x2T_hi = sb("x2T_hi", [P, 2, KC, P], F32R)
        x2T_lo = sb("x2T_lo", [P, 2, KC, P], F32R)
        gate = sb("gate4", [P, 2, D])
        gated = sb("gated4", [P, 2, D])
        normed = sb("normed4", [P, 2, D])
        result = sb("result4", [P, 4, D])
        stats = sb("stats4", [P, 2, 6])
        mom = sb("mom4", [P, 4, 2, 2])
        eps_var = sb("eps_var4", [P, 4, 2])
        rstd = sb("rstd4", [P, 4, 2])
        minus_half = sb("minus_half4", [P, 1])
        eps = sb("eps4", [P, 2])
        bc_in = sb("bc_in4", [P, 2, D])
        ps_y = pb("ps_y", [P, 2, D])
        ps_t = pb("ps_t4", [P, 2, KC, P])
        ps_g = pb("ps_g", [P, 2, D])

        const_ready = sem("const_ready4")
        vec_loaded = sem("vec_loaded4")
        y_ready, x1_ready, x1_beta_ready = sem("y_ready4"), sem("x1_ready4"), sem("x1_beta_ready4")
        stats_ready = [sem(f"stats_ready4{w}") for w in range(2)]
        mom_ready = [sem(f"mom_ready4{w}") for w in range(2)]
        eps_ready = [sem(f"eps_ready4{w}") for w in range(2)]
        rstd_ready = [sem(f"rstd_ready4{w}") for w in range(2)]
        x2_ready, turned, hi_ready, lo_ready = sem("x2_ready4"), sem("turned4"), sem("hi_ready4"), sem("lo_ready4")
        g_ready, gate_ready, gated_ready = (sem(n) for n in ("g_ready4", "gate_ready4", "gated_ready4"))
        bias_hi_ready, bias_ready = sem("bias_hi_ready4"), sem("bias_ready4")
        bc_loaded = [sem(f"bc_loaded4{p}") for p in range(2)]
        sum_ready, normed_ready = sem("sum_ready4"), sem("normed_ready4")
        scaled_ready, result_ready = sem("scaled_ready4"), sem("result_ready4")
        stored = [sem(f"stored4{p}") for p in range(4)]
        block = ctx.enter_context(nc.Block())

        out_rows = out.rearrange("b (r p) d -> p (b r) d", p=P)

        def staged(stages):
            def body(i):
                for r in range(R):
                    for lag, stage in stages:
                        if positive(R * i + r - lag + 1):
                            stage(i + (r - lag) // R, (r - lag) % R)
            return body

        def rest(stages):
            for late in range(max(lag for lag, _ in stages)):
                for lag, stage in stages:
                    if lag > late:
                        r = R + late - lag
                        stage(N - 1 + r // R, r % R)

        @block.sync
        def _(sp):
            for dst, vec in ((gate_bias, gate_b), (gamma, out_gamma), (beta, out_beta)):
                sp.dma_start(dst[:, :], vec.partition_broadcast(P)).then_inc(vec_loaded, 16)

            def load(i, r):
                if r % RT or (is_last(i, N) and r == RT):
                    return
                i, par = i + (r // RT + 1) // 2, (r // RT + 1) % 2
                n = 2 * i + par
                if positive(RT * (n - 1)):
                    sp.wait_ge(x1_ready, RT * (n - 1))
                load_chunk(sp, n, par, x, att_scr, attT, x_in, loaded)

            def load_bc(i, r):
                if r % RT or (is_last(i, N) and r == RT):
                    return
                load_bc_chunk(i + (r // RT + 1) // 2, (r // RT + 1) % 2)

            def load_bc_chunk(i, par):
                n = 2 * i + par
                if positive(RT * (n - 1)):
                    sp.wait_ge(gated_ready, RT * (n - 1))
                b = i // 2
                sp.dma_start(bc_in[:, par], bc_scr[bass.ds(b, 1), :].rearrange("o d -> (o d)").partition_broadcast(P))\
                    .then_inc(bc_loaded[par], 16)

            def store(i, r):
                m = R * i + r
                sp.wait_ge(result_ready, m + 1)
                sp.dma_start(out_rows[:, bass.ds(m, 1), :].rearrange("p o d -> p (o d)"), result[:, r % 4])\
                    .then_inc(stored[r % 4], 16)

            load_bc_chunk(0, 0)
            stages = ((0, load), (OUT, store), (GATE, load_bc))
            peeled(sp, staged(stages), N)
            rest(stages)
            for s in stored:
                sp.wait_ge(s, 16 * TILES // 4)

        @block.gpsimd
        def _(pool):
            pool.memset(minus_half[:, :], -0.5).then_inc(const_ready, 1)
            for w, value in enumerate((LN_EPS, FFN_EPS)):
                pool.memset(eps[:, w:w + 1], value).then_inc(const_ready, 1)
            pool.memset(pick[:, :].bitcast(F32), 0.0).then_inc(const_ready, 1)
            pool.wait_ge(const_ready, 4)
            for row in (0, 32):
                pool.memset(pick[row:row + 1, :].bitcast(F32), 1.0).then_inc(const_ready, 1)
            pool.wait_ge(const_ready, 6)
            pool.wait_ge(vec_loaded, 48)

            def invert(w):
                def stage(i, r):
                    m, v = R * i + r, r % 4
                    pool.wait_ge(mom_ready[w], m + 1)
                    if positive(m - 3):
                        pool.wait_ge((x2_ready, normed_ready)[w], m - 3)
                    pool.tensor_tensor(eps_var[:, v, w:w + 1], mom[:, v, w, 1:2], eps[:, w:w + 1], ALU.add)\
                        .then_inc(eps_ready[w], 1)
                    pool.wait_ge(eps_ready[w], m + 1)
                    pool.tensor_tensor(rstd[:, v, w:w + 1], eps_var[:, v, w:w + 1], minus_half[:, :], ALU.pow)\
                        .then_inc(rstd_ready[w], 1)
                return stage

            def add_beta(i, r):
                m, v = R * i + r, r % 4
                pool.wait_ge(x1_ready, m + 1)
                if positive(m - 3):
                    pool.wait_ge(result_ready, m - 3)
                pool.tensor_tensor(x1_beta[:, v], x1[:, v], beta[:, :], ALU.add).then_inc(x1_beta_ready, 1)

            def gate_bc(i, r):
                m, u = R * i + r, r % 2
                pool.wait_ge(bc_loaded[r // RT], 16 * (i + 1))
                pool.wait_ge(gate_ready, m + 1)
                if positive(m - 1):
                    pool.wait_ge(normed_ready, m - 1)
                pool.tensor_tensor(gated[:, u], gate[:, u], bc_in[:, r // RT], ALU.mult).then_inc(gated_ready, 1)

            def scale(i, r):
                m, u = R * i + r, r % 2
                pool.wait_ge(normed_ready, m + 1)
                pool.tensor_tensor(normed[:, u], normed[:, u], gamma[:, :], ALU.mult).then_inc(scaled_ready, 1)

            stages = ((0, invert(0)), (NORM, invert(1)), (TURN, add_beta), (NORM, scale), (GATE, gate_bc))
            peeled(pool, staged(stages), N)
            rest(stages)

        @block.vector
        def _(dve):
            dve.wait_ge(bias_hi_ready, 1)
            low_rows = slice(32, 64)
            nc.vector.tensor_tensor(bias_rows[low_rows], gate_bias[low_rows], bias_rows[low_rows].bitcast(F32), ALU.subtract)\
                .then_inc(bias_ready, 1)

            def first(i, r):
                m, v = R * i + r, r % 4
                dve.wait_ge(loaded[r // RT], 48 * (i + 1))
                dve.wait_ge(y_ready, m + 1)
                if positive(m - 3):
                    dve.wait_ge(x1_beta_ready, m - 3)
                nc.vector.tensor_tensor(x1[:, v], ps_y[:, r % 2], x_in[:, r // RT, r % RT], ALU.add).then_inc(x1_ready, 1)
                dve.wait_ge(x1_ready, m + 1)
                nc.vector.bn_stats(stats[:, 0], x1[:, v]).then_inc(stats_ready[0], 1)

            def moments(w):
                def stage(i, r):
                    m = R * i + r
                    if isinstance(m, int):
                        dve.wait_ge(stats_ready[w], m + 1)
                    nc.vector.bn_aggr(mom[:, r % 4, w], stats[:, w]).then_inc(mom_ready[w], 1)
                return stage

            def normalise(i, r):
                m, v = R * i + r, r % 4
                dve.wait_ge(mom_ready[0], m + 1)
                dve.wait_ge(rstd_ready[0], m + 1)
                nc.vector.tensor_scalar(x2[:, v], x1[:, v], mom[:, v, 0, 0:1], rstd[:, v, 0:1], ALU.subtract, ALU.mult)\
                    .then_inc(x2_ready, 1)

            def low(i, r):
                m, u = R * i + r, r % 2
                dve.wait_ge(hi_ready, m + 1)
                nc.vector.tensor_tensor(x2T_lo[:, u], ps_t[:, u], x2T_hi[:, u].bitcast(F32), ALU.subtract).then_inc(lo_ready, 1)

            def add_x2(i, r):
                m, v, u = R * i + r, r % 4, r % 2
                if not isinstance(m, int):
                    dve.wait_ge(stats_ready[0], m + NORM + 1)
                    dve.wait_ge(rstd_ready[0], m + NORM - 3)
                dve.wait_ge(gated_ready, m + 1)
                nc.vector.tensor_tensor(gated[:, u], gated[:, u], x2[:, v], ALU.add).then_inc(sum_ready, 1)
                dve.wait_ge(sum_ready, m + 1)
                nc.vector.bn_stats(stats[:, 1], gated[:, u]).then_inc(stats_ready[1], 1)

            def normalise2(i, r):
                m, v, u = R * i + r, r % 4, r % 2
                dve.wait_ge(mom_ready[1], m + 1)
                dve.wait_ge(rstd_ready[1], m + 1)
                if positive(m - 1):
                    dve.wait_ge(result_ready, m - 1)
                nc.vector.tensor_scalar(normed[:, u], gated[:, u], mom[:, v, 1, 0:1], rstd[:, v, 1:2],
                                        ALU.subtract, ALU.mult).then_inc(normed_ready, 1)

            def add_up(i, r):
                m, v, u = R * i + r, r % 4, r % 2
                if not isinstance(m, int):
                    dve.wait_ge(stats_ready[1], m + OUT - NORM + 1)
                    dve.wait_ge(rstd_ready[1], m + OUT - NORM - 3)
                dve.wait_ge(scaled_ready, m + 1)
                dve.wait_ge(x1_beta_ready, m + 1)
                if positive(m - 3):
                    dve.wait_ge(stored[v], 16 * (2 * i + r // 4))
                nc.vector.tensor_tensor(result[:, v], normed[:, u], x1_beta[:, v], ALU.add).then_inc(result_ready, 1)

            stages = ((0, first), (TURN, low), (NORM, add_x2), (0, moments(0)), (OUT, add_up), (NORM, moments(1)),
                      (0, normalise), (NORM, normalise2))
            peeled(dve, staged(stages), N)
            rest(stages)

        @block.scalar
        def _(act):
            act.wait_ge(vec_loaded, 48)
            nc.scalar.activation(bias_rows[:, :], gate_bias[:, :], ACT.Copy).then_inc(bias_hi_ready, 1)

            def high(i, r):
                m, u = R * i + r, r % 2
                act.wait_ge(turned, m + 1)
                if positive(m - 1):
                    act.wait_ge(g_ready, m - 1)
                nc.scalar.activation(x2T_hi[:, u], ps_t[:, u], ACT.Copy).then_inc(hi_ready, 1)

            def sigmoid(i, r):
                m, u = R * i + r, r % 2
                act.wait_ge(g_ready, m + 1)
                if positive(m - 1):
                    act.wait_ge(gated_ready, m - 1)
                nc.scalar.activation(gate[:, u], ps_g[:, u], ACT.Sigmoid).then_inc(gate_ready, 1)

            stages = ((TURN, high), (GATE, sigmoid))
            peeled(act, staged(stages), N)
            rest(stages)

        @block.tensor
        def _(pe):
            def project(i, r):
                m, par = R * i + r, r // RT
                pe.wait_ge(loaded[par], 48 * (i + 1))
                if positive(m - 1):
                    pe.wait_ge(x1_ready, m - 1)
                for c in range(KC):
                    for t, (a, w) in enumerate(((0, wg_hi), (0, wg_lo), (1, wg_hi))):
                        last = nc.tensor.matmul(ps_y[:, r % 2], attT[:, par, a, c, (r % RT) * P:(r % RT + 1) * P], w[:, 0, c],
                                                start=(c == 0 and t == 0), stop=(c == KC - 1 and t == 2))
                last.then_inc(y_ready, 1)

            def turn(i, r):
                m, u, v = R * i + r, r % 2, r % 4
                pe.wait_ge(x2_ready, m + 1)
                if positive(m - 1):
                    pe.wait_ge(lo_ready, m - 1)
                for c in range(KC):
                    last = nc.tensor.transpose(ps_t[:, u, c], x2[:, v, c * P:(c + 1) * P], ident[:, :])
                last.then_inc(turned, 1)

            def gates(i, r):
                m, u = R * i + r, r % 2
                pe.wait_ge(lo_ready, m + 1)
                if positive(m - 1):
                    pe.wait_ge(gate_ready, m - 1)
                nc.tensor.matmul(ps_g[:, u], pick[:, :], bias_rows[:, :], start=True, stop=False)
                for c in range(KC):
                    for t, (xT, w) in enumerate(((x2T_hi, wg_hi), (x2T_hi, wg_lo), (x2T_lo, wg_hi))):
                        last = nc.tensor.matmul(ps_g[:, u], xT[:, u, c], w[:, 1, c], start=False, stop=(c == KC - 1 and t == 2))
                last.then_inc(g_ready, 1)

            pe.wait_ge(bias_ready, 1)
            pe.wait_ge(const_ready, 6)
            stages = ((0, project), (TURN, turn), (GATE, gates))
            peeled(pe, staged(stages), N)
            rest(stages)


def build(nc, x, Wq, Wk, Wv, Wo, in_gamma, in_beta, agg_w, agg_b, pn_gamma, pn_beta, d1_w, d1_b, d2_w, d2_b,
          bc_w, bc_b, gate_w, gate_b, out_gamma, out_beta, out):
    qk_scr = nc.dram_tensor("qk_scr", [2, 2, D, B * T], F32, kind="Internal").ap()
    v_scr = nc.dram_tensor("v_scr", [B * T, D], F32, kind="Internal").ap()
    att_scr = nc.dram_tensor("att_scr", [2, D, B * T], F32, kind="Internal").ap()
    project(nc, x, Wq, Wk, Wv, qk_scr, v_scr)
    attend(nc, qk_scr, v_scr, att_scr)
    conclude(nc, x, att_scr, Wo, agg_w, agg_b, in_gamma, in_beta, pn_gamma, pn_beta, d1_w, d1_b, d2_w, d2_b,
             bc_w, bc_b, gate_w, gate_b, out_gamma, out_beta, out)


_INS = ["L0_attn_x", "L0_attn_Wq", "L0_attn_Wk", "L0_attn_Wv", "L0_attn_Wo", "L0_ffn_in_gamma", "L0_ffn_in_beta",
        "L0_ffn_agg_w", "L0_ffn_agg_b", "L0_ffn_pn_gamma", "L0_ffn_pn_beta", "L0_ffn_d1_w", "L0_ffn_d1_b",
        "L0_ffn_d2_w", "L0_ffn_d2_b", "L0_ffn_bc_w", "L0_ffn_bc_b", "L0_ffn_gate_w", "L0_ffn_gate_b",
        "L0_ffn_out_gamma", "L0_ffn_out_beta"]


def kernel(**inputs):
    import numpy as _np
    import concourse.bacc as _bacc
    from concourse import mybir as _mybir
    from concourse.bass_utils import run_bass_kernel_spmd as _run

    nc = _bacc.Bacc("TRN2", target_bir_lowering=False, num_devices=1)
    arrays, args = {}, []
    for name in _INS:
        a = _np.ascontiguousarray(inputs[name])
        arrays[f"in_{name}"] = a
        args.append(nc.dram_tensor(f"in_{name}", a.shape, _mybir.dt.from_np(a.dtype), kind="ExternalInput").ap())
    args.append(nc.dram_tensor("out_x", (B, T, D), _mybir.dt.float32, kind="ExternalOutput").ap())
    build(nc, *args)
    r = _run(nc, [arrays], core_ids=[0])
    return r.results[0]["out_x"]
```
